# Optimizing a Trainium2 kernel written in Bass

```python
import numpy as np
import jax
import jax.numpy as jnp

def _softmax(x, axis=-1):
    return jax.nn.softmax(x, axis=axis)

def _gelu(x):
    return jax.nn.gelu(x, approximate=True)

def _silu(x):
    return jax.nn.silu(x)

def _sigmoid(x):
    return jax.nn.sigmoid(x)

def _layernorm(x, axis=-1, eps=1e-05):
    m = jnp.mean(x, axis=axis, keepdims=True)
    v = jnp.var(x, axis=axis, keepdims=True)
    return (x - m) / jnp.sqrt(v + eps)

def _scatter_add(tgt, idx, src, axis=0):
    return tgt.at[idx].add(src)

def _segment_sum(src, seg, n):
    return jax.ops.segment_sum(src, seg, n)
kernel_name = 'mk_seq_postln_d2_jaxref_r4_2f2ebc'

def setup_inputs(seed: int=0):
    np.random.seed(seed)
    _w = jnp.asarray

    def _L0_attn_setup():
        import jax, jax.numpy as jnp
        import numpy as np
        B, T, C, NH = (8, 256, 256, 16)
        HD = C // NH
        EPS = 1e-05

        def _decay_mask(nh, t, dtype):
            gamma = 1.0 - 2.0 ** (-5.0 - jnp.arange(nh, dtype=jnp.float32))
            idx = jnp.arange(t)
            diff = idx[:, None] - idx[None, :]
            mask = diff >= 0
            pow_ = gamma[:, None, None] ** jnp.where(mask, diff, 0).astype(jnp.float32)
            return (jnp.where(mask[None], pow_, 0.0).astype(dtype), gamma.astype(dtype))

        def _reference_tuple_inner(x, past_kv, W_qkv, gn_weight, gn_bias):
            b, t, c = x.shape
            nh = gn_weight.shape[0]
            hd = c // nh
            qkv = x @ W_qkv
            q, k, v = jnp.split(qkv, 3, axis=2)
            split_heads = lambda u: u.reshape(b, t, nh, hd).transpose(0, 2, 1, 3)
            q, k, v = (split_heads(q), split_heads(k), split_heads(v))
            decay, gamma = _decay_mask(nh, t, x.dtype)
            ret = jnp.einsum('bhtd,bhsd->bhts', q, k) * decay
            inner = jnp.einsum('bhts,bhsd->bhtd', ret, v)
            inner_decay = float(nh * hd)
            cross = jnp.einsum('bhtd,hde->bhte', q, past_kv) * inner_decay
            r = inner + cross
            current_kv = gamma[:, None, None] * past_kv + jnp.einsum('bhtd,bhte->bhde', k, v)
            current_kv = current_kv.mean(axis=0)
            y = r.transpose(0, 1, 3, 2)
            mu = y.mean(axis=(1, 2, 3), keepdims=True)
            var = y.var(axis=(1, 2, 3), keepdims=True)
            yn = (y - mu) * jax.lax.rsqrt(var + EPS)
            yn = yn * gn_weight[None, :, None, None] + gn_bias[None, :, None, None]
            out = yn.transpose(0, 3, 1, 2).reshape(b, t, c)
            return (out, current_kv)
        key = jax.random.key(seed)
        k1, k2, k3 = jax.random.split(key, 3)
        x = jax.random.normal(k1, (B, T, C), dtype=jnp.float32)
        past_kv = jax.random.normal(k2, (NH, HD, HD), dtype=jnp.float32) * 0.1
        W_qkv = jax.random.normal(k3, (C, 3 * C), dtype=jnp.float32) * 0.02
        gn_weight = jnp.ones((NH,), dtype=jnp.float32)
        gn_bias = jnp.zeros((NH,), dtype=jnp.float32)
        return {'x': x, 'past_kv': past_kv, 'W_qkv': W_qkv, 'gn_weight': gn_weight, 'gn_bias': gn_bias}
    _L0_attn_in = _L0_attn_setup()

    def _L0_ffn_setup():
        import jax, jax.numpy as jnp
        import numpy as np
        EPS = 1e-06
        LN_EPS = 1e-05

        def _absmean_core(W):
            gamma = jnp.mean(jnp.abs(W)) + EPS
            Ws = W / gamma
            Wq = jnp.sign(Ws) * jnp.minimum(jnp.round(jnp.abs(Ws)), 1.0)
            return (Wq, gamma)

        @jax.custom_vjp
        def absmean(W):
            return _absmean_core(W)[0]

        def _absmean_fwd(W):
            Wq, gamma = _absmean_core(W)
            return (Wq, gamma)

        def _absmean_bwd(gamma, g):
            return (g / gamma,)
        absmean.defvjp(_absmean_fwd, _absmean_bwd)

        def layernorm(x, w, b, eps=LN_EPS):
            mu = jnp.mean(x, axis=-1, keepdims=True)
            var = jnp.mean((x - mu) ** 2, axis=-1, keepdims=True)
            return (x - mu) * jax.lax.rsqrt(var + eps) * w + b
        key = jax.random.key(seed)
        k1, k2, k3 = jax.random.split(key, 3)
        d, h = (256, 1024)
        B, T = (8, 512)
        return {'x': jax.random.normal(k1, (B, T, d), jnp.float32), 'W_fc': jax.random.normal(k2, (h, d), jnp.float32), 'ln_w': jnp.ones((h,), jnp.float32), 'ln_b': jnp.zeros((h,), jnp.float32), 'W_proj': jax.random.normal(k3, (d, h), jnp.float32)}
    _L0_ffn_in = _L0_ffn_setup()

    def _L1_attn_setup():
        import jax, jax.numpy as jnp
        import numpy as np
        EPS = float(np.finfo(np.float32).eps)
        B, S, F_, E, H = (8, 1024, 256, 256, 16)
        HD = E // H
        LAYER = 1
        LAMBDA_INIT = 0.8 - 0.6 * float(np.exp(-0.3 * (LAYER - 1)))
        SCALE = 1.0 / float(np.sqrt(E // 2))

        def _rms(x, g):
            return x * jax.lax.rsqrt(jnp.mean(x * x, axis=-1, keepdims=True) + EPS) * g
        key = jax.random.key(seed)
        ks = jax.random.split(key, 7)
        x = jax.random.normal(ks[0], (B, S, F_), jnp.float32)
        s = 0.02
        Wq = jax.random.normal(ks[1], (E, F_), jnp.float32) * s
        Wk = jax.random.normal(ks[2], (E, F_), jnp.float32) * s
        Wv = jax.random.normal(ks[3], (E, F_), jnp.float32) * s
        W1 = jax.random.normal(ks[4], (E, E), jnp.float32) * s
        W2 = jax.random.normal(ks[5], (E, E), jnp.float32) * s
        lambda_params = jnp.full((4,), 0.8, jnp.float32)
        g1 = jnp.ones((F_,), jnp.float32)
        g2 = jnp.ones((HD,), jnp.float32)
        g3 = jnp.ones((E,), jnp.float32)
        return dict(x=x, Wq=Wq, Wk=Wk, Wv=Wv, lambda_params=lambda_params, g1=g1, g2=g2, g3=g3, W1=W1, W2=W2)
    _L1_attn_in = _L1_attn_setup()

    def _L1_ffn_setup():
        import jax, jax.numpy as jnp
        import numpy as np
        NUM_GROUPS = 2
        EXPERT_CAPACITY = 160
        NUM_SELECTED = 2
        key = jax.random.key(seed)
        k1, k2, k3, k4 = jax.random.split(key, 4)
        B, S, H, E, F = (4, 512, 256, 8, 1024)
        return {'input_emb': jax.random.normal(k1, (B, S, H), dtype=jnp.float32), 'w_router': jax.random.normal(k2, (H, E), dtype=jnp.float32) * 0.02, 'wi': jax.random.normal(k3, (E, H, F), dtype=jnp.float32) * 0.02, 'wo': jax.random.normal(k4, (E, F, H), dtype=jnp.float32) * 0.02}
    _L1_ffn_in = _L1_ffn_setup()
    _d = {'L0_attn_x': _L0_attn_in['x'], 'L0_attn_past_kv': _L0_attn_in['past_kv'], 'L0_attn_W_qkv': _L0_attn_in['W_qkv'], 'L0_attn_gn_weight': _L0_attn_in['gn_weight'], 'L0_attn_gn_bias': _L0_attn_in['gn_bias'], 'L0_ffn_W_fc': _L0_ffn_in['W_fc'], 'L0_ffn_ln_w': _L0_ffn_in['ln_w'], 'L0_ffn_ln_b': _L0_ffn_in['ln_b'], 'L0_ffn_W_proj': _L0_ffn_in['W_proj'], 'L1_attn_Wq': _L1_attn_in['Wq'], 'L1_attn_Wk': _L1_attn_in['Wk'], 'L1_attn_Wv': _L1_attn_in['Wv'], 'L1_attn_lambda_params': _L1_attn_in['lambda_params'], 'L1_attn_g1': _L1_attn_in['g1'], 'L1_attn_g2': _L1_attn_in['g2'], 'L1_attn_g3': _L1_attn_in['g3'], 'L1_attn_W1': _L1_attn_in['W1'], 'L1_attn_W2': _L1_attn_in['W2'], 'L1_ffn_w_router': _L1_ffn_in['w_router'], 'L1_ffn_wi': _L1_ffn_in['wi'], 'L1_ffn_wo': _L1_ffn_in['wo']}
    _x0 = _d['L0_attn_x']
    _d['L0_attn_x'] = jax.random.normal(jax.random.fold_in(jax.random.key(seed), 1), (8, 512, 256), dtype=_x0.dtype)
    del _x0
    return _d

def reference(L0_attn_x, L0_attn_past_kv, L0_attn_W_qkv, L0_attn_gn_weight, L0_attn_gn_bias, L0_ffn_W_fc, L0_ffn_ln_w, L0_ffn_ln_b, L0_ffn_W_proj, L1_attn_Wq, L1_attn_Wk, L1_attn_Wv, L1_attn_lambda_params, L1_attn_g1, L1_attn_g2, L1_attn_g3, L1_attn_W1, L1_attn_W2, L1_ffn_w_router, L1_ffn_wi, L1_ffn_wo):

    def _L0_attn_ref(x, past_kv, W_qkv, gn_weight, gn_bias):
        import jax, jax.numpy as jnp
        import numpy as np
        B, T, C, NH = (8, 256, 256, 16)
        HD = C // NH
        EPS = 1e-05

        def _decay_mask(nh, t, dtype):
            gamma = 1.0 - 2.0 ** (-5.0 - jnp.arange(nh, dtype=jnp.float32))
            idx = jnp.arange(t)
            diff = idx[:, None] - idx[None, :]
            mask = diff >= 0
            pow_ = gamma[:, None, None] ** jnp.where(mask, diff, 0).astype(jnp.float32)
            return (jnp.where(mask[None], pow_, 0.0).astype(dtype), gamma.astype(dtype))

        def _reference_tuple_inner(x, past_kv, W_qkv, gn_weight, gn_bias):
            b, t, c = x.shape
            nh = gn_weight.shape[0]
            hd = c // nh
            qkv = x @ W_qkv
            q, k, v = jnp.split(qkv, 3, axis=2)
            split_heads = lambda u: u.reshape(b, t, nh, hd).transpose(0, 2, 1, 3)
            q, k, v = (split_heads(q), split_heads(k), split_heads(v))
            decay, gamma = _decay_mask(nh, t, x.dtype)
            ret = jnp.einsum('bhtd,bhsd->bhts', q, k) * decay
            inner = jnp.einsum('bhts,bhsd->bhtd', ret, v)
            inner_decay = float(nh * hd)
            cross = jnp.einsum('bhtd,hde->bhte', q, past_kv) * inner_decay
            r = inner + cross
            current_kv = gamma[:, None, None] * past_kv + jnp.einsum('bhtd,bhte->bhde', k, v)
            current_kv = current_kv.mean(axis=0)
            y = r.transpose(0, 1, 3, 2)
            mu = y.mean(axis=(1, 2, 3), keepdims=True)
            var = y.var(axis=(1, 2, 3), keepdims=True)
            yn = (y - mu) * jax.lax.rsqrt(var + EPS)
            yn = yn * gn_weight[None, :, None, None] + gn_bias[None, :, None, None]
            out = yn.transpose(0, 3, 1, 2).reshape(b, t, c)
            return (out, current_kv)
        return _reference_tuple_inner(x, past_kv, W_qkv, gn_weight, gn_bias)[0]

    def _L0_ffn_ref(x, W_fc, ln_w, ln_b, W_proj):
        import jax, jax.numpy as jnp
        import numpy as np
        EPS = 1e-06
        LN_EPS = 1e-05

        def _absmean_core(W):
            gamma = jnp.mean(jnp.abs(W)) + EPS
            Ws = W / gamma
            Wq = jnp.sign(Ws) * jnp.minimum(jnp.round(jnp.abs(Ws)), 1.0)
            return (Wq, gamma)

        @jax.custom_vjp
        def absmean(W):
            return _absmean_core(W)[0]

        def _absmean_fwd(W):
            Wq, gamma = _absmean_core(W)
            return (Wq, gamma)

        def _absmean_bwd(gamma, g):
            return (g / gamma,)
        absmean.defvjp(_absmean_fwd, _absmean_bwd)

        def layernorm(x, w, b, eps=LN_EPS):
            mu = jnp.mean(x, axis=-1, keepdims=True)
            var = jnp.mean((x - mu) ** 2, axis=-1, keepdims=True)
            return (x - mu) * jax.lax.rsqrt(var + eps) * w + b
        h = jnp.einsum('btd,hd->bth', x, absmean(W_fc))
        h = jax.nn.gelu(h, approximate=False)
        h = layernorm(h, ln_w, ln_b)
        return jnp.einsum('bth,dh->btd', h, absmean(W_proj))

    def _L1_attn_ref(x, Wq, Wk, Wv, lambda_params, g1, g2, g3, W1, W2):
        import jax, jax.numpy as jnp
        import numpy as np
        EPS = float(np.finfo(np.float32).eps)
        B, S, F_, E, H = (8, 1024, 256, 256, 16)
        HD = E // H
        LAYER = 1
        LAMBDA_INIT = 0.8 - 0.6 * float(np.exp(-0.3 * (LAYER - 1)))
        SCALE = 1.0 / float(np.sqrt(E // 2))

        def _rms(x, g):
            return x * jax.lax.rsqrt(jnp.mean(x * x, axis=-1, keepdims=True) + EPS) * g
        b, s_len, _ = x.shape
        xn = _rms(x, g1)
        Q = jnp.einsum('bsf,ef->bse', xn, Wq).reshape(b, s_len, H, HD)
        K = jnp.einsum('bsf,ef->bse', xn, Wk).reshape(b, s_len, H, HD)
        V = jnp.einsum('bsf,ef->bse', xn, Wv).reshape(b, s_len, H, HD)
        pQ = jax.nn.elu(Q)
        pK = jax.nn.elu(K)
        Q1, Q2 = jnp.split(pQ, 2, axis=-1)
        K1, K2 = jnp.split(pK, 2, axis=-1)
        kv1 = jnp.einsum('bshe,bshd->bsed', K1, V) * SCALE
        kv2 = jnp.einsum('bshe,bshd->bsed', K2, V) * SCALE
        w1 = jnp.einsum('bshe,bsed->bshd', Q1, kv1)
        w2 = jnp.einsum('bshe,bsed->bshd', Q2, kv2)
        lmb = jnp.exp(lambda_params[0] * lambda_params[1]) - jnp.exp(lambda_params[2] * lambda_params[3]) + LAMBDA_INIT
        attn = w1 - lmb * w2
        attn = (1.0 - LAMBDA_INIT) * _rms(attn, g2)
        attn = attn.reshape(b, s_len, E)
        attn = _rms(attn, g3) + attn
        h = jax.nn.gelu(jnp.einsum('bse,fe->bsf', attn, W1), approximate=False)
        out = jnp.einsum('bsf,ef->bse', h, W2) + attn
        return out

    def _L1_ffn_ref(input_emb, w_router, wi, wo):
        import jax, jax.numpy as jnp
        import numpy as np
        NUM_GROUPS = 2
        EXPERT_CAPACITY = 160
        NUM_SELECTED = 2
        B, S, H = input_emb.shape
        E = w_router.shape[1]
        G = NUM_GROUPS
        T = B * S // G
        C = EXPERT_CAPACITY
        K = NUM_SELECTED
        x = input_emb.reshape(G, T, H)
        router_logits = jnp.einsum('gth,he->gte', x.astype(jnp.float32), w_router.astype(jnp.float32))
        router_probs = jax.nn.softmax(router_logits, axis=-1)
        gate, idx = jax.lax.top_k(router_probs, K)
        mask = jax.nn.one_hot(idx, E, dtype=jnp.float32)
        mask_kt = jnp.swapaxes(mask, 1, 2).reshape(G, K * T, E)
        pos = jnp.cumsum(mask_kt, axis=1) * mask_kt - 1.0
        pos = jnp.swapaxes(pos.reshape(G, K, T, E), 1, 2)
        disp_k = jax.nn.one_hot(pos, C, dtype=jnp.float32) * mask[..., None]
        dispatch = disp_k.sum(axis=2)
        combine = jnp.einsum('gtk,gtkec->gtec', gate, disp_k)
        expert_in = jnp.einsum('gtec,gth->egch', dispatch, x)
        h = jax.nn.relu(jnp.einsum('egch,ehf->egcf', expert_in, wi))
        expert_out = jnp.einsum('egcf,efh->egch', h, wo)
        y = jnp.einsum('gtec,egch->gth', combine, expert_out)
        return y.reshape(B, S, H)
    x = L0_attn_x
    x = _layernorm(x + _L0_attn_ref(x, L0_attn_past_kv, L0_attn_W_qkv, L0_attn_gn_weight, L0_attn_gn_bias), axis=-1)
    x = _layernorm(x + _L0_ffn_ref(x, L0_ffn_W_fc, L0_ffn_ln_w, L0_ffn_ln_b, L0_ffn_W_proj), axis=-1)
    x = _layernorm(x + _L1_attn_ref(x, L1_attn_Wq, L1_attn_Wk, L1_attn_Wv, L1_attn_lambda_params, L1_attn_g1, L1_attn_g2, L1_attn_g3, L1_attn_W1, L1_attn_W2), axis=-1)
    x = _layernorm(x + _L1_ffn_ref(x, L1_ffn_w_router, L1_ffn_wi, L1_ffn_wo), axis=-1)
    return x

_drawn_inputs = setup_inputs


def setup_inputs(seed=0):
    import zlib

    import numpy as np

    out = dict(_drawn_inputs(seed))
    spreads = {'L0_attn_gn_weight': (1.0, 0.2),
     'L0_attn_gn_bias': (0.0, 0.1),
     'L0_ffn_ln_w': (1.0, 0.2),
     'L0_ffn_ln_b': (0.0, 0.1),
     'L1_attn_lambda_params': (0.800000011920929, 0.2),
     'L1_attn_g1': (1.0, 0.2),
     'L1_attn_g2': (1.0, 0.2),
     'L1_attn_g3': (1.0, 0.2)}
    factors = {'L1_ffn_w_router': 2.679, 'L1_ffn_wi': 3.062}
    for name, (base, spread) in spreads.items():
        noise = np.random.default_rng([zlib.crc32(name.encode()), seed]).standard_normal(out[name].shape)
        drawn = base * np.exp(spread * noise) if base else spread * noise
        out[name] = jnp.asarray(drawn.astype(out[name].dtype))
    for name, factor in factors.items():
        out[name] = (out[name] * factor).astype(out[name].dtype)
    return out
```

```python
from contextlib import ExitStack

import numpy as np
import concourse.bass as bass
from concourse import mybir

F32 = mybir.dt.float32
I32 = mybir.dt.int32
U32 = mybir.dt.uint32
ALU = mybir.AluOpType
ACT = mybir.ActivationFunctionType
AX = mybir.AxisListType

P = 128
BATCH, SEQ, DIM = 8, 512, 256
TOKENS = BATCH * SEQ
TILES = TOKENS // P
TPB = SEQ // P
KD = DIM // P
HEADS, HD = 16, 16
HPK = P // HD
HID = 1024
NH = HID // P
LN_EPS = 1e-5
ABS_EPS = 1e-6
RMS_EPS = float(np.finfo(np.float32).eps)
LAMBDA_INIT = 0.8 - 0.6 * float(np.exp(-0.3 * 0))
RET_SCALE = 1.0 / float(np.sqrt(DIM // 2))
UNIT = 8 * P
UNITS = TOKENS // UNIT
GROUPS = UNIT // P
HALF = 64
EXPERTS, CAP, TOPK, MGROUPS = 8, 160, 2, 2
TPG = TILES // MGROUPS
ROWS = MGROUPS * CAP
SLOTS = EXPERTS * ROWS
RTILES = [(0, 128), (128, 128), (256, 64)]



def constant_table():
    gamma = 1.0 - 2.0 ** (-5.0 - np.arange(HEADS, dtype=np.float64))
    p = np.arange(P)
    parts = {}
    parts["ident"] = np.eye(P)
    parts["ones"] = np.ones((P, P))
    parts["tri"] = (p[:, None] <= p[None, :]).astype(np.float64)
    order = [half * HPK + 2 * r + par for r in range(4) for half in range(2) for par in range(2)]
    diff = p[None, :] - p[:, None]
    dec = np.where(diff[None] >= 0, gamma[order][:, None, None] ** np.maximum(diff, 0)[None], 0.0)
    parts["decay"] = dec.transpose(1, 0, 2).reshape(P, -1)
    hrow = np.arange(P) // HD
    qd = np.stack([gamma[half * HPK + hrow][:, None] ** (p[None, :] + 1) for half in range(2)], 1)
    parts["qdecay"] = qd.reshape(P, -1)
    parts["kdecay"] = gamma[np.arange(DIM) // HD][None, :] ** (P - 1 - p)[:, None]
    parts["tiledecay"] = np.stack([gamma[half * HPK + hrow] ** P for half in range(2)], 1)
    parts["block"] = (hrow[:, None] == hrow[None, :]).astype(np.float64)
    parts["even"] = (hrow % 2 == 0).astype(np.float64)[:, None]
    parts["odd"] = (hrow % 2 == 1).astype(np.float64)[:, None]
    parts["first"] = np.tile(EXPERTS - np.arange(EXPERTS), (P, 1))
    parts["base"] = np.tile(np.arange(EXPERTS) * ROWS, (P, 1))
    parts["firsthalf"] = (p % HD < HD // 2).astype(np.float64)[:, None]
    parts["rmseps"] = np.full((P, 1), RMS_EPS)
    parts["minushalf"] = np.full((P, HEADS), -0.5)
    at, where = 0, {}
    for name, a in parts.items():
        where[name] = (at, a.shape[1])
        at += a.shape[1]
    return np.concatenate([a for a in parts.values()], 1).astype(np.float32), where


CONSTS, WHERE = constant_table()


class Signal:

    def __init__(self, net, ctx, name, head=0):
        self.sem = ctx.enter_context(net.nc.semaphore(name))
        self.head = head
        net.signals.append(self.sem)
        if head:
            net.nc.sync.sem_inc(self.sem, head)

    def after(self, count):
        return count + self.head


class Steps:

    def __init__(self, sem):
        self.sem, self.base, self.k = sem, 0, 0

    def done(self, more=0):
        self.k += more
        return self.base + self.k

    def enter(self, i, per):
        self.entry, self.per = self.base + self.k, per
        self.base, self.k = self.entry + i * per, 0

    def leave(self, times):
        assert self.k == self.per, (self.k, self.per)
        self.base, self.k = self.entry + times * self.per, 0


class Net:

    def __init__(self, nc, ctx, args):
        self.nc, self.args, self.ctx = nc, args, ctx
        self.sb = lambda name, shape, dt=F32: ctx.enter_context(nc.sbuf_tensor(name, shape, dt))
        self.passed = ctx.enter_context(nc.semaphore("passed"))
        self.passed_act = ctx.enter_context(nc.semaphore("passed_act"))
        self.passed_pool = ctx.enter_context(nc.semaphore("passed_pool"))
        self.x_res = self.sb("x_res", [P, TILES, DIM])
        self.wfcT = self.sb("wfcT", [P, KD, HID])
        self.wpjT = self.sb("wpjT", [P, NH, DIM])
        self.wqkvT = self.sb("wqkvT", [P, KD, 3 * DIM])
        self.w1T = self.sb("w1T", [P, KD, DIM])
        self.w2T = self.sb("w2T", [P, KD, DIM])
        self.qkv_dram = nc.dram_tensor("qkv_dram", [3, DIM, TOKENS], F32).ap()
        self.xe_dram = nc.dram_tensor("xe_dram", [SLOTS, DIM], F32).ap()
        self.ye_dram = nc.dram_tensor("ye_dram", [SLOTS + 1, DIM], F32).ap()
        self.att_res = self.sb("att_res", [P, TILES, DIM])
        self.gates = self.sb("gates", [P, TOPK, TILES])
        self.idx_back = self.sb("idx_back", [P, TILES, TOPK], U32)
        self.const = self.sb("const", [P, CONSTS.shape[1]])
        self.table = {}
        for name, (at, n) in WHERE.items():
            self.table[name] = self.const[:, at:at + n]


def retention(net, ctx):
    nc, a = net.nc, net.args

    def sb(name, shape, dt=F32):
        return ctx.enter_context(nc.sbuf_tensor("r_" + name, shape, dt))

    def ps(name, shape):
        return ctx.enter_context(nc.psum_tensor("r_" + name, shape, F32))

    def sig(name, head=0):
        return Signal(net, ctx, "r_" + name, head)

    w = sb("w", [P, KD, 3 * DIM])
    pkv = sb("pkv", [P, KD, P])
    pkv_raw = sb("pkv_raw", [P, KD, HD])
    gnw, gnb = sb("gnw", [P, HEADS]), sb("gnb", [P, HEADS])
    r_res = sb("r_res", [P, TILES, DIM])
    xin = [sb(f"xin{i}", [P, DIM]) for i in range(4)]
    two = range(2)
    xT = [sb(f"xT{i}", [P, KD, P]) for i in two]
    qT = [sb(f"qT{i}", [P, KD, P]) for i in range(TPB)]
    qS = [sb(f"qS{i}", [P, KD, P]) for i in range(TPB)]
    qE = [sb(f"qE{i}", [P, KD, P]) for i in range(TPB)]
    qO = [sb(f"qO{i}", [P, KD, P]) for i in range(TPB)]
    kT = [sb(f"kT{i}", [P, KD, P]) for i in two]
    v = [sb(f"v{i}", [P, DIM]) for i in range(TPB)]
    ks = [sb(f"ks{i}", [P, DIM]) for i in two]
    prob = [sb(f"prob{i}", [P, 4, 4, P]) for i in two]
    state = [sb(f"state{i}", [P, KD, P]) for i in two]
    upd = sb("upd", [P, KD, P])
    rsq = [sb(f"rsq{i}", [P, DIM]) for i in two]
    gst = sb("gst", [P, TPB, 2, HEADS])
    gsum = sb("gsum", [P, 4])
    gaff = sb("gaff", [P, 3, HEADS])
    bst = sb("bst", [P, TPB, 6])
    mv = sb("mv", [P, TPB, 2])
    rstd = sb("rstd", [P, TPB])
    y1 = [sb(f"y1{i}", [P, DIM]) for i in range(TPB)]

    pXR = ps("pXR", [P, 512])
    pX, pR = pXR[:, 0:DIM], pXR[:, DIM:2 * DIM]
    pQV = ps("pQV", [P, 512])
    pQ, pV = pQV[:, 0:DIM].rearrange("p (k t) -> p k t", k=KD), pQV[:, DIM:2 * DIM]
    pKK = ps("pKK", [P, 512])
    pKT, pK = pKK[:, 0:DIM].rearrange("p (k t) -> p k t", k=KD), pKK[:, DIM:2 * DIM]
    pUG = ps("pUG", [P, 512])
    pU, pG = pUG[:, 0:DIM], pUG[:, DIM:DIM + 2 * HEADS]
    pS = [ps(f"pS{i}", [P, 4, P]) for i in range(4)]

    w_in = sig("w_in")
    x_in = [sig(f"x_in{i}") for i in range(4)]
    x_kept = sig("x_kept", 4)
    x_turned = sig("x_turned", 4)
    xT_ready = sig("xT_ready")
    kT_made = sig("kT_made")
    qv_made = sig("qv_made")
    q_copied = sig("q_copied")
    qv_taken = sig("qv_taken")
    qS_ready = sig("qS_ready")
    k_taken = sig("k_taken")
    k_turned = sig("k_turned")
    ks_ready = sig("ks_ready")
    s_made = sig("s_made")
    s_taken = sig("s_taken", 4)
    r_made = sig("r_made", 4)
    r_taken = sig("r_taken")
    upd_made = sig("upd_made")
    state_ready = sig("state_ready")
    sums_ready = sig("sums_ready")
    rsq_ready = sig("rsq_ready")
    rsq_free = sig("rsq_free", 2)
    g_made = sig("g_made")
    g_taken = sig("g_taken")
    pkv_ready = sig("pkv_ready")
    shifted = sig("shifted")
    affine = sig("affine")
    y_free = sig("y_free", 4)
    gvar_ready = sig("gvar_ready")
    grstd_ready = sig("grstd_ready")
    mv_ready = sig("mv_ready")
    rstd_ready = sig("rstd_ready")
    pool_step = sig("pool_step")
    dve_step = sig("dve_step")

    x_rows = a["L0_attn_x"].rearrange("b (t p) d -> (b t) p d", p=P)

    nc.all_engine_barrier()
    block = ctx.enter_context(nc.Block())

    @block.sync
    def _(sp):
        sp.dma_start(w[:, :, :], a["L0_attn_W_qkv"].rearrange("(k p) n -> p k n", p=P)).then_inc(w_in.sem, 16)
        sp.dma_start(pkv_raw[:, :, :], a["L0_attn_past_kv"].rearrange("(k h) d e -> (h d) k e", k=KD)).then_inc(w_in.sem, 16)
        for t, src in ((gnw, "L0_attn_gn_weight"), (gnb, "L0_attn_gn_bias")):
            sp.dma_start(t[:, :], a[src].rearrange("(a h) -> a h", a=1).broadcast_to([P, HEADS])).then_inc(w_in.sem, 16)

        with sp.Fori(0, BATCH) as b:
            for t in range(TPB):
                sp.wait_ge(x_turned.sem, x_turned.after(b * TPB + (t + 1 - 4)))
                sp.wait_ge(x_kept.sem, x_kept.after(b * TPB + (t + 1 - 4)))
                sp.dma_start(xin[t][:, :], x_rows[bass.ds(b * TPB + t, 1), :, :].rearrange("a p d -> (a p) d"))\
                    .then_inc(x_in[t].sem, 16)

    @block.gpsimd
    def _(pool):

        def group_pow(b):
            pool.wait_ge(gvar_ready.sem, gvar_ready.after(b + 1))
            rstd_of(pool, steps, gsum[:, 3:4], gsum[:, 2:3], LN_EPS, net).then_inc(grstd_ready.sem, 1)

        def row_pow(b, t):
            i = b * TPB + t
            pool.wait_ge(mv_ready.sem, mv_ready.after(i + 1))
            rstd_of(pool, steps, rstd[:, t:t + 1], mv[:, t, 1:2], LN_EPS, net).then_inc(rstd_ready.sem, 1)

        def shift(b, t):
            if t == 0:
                pool.wait_ge(affine.sem, affine.after(b + 1))
                pool.wait_ge(x_kept.sem, x_kept.after((b + 1) * TPB))
            tile = net.x_res[:, bass.ds(b * TPB + t, 1), :].rearrange("p a (h e) -> p (a h) e", e=HD)
            pool.tensor_tensor(tile, tile, gaff[:, 1, :].rearrange("p (h a) -> p h a", a=1).broadcast_to([P, HEADS, HD]), ALU.add)\
                .then_inc(shifted.sem, 1)

        def keep(b, t):
            pool.wait_ge(x_in[t].sem, x_in[t].after((b + 1) * 16))
            pool.tensor_copy(net.x_res[:, bass.ds(b * TPB + t, 1), :].rearrange("p a d -> p (a d)"), xin[t][:, :])\
                .then_inc(x_kept.sem, 1)

        def decay_queries(b, t):
            i = b * TPB + t
            pool.wait_ge(q_copied.sem, q_copied.after(i + 1))
            pool.wait_ge(r_made.sem, r_made.after(i + 1 - TPB))
            pool.tensor_tensor(qS[t][:, :, :], qT[t][:, :, :], net.table["qdecay"].rearrange("p (k t) -> p k t", k=KD),
                               ALU.mult).then_inc(qS_ready.sem, 1)

        steps = Steps(pool_step.sem)
        for t in range(TPB):
            keep(0, t)
            decay_queries(0, t)
        with pool.Fori(1, BATCH) as b:
            steps.enter(b - 1, 5)
            keep(b, 0)
            decay_queries(b, 0)
            group_pow(b - 1)
            keep(b, 1)
            decay_queries(b, 1)
            for t in range(TPB):
                shift(b - 1, t)
            for t in range(TPB):
                row_pow(b - 1, t)
                if t + 2 < TPB:
                    keep(b, t + 2)
                    decay_queries(b, t + 2)
            steps.leave(BATCH - 1)
        group_pow(BATCH - 1)
        for t in range(TPB):
            shift(BATCH - 1, t)
        for t in range(TPB):
            row_pow(BATCH - 1, t)

    @block.scalar
    def _(act):
        def turn(b, t):
            xT_free = b * TPB + t + 1
            act.wait_ge(x_turned.sem, x_turned.after(xT_free))
            nc.scalar.activation(xT[t % 2][:, :, :], pX.rearrange("p (k t) -> p k t", k=KD), ACT.Copy)\
                .then_inc(xT_ready.sem, 1)

        def take(b, t):
            i = b * TPB + t
            act.wait_ge(qv_made.sem, qv_made.after(i + 1))
            act.wait_ge(r_made.sem, r_made.after(i + 1 - TPB))
            nc.scalar.activation(qT[t][:, :, :], pQ, ACT.Copy).then_inc(q_copied.sem, 1)
            nc.scalar.activation(qE[t][:, :, :], pQ, ACT.Copy, scale=net.table["even"])
            nc.scalar.activation(qO[t][:, :, :], pQ, ACT.Copy, scale=net.table["odd"])
            nc.scalar.activation(v[t][:, :], pV, ACT.Copy).then_inc(qv_taken.sem, 1)

        def result(b, t):
            i = b * TPB + t
            act.wait_ge(r_made.sem, r_made.after(i + 1))
            nc.scalar.activation(r_res[:, bass.ds(i, 1), :].rearrange("p a d -> p (a d)"), pR, ACT.Copy)
            act.wait_ge(rsq_free.sem, rsq_free.after(i + 1 - 2))
            nc.scalar.activation(rsq[t % 2][:, :], pR, ACT.Square).then_inc(r_taken.sem, 1)

        with act.Fori(0, BATCH) as b:
            turn(b, 0)
            turn(b, 1)
            take(b, 0)
            for t in range(TPB):
                if t + 1 < TPB:
                    take(b, t + 1)
                if t + 2 < TPB:
                    turn(b, t + 2)
                if t >= 1:
                    result(b, t - 1)
            result(b, TPB - 1)

    @block.tensor
    def _(pe):
        pe.wait_ge(w_in.sem, w_in.after(64))

        def turn(b, t):
            i = b * TPB + t
            pe.wait_ge(x_in[t].sem, x_in[t].after((b + 1) * 16))
            if t:
                pe.wait_ge(xT_ready.sem, xT_ready.after(i))
            if t > 2:
                pe.wait_ge(r_taken.sem, r_taken.after(i - 3))
            elif t == 0 and not isinstance(b, int):
                pe.wait_ge(r_taken.sem, r_taken.after(i))
            for k in range(KD):
                mm = pe.transpose(pX[:, k * P:(k + 1) * P], xin[t][:, k * P:(k + 1) * P], net.table["ident"])
            mm.then_inc(x_turned.sem, 1)

        def project(b, t):
            i = b * TPB + t
            first = isinstance(b, int) and t == 0
            pe.wait_ge(xT_ready.sem, xT_ready.after(i + 1))
            if not first:
                pe.wait_ge(qv_taken.sem, qv_taken.after(i))
            for m in range(2):
                for k in range(KD):
                    pe.matmul(pQ[:, m, :], w[:, k, m * P:(m + 1) * P], xT[t % 2][:, k, :],
                              start=(k == 0), stop=(k == KD - 1))
            for k in range(KD):
                mm = pe.matmul(pV, xT[t % 2][:, k, :], w[:, k, 2 * DIM:], start=(k == 0), stop=(k == KD - 1))
            mm.then_inc(qv_made.sem, 1)
            if not first:
                pe.wait_ge(k_taken.sem, k_taken.after(i))
                pe.wait_ge(ks_ready.sem, ks_ready.after(i if t == 0 else i - 1)) if (t != 1 or not isinstance(b, int)) else None
            for m in range(2):
                for k in range(KD):
                    mm = pe.matmul(pKT[:, m, :], w[:, k, DIM + m * P:DIM + (m + 1) * P], xT[t % 2][:, k, :],
                                   start=(k == 0), stop=(k == KD - 1))
            mm.then_inc(kT_made.sem, 1)

        def scores(b, t):
            i = b * TPB + t
            pe.wait_ge(qv_taken.sem, qv_taken.after(i + 1))
            pe.wait_ge(k_taken.sem, k_taken.after(i + 1))
            for r in range(4):
                pe.wait_ge(s_taken.sem, s_taken.after(4 * i + (r + 1 - 4)))
                rows = slice(32 * r, 32 * r + 32)
                for g in range(4):
                    half, q = g // 2, (qE, qO)[g % 2][t]
                    mm = pe.matmul(pS[r][:, g, :], kT[t % 2][rows, half, :], q[rows, half, :], start=True, stop=True)
                mm.then_inc(s_made.sem, 1)

        def turn_keys(b, t):
            i = b * TPB + t
            pe.wait_ge(k_taken.sem, k_taken.after(i + (2 if t < TPB - 1 else 1)))
            for k in range(KD):
                mm = pe.transpose(pK[:, k * P:(k + 1) * P], kT[t % 2][:, k, :], net.table["ident"])
            mm.then_inc(k_turned.sem, 1)

        def mix(b, t):
            i = b * TPB + t
            pe.wait_ge(xT_ready.sem, xT_ready.after(i + min(4, TPB - t)))
            if t or not isinstance(b, int):
                pe.wait_ge(r_taken.sem, r_taken.after(i))
            if t == 0:
                pe.wait_ge(pkv_ready.sem, pkv_ready.after(1))
            for half in range(KD):
                pe.matmul(pR[:, half * P:(half + 1) * P], qT[t][:, half, :], pkv[:, half, :],
                          start=(half == 0), stop=False, skip_group_check=True)
            if t:
                pe.wait_ge(state_ready.sem, state_ready.after(b * (TPB - 1) + t))
                pe.wait_ge(qS_ready.sem, qS_ready.after(i + 1))
                for half in range(KD):
                    pe.matmul(pR[:, half * P:(half + 1) * P], qS[t][:, half, :], state[t % 2][:, half, :],
                              start=False, stop=False, skip_group_check=True)
            for r in range(4):
                pe.wait_ge(s_taken.sem, s_taken.after(4 * i + r + 1))
                for g in range(4):
                    h = (g // 2) * HPK + 2 * r + g % 2
                    mm = pe.matmul(pR[:, h * HD:(h + 1) * HD], prob[t % 2][:, r, g, :], v[t][:, h * HD:(h + 1) * HD],
                                   start=False, stop=(r == 3 and g == 3), skip_group_check=True)
            mm.then_inc(r_made.sem, 1)
            if t < TPB - 1:
                pe.wait_ge(ks_ready.sem, ks_ready.after(i + 1))
                if t == 0 and not isinstance(b, int):
                    pe.wait_ge(g_taken.sem, g_taken.after(b))
                for half in range(KD):
                    cols = slice(half * P, (half + 1) * P)
                    mm = pe.matmul(pU[:, cols], ks[t % 2][:, cols], v[t][:, cols], start=True, stop=True)
                mm.then_inc(upd_made.sem, 1)

        def totals(b):
            pe.wait_ge(sums_ready.sem, sums_ready.after((b + 1) * TPB))
            pe.wait_ge(state_ready.sem, state_ready.after((b + 1) * (TPB - 1)))
            for t in range(TPB):
                mm = pe.matmul(pG, net.table["ones"], gst[:, t, :, :].rearrange("p a h -> p (a h)"),
                               start=(t == 0), stop=(t == TPB - 1))
            mm.then_inc(g_made.sem, 1)

        def batch(b, before):
            turn(b, 0)
            turn(b, 1)
            project(b, 0)
            if before:
                totals(b - 1)
            for t in range(TPB):
                if t + 1 < TPB:
                    project(b, t + 1)
                if t + 2 < TPB:
                    turn(b, t + 2)
                scores(b, t)
                if t >= 1:
                    mix(b, t - 1)
                turn_keys(b, t)
            mix(b, TPB - 1)

        batch(0, False)
        with pe.Fori(1, BATCH) as b:
            batch(b, True)
        totals(BATCH - 1)

    @block.vector
    def _(dve):
        steps = Steps(dve_step.sem)
        dve.wait_ge(w_in.sem, w_in.after(64))
        blk = net.table["block"].rearrange("p (h e) -> p h e", e=HD)
        for half in range(KD):
            ins = dve.scalar_tensor_tensor(out=pkv[:, half, :].rearrange("p (h e) -> p h e", e=HD),
                                           in0=pkv_raw[:, half:half + 1, :].broadcast_to([P, HPK, HD]),
                                           scalar=float(HEADS * HD), in1=blk, op0=ALU.mult, op1=ALU.mult)
        ins.then_inc(pkv_ready.sem, 1)

        def take(b, t):
            i = b * TPB + t
            dve.wait_ge(kT_made.sem, kT_made.after(i + 1))
            dve.tensor_copy(kT[t % 2][:, :, :], pKT).then_inc(k_taken.sem, 1)

        def decay(b, t):
            i = b * TPB + t
            dec = net.table["decay"].rearrange("p (r g t) -> p r g t", r=4, g=4)
            for r in range(4):
                dve.wait_ge(s_made.sem, s_made.after(4 * i + r + 1))
                if r == 0:
                    dve.wait_ge(r_made.sem, r_made.after(i + 1 - 2))
                dve.tensor_tensor(prob[t % 2][:, r, :, :], pS[r][:, :, :], dec[:, r, :, :], ALU.mult)\
                    .then_inc(s_taken.sem, 1)

        def keys(b, t):
            i = b * TPB + t
            dve.wait_ge(k_turned.sem, k_turned.after(i + 1))
            if t >= 2:
                dve.wait_ge(upd_made.sem, upd_made.after(b * (TPB - 1) + t - 1))
            elif not isinstance(b, int):
                dve.wait_ge(upd_made.sem, upd_made.after(b * (TPB - 1)))
            dve.tensor_tensor(ks[t % 2][:, :], pK, net.table["kdecay"], ALU.mult).then_inc(ks_ready.sem, 1)

        def carry(b, t):
            n = b * (TPB - 1) + t + 1
            dve.wait_ge(upd_made.sem, upd_made.after(n))
            new = state[(t + 1) % 2]
            pu = pU.rearrange("p (k n) -> p k n", k=KD)
            blk2 = net.table["block"].rearrange("p (a n) -> p a n", a=1).broadcast_to([P, KD, P])
            if t == 0:
                dve.tensor_tensor(new[:, :, :], pu, blk2, ALU.mult).then_inc(state_ready.sem, 1)
            else:
                dve.tensor_tensor(upd[:, :, :], pu, blk2, ALU.mult).then_inc(steps.sem, 1)
                dve.wait_ge(steps.sem, steps.done(1))
                dve.wait_ge(state_ready.sem, state_ready.after(n - 1))
                for half in range(KD):
                    ins = dve.scalar_tensor_tensor(out=new[:, half, :], in0=state[t % 2][:, half, :],
                                                   scalar=net.table["tiledecay"][:, half:half + 1], in1=upd[:, half, :],
                                                   op0=ALU.mult, op1=ALU.add)
                ins.then_inc(state_ready.sem, 1)

        def sums(b, t):
            i = b * TPB + t
            dve.wait_ge(r_taken.sem, r_taken.after(i + 1))
            if t == 0 and not isinstance(b, int):
                dve.wait_ge(g_made.sem, g_made.after(b))
            r = r_res[:, bass.ds(i, 1), :].rearrange("p a (h e) -> p (a h) e", e=HD)
            dve.tensor_reduce(gst[:, t, 0, :], r, AX.X, ALU.add)
            dve.tensor_reduce(gst[:, t, 1, :], rsq[t % 2][:, :].rearrange("p (h e) -> p h e", e=HD), AX.X, ALU.add).then_inc(steps.sem, 1)
            steps.done(1)
            dve.wait_ge(steps.sem, steps.done())
            dve.sem_inc(sums_ready.sem, 1)
            dve.sem_inc(rsq_free.sem, 1)

        mean, ex2, var, rs = (gsum[:, j:j + 1] for j in range(4))
        scale, shift, tmp = (gaff[:, j, :] for j in range(3))

        def group_var(b):
            dve.wait_ge(g_made.sem, g_made.after(b + 1))
            dve.tensor_reduce(gsum[:, 0:2], pG.rearrange("p (a h) -> p a h", a=2), AX.X, ALU.add).then_inc(steps.sem, 1)
            dve.wait_ge(steps.sem, steps.done(1))
            dve.sem_inc(g_taken.sem, 1)
            dve.tensor_scalar(gsum[:, 0:2], gsum[:, 0:2], 1.0 / (SEQ * DIM), None, ALU.mult).then_inc(steps.sem, 1)
            dve.wait_ge(steps.sem, steps.done(1))
            dve.tensor_tensor(var, mean, mean, ALU.mult).then_inc(steps.sem, 1)
            dve.wait_ge(steps.sem, steps.done(1))
            dve.tensor_tensor(var, ex2, var, ALU.subtract).then_inc(gvar_ready.sem, 1)

        def group_affine(b):
            dve.wait_ge(grstd_ready.sem, grstd_ready.after(b + 1))
            if not isinstance(b, int) or b:
                dve.wait_ge(shifted.sem, shifted.after(b * TPB))
            dve.tensor_scalar(scale, gnw[:, :], rs, None, ALU.mult).then_inc(steps.sem, 1)
            dve.wait_ge(steps.sem, steps.done(1))
            dve.tensor_scalar(tmp, scale, mean, None, ALU.mult).then_inc(steps.sem, 1)
            dve.wait_ge(steps.sem, steps.done(1))
            dve.tensor_tensor(shift, gnb[:, :], tmp, ALU.subtract).then_inc(affine.sem, 1)

        def flat(i):
            return net.x_res[:, bass.ds(i, 1), :].rearrange("p a d -> p (a d)")

        def add_rows(b, t):
            i = b * TPB + t
            r = r_res[:, bass.ds(i, 1), :].rearrange("p a (h e) -> p (a h) e", e=HD)
            sc = scale.rearrange("p (h a) -> p h a", a=1).broadcast_to([P, HEADS, HD])
            dve.tensor_tensor(y1[t][:, :].rearrange("p (h e) -> p h e", e=HD), r, sc, ALU.mult).then_inc(steps.sem, 1)
            steps.done(1)
            dve.wait_ge(shifted.sem, shifted.after(i + 1))
            dve.wait_ge(steps.sem, steps.done())
            dve.tensor_tensor(y1[t][:, :], y1[t][:, :], flat(i), ALU.add).then_inc(steps.sem, 1)
            dve.wait_ge(steps.sem, steps.done(1))
            dve.bn_stats(bst[:, t, :], y1[t][:, :]).then_inc(steps.sem, 1)
            dve.wait_ge(steps.sem, steps.done(1))
            dve.sem_inc(net.passed, 1)
            dve.bn_aggr(mv[:, t, :], bst[:, t, :]).then_inc(mv_ready.sem, 1)

        def norm_rows(b, t):
            i = b * TPB + t
            dve.wait_ge(rstd_ready.sem, rstd_ready.after(i + 1))
            dve.tensor_scalar(flat(i), y1[t][:, :], mv[:, t, 0:1], rstd[:, t:t + 1], ALU.subtract, ALU.mult)

        def batch(b, before):
            take(b, 0)
            if before:
                group_var(b - 1)
            for t in range(TPB):
                if t + 1 < TPB:
                    take(b, t + 1)
                decay(b, t)
                if t >= 1:
                    carry(b, t - 1)
                    sums(b, t - 1)
                keys(b, t)
                if before and t == 0:
                    group_affine(b - 1)
                if before:
                    add_rows(b - 1, t)
                if before and t:
                    norm_rows(b - 1, t - 1)
            sums(b, TPB - 1)
            if before:
                norm_rows(b - 1, TPB - 1)

        batch(0, False)
        with dve.Fori(1, BATCH) as b:
            steps.enter(b - 1, 23)
            batch(b, True)
            steps.leave(BATCH - 1)
        group_var(BATCH - 1)
        group_affine(BATCH - 1)
        for t in range(TPB):
            add_rows(BATCH - 1, t)
        for t in range(TPB):
            norm_rows(BATCH - 1, t)


def rstd_of(pool, steps, out, var, eps, net, scale=1.0):
    pool.sem_inc(net.passed_pool, 1)
    pool.tensor_scalar(out, var, scale, eps, ALU.mult, ALU.add).then_inc(steps.sem, 1)
    pool.wait_ge(steps.sem, steps.done(1))
    return pool.tensor_tensor(out, out, net.table["minushalf"][:, 0:out.shape[1]], ALU.pow)


def staggered(eng, count, front, back, steps=None, per=0):
    front(0, 0)
    with eng.Fori(0, count // 2 - 1) as i:
        if steps:
            steps.enter(i, per)
        for p in range(2):
            front(2 * i + p + 1, (p + 1) % 2)
            back(2 * i + p, p)
        if steps:
            steps.leave(count // 2 - 1)
    front(count - 1, 1)
    back(count - 2, 0)
    back(count - 1, 1)


def tile_of(net, i):
    return net.x_res[:, bass.ds(i, 1), :].rearrange("p a d -> p (a d)")


class Phase:

    def __init__(self, net, ctx, prefix):
        self.net, self.ctx, self.prefix = net, ctx, prefix

    def sb(self, name, shape, dt=F32):
        return self.ctx.enter_context(self.net.nc.sbuf_tensor(f"{self.prefix}_{name}", shape, dt))

    def ps(self, name, shape):
        return self.ctx.enter_context(self.net.nc.psum_tensor(f"{self.prefix}_{name}", shape, F32))

    def sig(self, name, head=0):
        return Signal(self.net, self.ctx, f"{self.prefix}_{name}", head)


def prepare(net, ctx):
    nc, a = net.nc, net.args
    ph = Phase(net, ctx, "w")
    raw_fc = ph.sb("raw_fc", [P, NH, DIM])
    raw_pj = ph.sb("raw_pj", [P, KD, HID])
    neg = ph.sb("neg", [P, 2, NH * DIM])
    sq = [ph.sb(f"sq{i}", [P, KD, DIM]) for i in range(5)]
    absum, thr = ph.sb("absum", [P, 2]), ph.sb("thr", [P, 2, 2])
    pT = [ph.ps(f"pT{i}", [P, 4, P]) for i in range(2)]
    pM = ph.ps("pM", [P, 2])
    c_in, fc_in, pj_in, sq_in = (ph.sig(n) for n in ("c_in", "fc_in", "pj_in", "sq_in"))
    sums, total, quant, turned, taken, step = (ph.sig(n) for n in ("sums", "total", "quant", "turned", "taken", "step"))

    banks = []
    for k in range(KD):
        for c in range(0, NH, 4):
            banks.append(([(raw_fc, c + j, k) for j in range(4)], net.wfcT[:, k, c * P:(c + 4) * P]))
    for c in range(0, NH, 2):
        banks.append(([(raw_pj, m, c + j) for j in range(2) for m in range(KD)],
                      net.wpjT[:, c:c + 2, :].rearrange("p c n -> p (c n)")))
    for n in range(5):
        dst = net.wqkvT[:, :, n * DIM:(n + 1) * DIM] if n < 3 else (net.w1T, net.w2T)[n - 3][:, :, :]
        banks.append(([(sq[n], m, k) for k in range(KD) for m in range(KD)], dst))

    nc.all_engine_barrier()
    block = ctx.enter_context(nc.Block())

    @block.sync
    def _(sp):
        sp.dma_start(net.const[:, :], a["consts"]).then_inc(c_in.sem, 16)
        sp.dma_start(raw_fc[:, :, :], a["L0_ffn_W_fc"].rearrange("(c p) n -> p c n", p=P)).then_inc(fc_in.sem, 16)
        sp.dma_start(raw_pj[:, :, :], a["L0_ffn_W_proj"].rearrange("(c p) n -> p c n", p=P)).then_inc(pj_in.sem, 16)
        for n, name in enumerate(("Wq", "Wk", "Wv", "W1", "W2")):
            sp.dma_start(sq[n][:, :, :], a["L1_attn_" + name].rearrange("(c p) n -> p c n", p=P)).then_inc(sq_in.sem, 16)

    @block.vector
    def _(dve):
        steps = Steps(step.sem)
        dve.wait_ge(fc_in.sem, fc_in.after(16))
        dve.tensor_reduce(absum[:, 0:1], raw_fc[:, :, :].rearrange("p c n -> p (c n)"), AX.X, ALU.add,
                          apply_absolute_value=True)
        dve.wait_ge(pj_in.sem, pj_in.after(16))
        dve.tensor_reduce(absum[:, 1:2], raw_pj[:, :, :].rearrange("p c n -> p (c n)"), AX.X, ALU.add,
                          apply_absolute_value=True).then_inc(sums.sem, 1)
        dve.wait_ge(total.sem, total.after(1))
        n = float(HID * DIM)
        dve.tensor_scalar(thr[:, 0, :], pM[:, :], 1.0 / n, ABS_EPS, ALU.mult, ALU.add).then_inc(steps.sem, 1)
        dve.wait_ge(steps.sem, steps.done(1))
        dve.tensor_scalar(thr[:, 0, :], thr[:, 0, :], 0.5, None, ALU.mult).then_inc(steps.sem, 1)
        dve.wait_ge(steps.sem, steps.done(1))
        dve.tensor_scalar(thr[:, 1, :], thr[:, 0, :], -1.0, None, ALU.mult).then_inc(steps.sem, 1)
        dve.wait_ge(steps.sem, steps.done(1))
        for j, raw in enumerate((raw_fc, raw_pj)):
            flat = raw[:, :, :].rearrange("p c n -> p (c n)")
            dve.tensor_scalar(neg[:, j, :], flat, thr[:, 1, j:j + 1], -1.0, ALU.is_lt, ALU.mult).then_inc(steps.sem, 1)
            dve.wait_ge(steps.sem, steps.done(1))
            dve.scalar_tensor_tensor(out=flat, in0=flat, scalar=thr[:, 0, j:j + 1], in1=neg[:, j, :],
                                     op0=ALU.is_gt, op1=ALU.add).then_inc(quant.sem, 1)
        for n, (_, dst) in enumerate(banks):
            dve.wait_ge(turned.sem, turned.after(n + 1))
            src = pT[n % 2][:, :, :]
            if len(dst.shape) == 3:
                src = src.rearrange("p (k m) n -> p k (m n)", k=KD)
            else:
                src = src.rearrange("p k n -> p (k n)")
            dve.tensor_copy(dst, src).then_inc(taken.sem, 1)

    @block.tensor
    def _(pe):
        pe.wait_ge(c_in.sem, c_in.after(16))
        pe.wait_ge(sums.sem, sums.after(1))
        pe.matmul(pM[:, :], net.table["ones"], absum[:, :], start=True, stop=True).then_inc(total.sem, 1)
        for n, (blocks, _) in enumerate(banks):
            if n >= 2:
                pe.wait_ge(taken.sem, taken.after(n - 1))
            if blocks[0][0] is raw_fc:
                pe.wait_ge(quant.sem, quant.after(1))
            elif blocks[0][0] is raw_pj:
                pe.wait_ge(quant.sem, quant.after(2))
            else:
                pe.wait_ge(sq_in.sem, sq_in.after(80))
            for j, (src, row, col) in enumerate(blocks):
                mm = pe.transpose(pT[n % 2][:, j, :], src[:, row, col * P:(col + 1) * P], net.table["ident"])
            mm.then_inc(turned.sem, 1)


def ternary_ffn(net, ctx):
    nc, a = net.nc, net.args
    ph = Phase(net, ctx, "f")
    two = range(2)
    lnw, lnb = ph.sb("lnw", [P, NH]), ph.sb("lnb", [P, NH])
    xs = [ph.sb(f"xs{i}", [P, DIM]) for i in two]
    xT = [ph.sb(f"xT{i}", [P, KD, P]) for i in two]
    h = [ph.sb(f"h{i}", [P, HID]) for i in two]
    hT = [ph.sb(f"hT{i}", [P, NH, P]) for i in two]
    y = [ph.sb(f"y{i}", [P, DIM]) for i in two]
    hst = [ph.sb(f"hst{i}", [P, 2, 6]) for i in two]
    yst = [ph.sb(f"yst{i}", [P, 6]) for i in two]
    hmv, ymv = [ph.sb(f"hmv{i}", [P, 2]) for i in two], [ph.sb(f"ymv{i}", [P, 2]) for i in two]
    hrs, yrs = [ph.sb(f"hrs{i}", [P, 1]) for i in two], [ph.sb(f"yrs{i}", [P, 1]) for i in two]
    pX = ph.ps("pX", [P, KD, P])
    pH = [ph.ps(f"pH{i}", [P, 2, 512]) for i in two]
    pT = [ph.ps(f"pT{i}", [P, 4, P]) for i in two]
    pY = ph.ps("pY", [P, 512])
    ln_in, copied, xT_ready, up_made = (ph.sig(n) for n in ("ln_in", "copied", "xT_ready", "up_made"))
    turned, gelued = (ph.sig(n, 2) for n in ("turned", "gelued"))
    hmv_ready, hrs_ready, normed, h_turned = (ph.sig(n) for n in ("hmv_ready", "hrs_ready", "normed", "h_turned"))
    hT_act, hT_dve, down_made, y_taken = (ph.sig(n, 1) for n in ("hT_act", "hT_dve", "down_made", "y_taken"))
    ymv_ready, yrs_ready, step, pool_step = (ph.sig(n) for n in ("ymv_ready", "yrs_ready", "step", "pool_step"))

    nc.all_engine_barrier()
    block = ctx.enter_context(nc.Block())

    @block.sync
    def _(sp):
        with nc.allow_non_contiguous_dma(reason="2 x 4 KB, once"):
            for t, name in ((lnw, "L0_ffn_ln_w"), (lnb, "L0_ffn_ln_b")):
                sp.dma_start(t[:, :], a[name].rearrange("(c p) -> p c", p=P)).then_inc(ln_in.sem, 16)

    @block.gpsimd
    def _(pool):
        steps = Steps(pool_step.sem)

        def front(i, p):
            pool.wait_ge(turned.sem, turned.after(i + 1 - 2))
            pool.tensor_copy(xs[p][:, :], tile_of(net, i)).then_inc(copied.sem, 1)
            pool.wait_ge(hmv_ready.sem, hmv_ready.after(i + 1))
            rstd_of(pool, steps, hrs[p][:, :], hmv[p][:, 1:2], LN_EPS, net).then_inc(hrs_ready.sem, 1)

        def back(i, p):
            pool.wait_ge(ymv_ready.sem, ymv_ready.after(i + 1))
            rstd_of(pool, steps, yrs[p][:, :], ymv[p][:, 1:2], LN_EPS, net).then_inc(yrs_ready.sem, 1)

        staggered(pool, TILES, front, back, steps, 4)

    @block.tensor
    def _(pe):

        def front(i, p):
            pe.wait_ge(copied.sem, copied.after(i + 1))
            if not (isinstance(i, int) and i == 0):
                pe.wait_ge(xT_ready.sem, xT_ready.after(i))
            for k in range(KD):
                mm = pe.transpose(pX[:, k, :], xs[p][:, k * P:(k + 1) * P], net.table["ident"])
            mm.then_inc(turned.sem, 1)
            pe.wait_ge(xT_ready.sem, xT_ready.after(i + 1))
            pe.wait_ge(gelued.sem, gelued.after(i + 1 - 2))
            for n in range(2):
                for k in range(KD):
                    mm = pe.matmul(pH[p][:, n, :], xT[p][:, k, :], net.wfcT[:, k, n * 512:(n + 1) * 512],
                                   start=(k == 0), stop=(k == KD - 1))
            mm.then_inc(up_made.sem, 1)

        def back(i, p):
            pe.wait_ge(normed.sem, normed.after(i + 1))
            for half in (1, 0):
                if not (isinstance(i, int) and i == 0):
                    pe.wait_ge((hT_act, hT_dve)[half].sem, (hT_act, hT_dve)[half].after(i))
                for j in range(4):
                    c = 4 * half + j
                    mm = pe.transpose(pT[half][:, j, :], h[p][:, c * P:(c + 1) * P], net.table["ident"])
                mm.then_inc(h_turned.sem, 1)
            if not (isinstance(i, int) and i == 0):
                pe.wait_ge(y_taken.sem, y_taken.after(i))
            for half in (1, 0):
                pe.wait_ge((hT_act, hT_dve)[half].sem, (hT_act, hT_dve)[half].after(i + 1))
                for j in range(4):
                    c = 4 * half + j
                    mm = pe.matmul(pY[:, 0:DIM], hT[p][:, c, :], net.wpjT[:, c, :],
                                   start=(half == 1 and j == 0), stop=(half == 0 and j == 3))
            mm.then_inc(down_made.sem, 1)

        staggered(pe, TILES, front, back)

    @block.scalar
    def _(act):
        act.wait_ge(ln_in.sem, ln_in.after(32))

        def front(i, p):
            act.wait_ge(turned.sem, turned.after(i + 1))
            nc.scalar.activation(xT[p][:, :, :], pX[:, :, :], ACT.Copy).then_inc(xT_ready.sem, 1)
            act.wait_ge(up_made.sem, up_made.after(i + 1))
            for n in range(2):
                ins = nc.scalar.activation(h[p][:, n * 512:(n + 1) * 512], pH[p][:, n, :], ACT.Gelu)
            ins.then_inc(gelued.sem, 1)

        def back(i, p):
            act.wait_ge(h_turned.sem, h_turned.after(2 * i + 2))
            for j in range(4):
                ins = nc.scalar.activation(hT[p][:, j, :], pT[0][:, j, :], ACT.Identity,
                                           bias=lnb[:, j:j + 1], scale=lnw[:, j:j + 1])
            ins.then_inc(hT_act.sem, 1)

        staggered(act, TILES, front, back)

    @block.vector
    def _(dve):
        steps = Steps(step.sem)
        dve.wait_ge(ln_in.sem, ln_in.after(32))

        def take(i, p):
            dve.wait_ge(h_turned.sem, h_turned.after(2 * i + 1))
            for j in range(4):
                c = 4 + j
                ins = dve.tensor_scalar(hT[p][:, c, :], pT[1][:, j, :], lnw[:, c:c + 1], lnb[:, c:c + 1], ALU.mult, ALU.add)
            ins.then_inc(hT_dve.sem, 1)

        def stats(i, p):
            dve.wait_ge(gelued.sem, gelued.after(i + 1))
            for n in range(2):
                ins = dve.bn_stats(hst[p][:, n, :], h[p][:, n * 512:(n + 1) * 512])
            ins.then_inc(steps.sem, 1)
            dve.wait_ge(steps.sem, steps.done(1))
            dve.sem_inc(net.passed, 1)
            dve.bn_aggr(hmv[p][:, :], hst[p][:, :, :].rearrange("p a b -> p (a b)")).then_inc(hmv_ready.sem, 1)

        def normalise(i, p):
            dve.wait_ge(hrs_ready.sem, hrs_ready.after(i + 1))
            dve.tensor_scalar(h[p][:, :], h[p][:, :], hmv[p][:, 0:1], hrs[p][:, :], ALU.subtract, ALU.mult)\
                .then_inc(normed.sem, 1)

        def add_rows(i, p):
            dve.wait_ge(down_made.sem, down_made.after(i + 1))
            dve.tensor_tensor(y[p][:, :], pY[:, 0:DIM], tile_of(net, i), ALU.add).then_inc(steps.sem, 1)
            steps.done(1)
            dve.wait_ge(steps.sem, steps.done())
            dve.sem_inc(y_taken.sem, 1)
            dve.bn_stats(yst[p][:, :], y[p][:, :]).then_inc(steps.sem, 1)
            dve.wait_ge(steps.sem, steps.done(1))
            dve.sem_inc(net.passed, 1)
            dve.bn_aggr(ymv[p][:, :], yst[p][:, :]).then_inc(ymv_ready.sem, 1)

        def norm_rows(i, p):
            dve.wait_ge(yrs_ready.sem, yrs_ready.after(i + 1))
            dve.tensor_scalar(tile_of(net, i), y[p][:, :], ymv[p][:, 0:1], yrs[p][:, :], ALU.subtract, ALU.mult)

        stats(0, 0)
        normalise(0, 0)

        def step_of(i, p, more=True):
            take(i, p)
            if more:
                stats(i + 1, 1 - p)
                normalise(i + 1, 1 - p)
            add_rows(i, p)
            norm_rows(i, p)

        with dve.Fori(0, TILES // 2 - 1) as i:
            steps.enter(i, 6)
            for p in range(2):
                step_of(2 * i + p, p)
            steps.leave(TILES // 2 - 1)
        step_of(TILES - 2, 0)
        step_of(TILES - 1, 1, False)


def attention_inputs(net, ctx):
    nc, a = net.nc, net.args
    ph = Phase(net, ctx, "q")
    two = range(2)
    g1 = ph.sb("g1", [P, KD])
    lam, lmb = ph.sb("lam", [P, 4]), ph.sb("lmb", [P, 4])
    qscale = ph.sb("qscale", [P, 1])
    sqv = ph.sb("sqv", [P, TPB, DIM])
    ssq = [ph.sb(f"ssq{i}", [P, TPB]) for i in two]
    rs = [ph.sb(f"rs{i}", [P, TPB]) for i in two]
    xn = [ph.sb(f"xn{i}", [P, TPB, DIM]) for i in two]
    xT = [ph.sb(f"xT{i}", [P, KD, SEQ]) for i in two]
    ex = [ph.sb(f"ex{i}", [P, SEQ]) for i in two]
    rl = [ph.sb(f"rl{i}", [P, SEQ]) for i in two]
    res = [[ph.sb(f"res{n}{i}", [P, KD, SEQ]) for n in range(3)] for i in two]
    pX = [ph.ps(f"pX{k}", [P, SEQ]) for k in range(KD)]
    pE = [ph.ps(f"pE{i}", [P, SEQ]) for i in two]
    pV = [ph.ps(f"pV{i}", [P, SEQ]) for i in two]
    par_in, lam_ready, exp_lam, qs_ready = (ph.sig(n) for n in ("par_in", "lam_ready", "exp_lam", "qs_ready"))
    ssq_ready, rs_ready, xn_ready, turned, xT_ready = (ph.sig(n, 1) for n in ("ssq_ready", "rs_ready", "xn_ready", "turned", "xT_ready"))
    e_made, e_taken, v_made, v_taken, elu_ready = (ph.sig(n, 1) for n in ("e_made", "e_taken", "v_made", "v_taken", "elu_ready"))
    ex_free, stored = ph.sig("ex_free", 2), [ph.sig(f"stored{i}", 16 * 3) for i in two]
    step, pool_step = ph.sig("step"), ph.sig("pool_step")

    nc.all_engine_barrier()
    block = ctx.enter_context(nc.Block())

    @block.sync
    def _(sp):
        with nc.allow_non_contiguous_dma(reason="1 KB, once"):
            sp.dma_start(g1[:, :], a["L1_attn_g1"].rearrange("(c p) -> p c", p=P)).then_inc(par_in.sem, 16)
        sp.dma_start(lam[:, :], a["L1_attn_lambda_params"].rearrange("(a h) -> a h", a=1).broadcast_to([P, 4])).then_inc(par_in.sem, 16)

        def store(b, p):
            sp.wait_ge(v_taken.sem, v_taken.after(2 * b + 2))
            for n in range(3):
                sp.dma_start(net.qkv_dram[n, :, bass.ds(b * SEQ, SEQ)].rearrange("(k p) t -> p k t", p=P), res[p][n][:, :, :])\
                    .then_inc(stored[p].sem, 16)

        with sp.Fori(0, BATCH // 2) as i:
            for p in two:
                store(2 * i + p, p)
        for p in two:
            sp.wait_ge(stored[p].sem, stored[p].after(48 * BATCH // 2))

    @block.gpsimd
    def _(pool):
        steps = Steps(pool_step.sem)

        def front(b, p):
            pool.wait_ge(ssq_ready.sem, ssq_ready.after(b + 1))
            rstd_of(pool, steps, rs[p][:, :], ssq[p][:, :], RMS_EPS, net, 1.0 / DIM).then_inc(rs_ready.sem, 1)

        staggered(pool, BATCH, front, lambda b, p: None, steps, 2)

    @block.scalar
    def _(act):
        act.wait_ge(par_in.sem, par_in.after(32))
        act.wait_ge(lam_ready.sem, lam_ready.after(1))
        nc.scalar.activation(lmb[:, 2:4], lmb[:, 0:2], ACT.Exp).then_inc(exp_lam.sem, 1)

        def front(b, p):
            xn_free = b + 1 - 2
            if not isinstance(b, int) or b >= 2:
                act.wait_ge(turned.sem, turned.after(xn_free))
                act.sem_inc(net.passed_act, 1)
            for t in range(TPB):
                ins = nc.scalar.activation(sqv[:, t, :], tile_of(net, b * TPB + t), ACT.Square, accum_out=ssq[p][:, t:t + 1])
            ins.then_inc(ssq_ready.sem, 1)
            act.wait_ge(rs_ready.sem, rs_ready.after(b + 1))
            act.sem_inc(net.passed_act, 1)
            for t in range(TPB):
                ins = nc.scalar.activation(xn[p][:, t, :], tile_of(net, b * TPB + t), ACT.Copy, scale=rs[p][:, t:t + 1])
            ins.then_inc(xn_ready.sem, 1)

        def back(b, p):
            for n in range(4):
                m = 4 * b + n
                act.wait_ge(e_made.sem, e_made.after(m + 1))
                act.wait_ge(ex_free.sem, ex_free.after(m + 1 - 2))
                nc.scalar.activation(ex[n % 2][:, :], pE[n % 2][:, :], ACT.Exp)
                nc.scalar.activation(rl[n % 2][:, :], pE[n % 2][:, :], ACT.Relu).then_inc(e_taken.sem, 1)

        staggered(act, BATCH, front, back)

    @block.tensor
    def _(pe):
        def front(b, p):
            pe.wait_ge(xn_ready.sem, xn_ready.after(b + 1))
            if not (isinstance(b, int) and b == 0):
                pe.wait_ge(xT_ready.sem, xT_ready.after(b))
            for k in range(KD):
                for t in range(TPB):
                    mm = pe.transpose(pX[k][:, t * P:(t + 1) * P], xn[p][:, t, k * P:(k + 1) * P], net.table["ident"])
            mm.then_inc(turned.sem, 1)

        def back(b, p):
            first = isinstance(b, int) and b == 0
            pe.wait_ge(xT_ready.sem, xT_ready.after(b + 1))
            for n in range(6):
                if n < 4:
                    if not (first and n < 2):
                        pe.wait_ge(e_taken.sem, e_taken.after(4 * b + n - 1))
                    out, made = pE[n % 2], e_made
                else:
                    if not first:
                        pe.wait_ge(v_taken.sem, v_taken.after(2 * b + n - 4 - 1))
                    out, made = pV[n % 2], v_made
                for k in range(KD):
                    mm = pe.matmul(out[:, :], net.wqkvT[:, k, n * P:(n + 1) * P], xT[p][:, k, :], start=(k == 0), stop=(k == KD - 1))
                mm.then_inc(made.sem, 1)

        staggered(pe, BATCH, front, back)

    @block.vector
    def _(dve):
        steps = Steps(step.sem)
        dve.wait_ge(par_in.sem, par_in.after(32))
        lv = lam[:, :].rearrange("p (a b) -> p a b", b=2)
        dve.tensor_tensor(lmb[:, 0:2], lv[:, :, 0], lv[:, :, 1], ALU.mult).then_inc(lam_ready.sem, 1)
        dve.wait_ge(exp_lam.sem, exp_lam.after(1))
        dve.tensor_tensor(lmb[:, 0:1], lmb[:, 2:3], lmb[:, 3:4], ALU.subtract).then_inc(steps.sem, 1)
        dve.wait_ge(steps.sem, steps.done(1))
        dve.tensor_scalar(lmb[:, 0:1], lmb[:, 0:1], LAMBDA_INIT, 1.0, ALU.add, ALU.add).then_inc(steps.sem, 1)
        dve.wait_ge(steps.sem, steps.done(1))
        dve.tensor_scalar(lmb[:, 1:2], net.table["firsthalf"], lmb[:, 0:1], 1.0, ALU.mult, ALU.add).then_inc(steps.sem, 1)
        dve.wait_ge(steps.sem, steps.done(1))
        dve.tensor_tensor(lmb[:, 1:2], lmb[:, 1:2], lmb[:, 0:1], ALU.subtract).then_inc(steps.sem, 1)
        dve.wait_ge(steps.sem, steps.done(1))
        dve.tensor_scalar(qscale[:, :], lmb[:, 1:2], RET_SCALE, None, ALU.mult).then_inc(steps.sem, 1)
        dve.wait_ge(steps.sem, steps.done(1))

        def front(b, p):
            dve.wait_ge(turned.sem, turned.after(b + 1))
            for k in range(KD):
                ins = dve.tensor_scalar(xT[p][:, k, :], pX[k][:, :], g1[:, k:k + 1], None, ALU.mult)
            ins.then_inc(xT_ready.sem, 1)

        def back(b, p):
            dve.wait_ge(stored[p].sem, stored[p].after(48 * (b // 2) if isinstance(b, int) else 24 * (b - p)))
            for n in range(4):
                dve.wait_ge(e_taken.sem, e_taken.after(4 * b + n + 1))
                dve.scalar_tensor_tensor(out=rl[n % 2][:, :], in0=ex[n % 2][:, :], scalar=1.0, in1=rl[n % 2][:, :],
                                         op0=ALU.min, op1=ALU.add).then_inc(steps.sem, 1)
                dve.wait_ge(steps.sem, steps.done(1))
                dst = res[p][n // 2][:, n % 2, :]
                if n < 2:
                    ins = dve.tensor_scalar(dst, rl[n % 2][:, :], 1.0, qscale[:, :], ALU.subtract, ALU.mult)
                else:
                    ins = dve.tensor_scalar(dst, rl[n % 2][:, :], 1.0, None, ALU.subtract)
                ins.then_inc(ex_free.sem, 1)
            for n in range(2):
                dve.wait_ge(v_made.sem, v_made.after(2 * b + n + 1))
                dve.tensor_copy(res[p][2][:, n, :], pV[n][:, :]).then_inc(v_taken.sem, 1)

        staggered(dve, BATCH, front, back, steps, 8)


def per_token_attention(net, ctx):
    nc, a = net.nc, net.args
    ph = Phase(net, ctx, "t")
    two = range(2)
    kb, vb = ph.sb("kb", [P, P, HALF]), ph.sb("vb", [P, P, HALF])
    q = [ph.sb(f"q{i}", [P, HEADS, HALF]) for i in two]
    at = ph.sb("at", [P, HALF, HEADS])
    ob = ph.sb("ob", [P, HEADS, P])
    g2 = ph.sb("g2", [P, HD])
    g3 = ph.sb("g3", [P, DIM])
    sqall = ph.sb("sqall", [P, GROUPS * DIM])
    sqv = ph.sb("sqv", [P, DIM])
    hs, hr, hy = ph.sb("hs", [P, GROUPS * HEADS]), ph.sb("hr", [P, GROUPS * HEADS]), ph.sb("hy", [P, GROUPS * HEADS])
    es, er = ph.sb("es", [P, GROUPS]), ph.sb("er", [P, GROUPS])
    mrow = [ph.sb(f"mrow{i}", [P, DIM]) for i in two]
    pA = [ph.ps(f"pA{i}", [P, HALF // 2, HEADS]) for i in two]
    pO = [ph.ps(f"pO{i}", [P, HALF // 2, HEADS]) for i in two]
    pW = [ph.ps(f"pW{i}", [P, 4, P]) for i in range(4)]
    g_in, cleared_k, cleared_v = (ph.sig(n) for n in ("g_in", "cleared_k", "cleared_v"))
    k_in, v_in, q_in = ph.sig("k_in"), ph.sig("v_in"), [ph.sig(f"q_in{i}") for i in two]
    a_made, o_made = ph.sig("a_made", 2), ph.sig("o_made", 1)
    a_act, a_dve, o_act, o_dve, w_made, w_act, w_dve = (
        ph.sig(n, 1) for n in ("a_act", "a_dve", "o_act", "o_dve", "w_made", "w_act", "w_dve"))
    sq_ready, sq_act, root_ready, es_ready, er_ready, step = (
        ph.sig(n) for n in ("sq_ready", "sq_act", "root_ready", "es_ready", "er_ready", "step"))
    att = net.att_res

    nc.all_engine_barrier()
    block = ctx.enter_context(nc.Block())

    @block.sync
    def _(sp):
        sp.dma_start(g2[:, :], a["L1_attn_g2"].rearrange("(a h) -> a h", a=1).broadcast_to([P, HD])).then_inc(g_in.sem, 16)
        sp.dma_start(g3[:, :], a["L1_attn_g3"].rearrange("(a h) -> a h", a=1).broadcast_to([P, DIM])).then_inc(g_in.sem, 16)
        q_src = net.qkv_dram[0].rearrange("(h e) t -> e h t", e=HD)
        k_src = net.qkv_dram[1].rearrange("(h e) t -> e h t", e=HD)
        v_src = net.qkv_dram[2].rearrange("(h d) t -> h d t", d=HD)

        def rows(dst, src, u, s, diagonal, sig):
            for j in range(GROUPS):
                to = dst[j * HD:(j + 1) * HD, j * HD:(j + 1) * HD, :] if diagonal else dst[j * HD:(j + 1) * HD, :, :]
                sp.dma_start(to, src[:, :, bass.ds(u * UNIT + j * P + s * HALF, HALF)]).then_inc(sig.sem, 16)

        with sp.Fori(0, UNITS) as u:
            for s in two:
                n = 2 * u + s
                sp.wait_ge(a_made.sem, a_made.after(2 * n - 2))
                rows(q[s], q_src, u, s, False, q_in[s])
                if s == 0:
                    sp.wait_ge(cleared_k.sem, cleared_k.after(1))
                sp.wait_ge(a_made.sem, a_made.after(2 * n))
                rows(kb, k_src, u, s, True, k_in)
                if s == 0:
                    sp.wait_ge(cleared_v.sem, cleared_v.after(1))
                sp.wait_ge(o_made.sem, o_made.after(2 * n))
                rows(vb, v_src, u, s, True, v_in)

    @block.gpsimd
    def _(pool):
        pool.memset(vb[:, :, :].rearrange("p a b -> p (a b)"), 0.0).then_inc(cleared_v.sem, 1)

    @block.tensor
    def _(pe):

        with pe.Fori(0, UNITS) as u:
            for s in two:
                n = 2 * u + s
                pe.wait_ge(k_in.sem, k_in.after(128 * (n + 1)))
                pe.wait_ge(q_in[s].sem, q_in[s].after(128 * (u + 1)))
                for c in two:
                    pe.wait_ge((a_act, a_dve)[c].sem, (a_act, a_dve)[c].after(n))
                    for t in range(c * 32, c * 32 + 32):
                        mm = pe.matmul(pA[c][:, t - c * 32, :], kb[:, :, t], q[s][:, :, t], start=True, stop=True)
                    mm.then_inc(a_made.sem, 1)
                pe.wait_ge(v_in.sem, v_in.after(128 * (n + 1)))
                for c in two:
                    pe.wait_ge((a_act, a_dve)[c].sem, (a_act, a_dve)[c].after(n + 1))
                    pe.wait_ge((o_act, o_dve)[c].sem, (o_act, o_dve)[c].after(n))
                    for t in range(c * 32, c * 32 + 32):
                        mm = pe.matmul(pO[c][:, t - c * 32, :], vb[:, :, t], at[:, t, :], start=True, stop=True)
                    mm.then_inc(o_made.sem, 1)
            pe.wait_ge(o_act.sem, o_act.after(2 * (u + 1)))
            pe.wait_ge(o_dve.sem, o_dve.after(2 * (u + 1)))
            for r in range(4):
                pe.wait_ge((w_act, w_dve)[r // 2].sem, (w_act, w_dve)[r // 2].after(2 * u + r % 2))
                for g in range(4):
                    mm = pe.transpose(pW[r][:, g, :], ob[:, 4 * r + g, :], net.table["ident"])
                mm.then_inc(w_made.sem, 1)

    def heads_of(u, r):
        return att[:, bass.ds(u * GROUPS, GROUPS), 4 * r * HD:4 * (r + 1) * HD].rearrange("p j (g d) -> p g j d", d=HD)

    def unit_rows(u):
        return att[:, bass.ds(u * GROUPS, GROUPS), :]

    def ob_at(s, c):
        at0 = s * HALF + c * 32
        return ob[:, :, at0:at0 + 32].rearrange("p h t -> p t h")

    @block.scalar
    def _(act):
        with act.Fori(0, UNITS) as u:
            for s in two:
                n = 2 * u + s
                act.wait_ge(a_made.sem, a_made.after(2 * n + 1))
                nc.scalar.activation(at[:, 0:32, :], pA[0][:, :, :], ACT.Copy).then_inc(a_act.sem, 1)
                act.wait_ge(o_made.sem, o_made.after(2 * n + 1))
                if s == 0:
                    act.wait_ge(w_made.sem, w_made.after(4 * u))
                nc.scalar.activation(ob_at(s, 0), pO[0][:, :, :], ACT.Copy).then_inc(o_act.sem, 1)
            for r in two:
                act.wait_ge(w_made.sem, w_made.after(4 * u + r + 1))
                act.sem_inc(net.passed_act, 1)
                ins = nc.scalar.activation(heads_of(u, r), pW[r][:, :, :].rearrange("p g (j d) -> p g j d", d=HD), ACT.Copy)
                ins.then_inc(w_act.sem, 1)
            act.wait_ge(sq_ready.sem, sq_ready.after(u + 1))
            nc.scalar.activation(hr[:, :], hs[:, :], ACT.Sqrt, bias=net.table["rmseps"], scale=1.0 / HD).then_inc(root_ready.sem, 1)
            act.wait_ge(es_ready.sem, es_ready.after(u + 1))
            act.sem_inc(net.passed_act, 1)
            for j in range(GROUPS):
                ins = nc.scalar.activation(sqall[:, j * DIM:(j + 1) * DIM], att[:, bass.ds(u * GROUPS + j, 1), :].rearrange("p a d -> p (a d)"),
                                           ACT.Square, accum_out=es[:, j:j + 1])
            ins.then_inc(sq_act.sem, 1)
            act.wait_ge(sq_act.sem, sq_act.after(u + 1))
            nc.scalar.activation(er[:, :], es[:, :], ACT.Sqrt, bias=net.table["rmseps"], scale=1.0 / DIM).then_inc(er_ready.sem, 1)

    @block.vector
    def _(dve):
        dve.memset(kb[:, :, :].rearrange("p a b -> p (a b)"), 0.0).then_inc(cleared_k.sem, 1)
        steps = Steps(step.sem)
        dve.wait_ge(g_in.sem, g_in.after(32))
        dve.tensor_scalar(g2[:, :], g2[:, :], 1.0 - LAMBDA_INIT, None, ALU.mult).then_inc(steps.sem, 1)
        dve.wait_ge(steps.sem, steps.done(1))

        def inverse(root, mean_sq_scale, sums, tmp, out):
            dve.reciprocal(out, root).then_inc(steps.sem, 1)
            dve.wait_ge(steps.sem, steps.done(1))
            dve.tensor_scalar(root, sums, mean_sq_scale, RMS_EPS, ALU.mult, ALU.add).then_inc(steps.sem, 1)
            dve.wait_ge(steps.sem, steps.done(1))
            dve.tensor_tensor(root, root, out, ALU.mult).then_inc(steps.sem, 1)
            dve.wait_ge(steps.sem, steps.done(1))
            dve.tensor_tensor(root, root, out, ALU.mult).then_inc(steps.sem, 1)
            dve.wait_ge(steps.sem, steps.done(1))
            dve.tensor_scalar(root, root, -0.5, 1.5, ALU.mult, ALU.add).then_inc(steps.sem, 1)
            dve.wait_ge(steps.sem, steps.done(1))
            dve.tensor_tensor(out, out, root, ALU.mult).then_inc(steps.sem, 1)
            dve.wait_ge(steps.sem, steps.done(1))

        with dve.Fori(0, UNITS) as u:
            steps.enter(u, 2 + 6 + 2 + 6 + 2 * GROUPS)
            for s in two:
                n = 2 * u + s
                dve.wait_ge(a_made.sem, a_made.after(2 * n + 2))
                dve.tensor_copy(at[:, 32:64, :], pA[1][:, :, :]).then_inc(a_dve.sem, 1)
                dve.wait_ge(o_made.sem, o_made.after(2 * n + 2))
                if s == 0:
                    dve.wait_ge(w_made.sem, w_made.after(4 * u))
                dve.tensor_copy(ob_at(s, 1), pO[1][:, :, :]).then_inc(o_dve.sem, 1)
            for r in (2, 3):
                dve.wait_ge(w_made.sem, w_made.after(4 * u + r + 1))
                ins = dve.tensor_copy(heads_of(u, r), pW[r][:, :, :].rearrange("p g (j d) -> p g j d", d=HD))
                ins.then_inc(w_dve.sem, 1)
            dve.wait_ge(w_act.sem, w_act.after(2 * (u + 1)))
            dve.wait_ge(w_dve.sem, w_dve.after(2 * (u + 1)))
            rows = unit_rows(u)
            per_head = rows.rearrange("p j (h d) -> p (j h) d", d=HD)
            dve.tensor_tensor(sqall[:, :].rearrange("p (j d) -> p j d", j=GROUPS), rows, rows, ALU.mult).then_inc(steps.sem, 1)
            dve.wait_ge(steps.sem, steps.done(1))
            dve.tensor_reduce(hs[:, :], sqall[:, :].rearrange("p (g d) -> p g d", d=HD), AX.X, ALU.add).then_inc(steps.sem, 1)
            dve.wait_ge(steps.sem, steps.done(1))
            dve.sem_inc(sq_ready.sem, 1)
            dve.wait_ge(root_ready.sem, root_ready.after(u + 1))
            inverse(hr[:, :], 1.0 / HD, hs[:, :], None, hy[:, :])
            dve.tensor_tensor(per_head, per_head, hy[:, :].rearrange("p (g a) -> p g a", a=1).broadcast_to([P, GROUPS * HEADS, HD]), ALU.mult).then_inc(steps.sem, 1)
            dve.wait_ge(steps.sem, steps.done(1))
            dve.tensor_tensor(per_head, per_head, g2[:, :].rearrange("p (a d) -> p a d", a=1).broadcast_to([P, GROUPS * HEADS, HD]), ALU.mult).then_inc(steps.sem, 1)
            dve.wait_ge(steps.sem, steps.done(1))
            dve.sem_inc(es_ready.sem, 1)
            dve.wait_ge(er_ready.sem, er_ready.after(u + 1))
            inverse(er[:, :], 1.0 / DIM, es[:, :], None, hy[:, 0:GROUPS])
            for j in range(GROUPS):
                row = att[:, bass.ds(u * GROUPS + j, 1), :].rearrange("p a d -> p (a d)")
                dve.tensor_scalar(mrow[j % 2][:, :], g3[:, :], hy[:, j:j + 1], 1.0, ALU.mult, ALU.add).then_inc(steps.sem, 1)
                dve.wait_ge(steps.sem, steps.done(1))
                dve.tensor_tensor(row, row, mrow[j % 2][:, :], ALU.mult).then_inc(steps.sem, 1)
                dve.wait_ge(steps.sem, steps.done(1))
            steps.leave(UNITS)


def attention_mlp(net, ctx):
    nc, a = net.nc, net.args
    ph = Phase(net, ctx, "m")
    two = range(2)
    xs = [ph.sb(f"xs{i}", [P, DIM]) for i in two]
    aT = [ph.sb(f"aT{i}", [P, KD, P]) for i in two]
    h = [ph.sb(f"h{i}", [P, DIM]) for i in two]
    hT = [ph.sb(f"hT{i}", [P, KD, P]) for i in two]
    y = [ph.sb(f"y{i}", [P, DIM]) for i in two]
    yst, ymv, yrs = ([ph.sb(f"{n}{i}", [P, w]) for i in two] for n, w in (("yst", 6), ("ymv", 2), ("yrs", 1)))
    pX, pH, pT, pY = ([ph.ps(f"{n}{i}", [P, KD, P] if i else [P, KD, P]) for i in two] for n in ("pX", "pH", "pT", "pY"))
    copied, turned, aT_ready, h_made, gelued, h_turned, hT_ready, y_made, ymv_ready, yrs_ready, step, pool_step, y_taken = (
        ph.sig(n, 0 if n in ("step", "pool_step") else 1) for n in ("copied", "turned", "aT_ready", "h_made", "gelued", "h_turned", "hT_ready", "y_made",
                            "ymv_ready", "yrs_ready", "step", "pool_step", "y_taken"))

    def att_tile(i):
        return net.att_res[:, bass.ds(i, 1), :].rearrange("p a d -> p (a d)")

    nc.all_engine_barrier()
    block = ctx.enter_context(nc.Block())

    def later(i, n):
        return not isinstance(i, int) or i >= n

    @block.gpsimd
    def _(pool):
        steps = Steps(pool_step.sem)

        def front(i, p):
            if later(i, 2):
                pool.wait_ge(turned.sem, turned.after(i - 1))
            pool.tensor_copy(xs[p][:, :], att_tile(i)).then_inc(copied.sem, 1)

        def back(i, p):
            pool.wait_ge(ymv_ready.sem, ymv_ready.after(i + 1))
            rstd_of(pool, steps, yrs[p][:, :], ymv[p][:, 1:2], LN_EPS, net).then_inc(yrs_ready.sem, 1)

        staggered(pool, TILES, front, back, steps, 2)

    @block.tensor
    def _(pe):
        def front(i, p):
            pe.wait_ge(copied.sem, copied.after(i + 1))
            if later(i, 2):
                pe.wait_ge(aT_ready.sem, aT_ready.after(i - 1))
            for k in range(KD):
                mm = pe.transpose(pX[p][:, k, :], xs[p][:, k * P:(k + 1) * P], net.table["ident"])
            mm.then_inc(turned.sem, 1)
            pe.wait_ge(aT_ready.sem, aT_ready.after(i + 1))
            if later(i, 2):
                pe.wait_ge(gelued.sem, gelued.after(i - 1))
            for k in range(KD):
                mm = pe.matmul(pH[p][:, :, :].rearrange("p k n -> p (k n)"), aT[p][:, k, :], net.w1T[:, k, :],
                               start=(k == 0), stop=(k == KD - 1))
            mm.then_inc(h_made.sem, 1)

        def back(i, p):
            pe.wait_ge(gelued.sem, gelued.after(i + 1))
            if later(i, 2):
                pe.wait_ge(hT_ready.sem, hT_ready.after(i - 1))
            for k in range(KD):
                mm = pe.transpose(pT[p][:, k, :], h[p][:, k * P:(k + 1) * P], net.table["ident"])
            mm.then_inc(h_turned.sem, 1)
            pe.wait_ge(hT_ready.sem, hT_ready.after(i + 1))
            if later(i, 2):
                pe.wait_ge(y_taken.sem, y_taken.after(i - 1))
            for k in range(KD):
                mm = pe.matmul(pY[p][:, :, :].rearrange("p k n -> p (k n)"), hT[p][:, k, :], net.w2T[:, k, :],
                               start=(k == 0), stop=(k == KD - 1))
            mm.then_inc(y_made.sem, 1)

        staggered(pe, TILES, front, back)

    @block.scalar
    def _(act):
        def front(i, p):
            act.wait_ge(turned.sem, turned.after(i + 1))
            nc.scalar.activation(aT[p][:, :, :], pX[p][:, :, :], ACT.Copy).then_inc(aT_ready.sem, 1)
            act.wait_ge(h_made.sem, h_made.after(i + 1))
            nc.scalar.activation(h[p][:, :].rearrange("p (k n) -> p k n", k=KD), pH[p][:, :, :], ACT.Gelu).then_inc(gelued.sem, 1)

        def back(i, p):
            act.wait_ge(h_turned.sem, h_turned.after(i + 1))
            nc.scalar.activation(hT[p][:, :, :], pT[p][:, :, :], ACT.Copy).then_inc(hT_ready.sem, 1)

        staggered(act, TILES, front, back)

    @block.vector
    def _(dve):
        steps = Steps(step.sem)

        def add_rows(i, p):
            dve.wait_ge(y_made.sem, y_made.after(i + 1))
            dve.tensor_tensor(y[p][:, :], pY[p][:, :, :].rearrange("p k n -> p (k n)"), att_tile(i), ALU.add).then_inc(steps.sem, 1)
            dve.wait_ge(steps.sem, steps.done(1))
            dve.sem_inc(y_taken.sem, 1)
            dve.tensor_tensor(y[p][:, :], y[p][:, :], tile_of(net, i), ALU.add).then_inc(steps.sem, 1)
            dve.wait_ge(steps.sem, steps.done(1))
            dve.bn_stats(yst[p][:, :], y[p][:, :]).then_inc(steps.sem, 1)
            dve.wait_ge(steps.sem, steps.done(1))
            dve.sem_inc(net.passed, 1)
            dve.bn_aggr(ymv[p][:, :], yst[p][:, :]).then_inc(ymv_ready.sem, 1)

        def norm_rows(i, p):
            dve.wait_ge(yrs_ready.sem, yrs_ready.after(i + 1))
            dve.tensor_scalar(tile_of(net, i), y[p][:, :], ymv[p][:, 0:1], yrs[p][:, :], ALU.subtract, ALU.mult).then_inc(steps.sem, 1)
            dve.wait_ge(steps.sem, steps.done(1))

        staggered(dve, TILES, add_rows, norm_rows, steps, 8)


def route(net, ctx):
    nc, a = net.nc, net.args
    ph = Phase(net, ctx, "g")
    two = range(2)
    wr = ph.sb("wr", [P, KD, EXPERTS])
    xs = [ph.sb(f"xs{i}", [P, DIM]) for i in two]
    xT = [ph.sb(f"xT{i}", [P, KD, P]) for i in two]
    lg = ph.sb("lg", [P, TILES, EXPERTS])
    pr, s8, tmp = ph.sb("pr", [P, TILES, EXPERTS]), ph.sb("s8", [P, TILES, EXPERTS]), ph.sb("tmp", [P, TILES, EXPERTS])
    m1 = ph.sb("m1", [P, TILES])
    big = [P, MGROUPS, TOPK, TPG, EXPERTS]
    mask, pos, tot = ph.sb("mask", big), ph.sb("pos", big), ph.sb("tot", big)
    acc = [ph.sb(f"acc{i}", big) for i in two]
    posk, row, keep, idxf = (ph.sb(n, big[:-1]) for n in ("posk", "row", "keep", "idxf"))
    idx_out = ph.sb("idx_out", big[:-1], U32)
    zeros = ph.sb("zeros", [P, SLOTS // P * DIM])
    pX = [ph.ps(f"pX{i}", [P, KD, P]) for i in two]
    pL = [ph.ps(f"pL{i}", [P, EXPERTS]) for i in two]
    pP, pN = ph.ps("pP", [P, 512]), ph.ps("pN", [P, 512])
    w_in, copied, turned, xT_ready, l_made, l_taken, shifted, exped, mask_ready, counted, idx_ready, step, act_done, cleared = (
        ph.sig(n, 1 if n in ("turned", "xT_ready", "l_taken") else 0) for n in ("w_in", "copied", "turned", "xT_ready", "l_made", "l_taken", "shifted", "exped", "mask_ready",
                            "counted", "idx_ready", "step", "act_done", "cleared"))
    zero_ready, sent = ph.sig("zero_ready"), ph.sig("sent")

    def later(i, n):
        return not isinstance(i, int) or i >= n

    def flat(t):
        return t[:, :, :, :, :].rearrange("p g k t e -> p (g k t e)")

    nc.all_engine_barrier()
    block = ctx.enter_context(nc.Block())

    @block.sync
    def _(sp):
        sp.dma_start(wr[:, :, :], a["L1_ffn_w_router"].rearrange("(k p) n -> p k n", p=P)).then_inc(w_in.sem, 16)
        sp.wait_ge(zero_ready.sem, zero_ready.after(1))
        sp.dma_start(net.xe_dram.rearrange("(p r) d -> p (r d)", p=P), zeros[:, :]).then_inc(cleared.sem, 16)
        sp.dma_start(net.ye_dram[SLOTS:SLOTS + 1, :], zeros[0:1, 0:DIM]).then_inc(cleared.sem, 16)
        sp.wait_ge(cleared.sem, cleared.after(32))

    @block.gpsimd
    def _(pool):
        def front(i, p):
            if later(i, 2):
                pool.wait_ge(turned.sem, turned.after(i - 1))
            pool.tensor_copy(xs[p][:, :], tile_of(net, i)).then_inc(copied.sem, 1)

        staggered(pool, TILES, front, lambda i, p: None)
        pool.wait_ge(idx_ready.sem, idx_ready.after(1))
        pool.wait_ge(cleared.sem, cleared.after(32))
        for g in range(MGROUPS):
            for k in range(TOPK):
                for t in range(TPG):
                    pool.indirect_dma_start(net.xe_dram[:, :], bass.IndirectOffsetOnAxis(ap=idx_out[:, g, k, t:t + 1], axis=0),
                                            net.x_res[:, g * TPG + t, :], None, bounds_check=SLOTS - 1, oob_is_err=False)\
                        .then_inc(sent.sem, 16)
        pool.wait_ge(sent.sem, sent.after(16 * MGROUPS * TOPK * TPG))

    @block.tensor
    def _(pe):
        pe.wait_ge(w_in.sem, w_in.after(16))

        def front(i, p):
            pe.wait_ge(copied.sem, copied.after(i + 1))
            if later(i, 2):
                pe.wait_ge(xT_ready.sem, xT_ready.after(i - 1))
            for k in range(KD):
                mm = pe.transpose(pX[p][:, k, :], xs[p][:, k * P:(k + 1) * P], net.table["ident"])
            mm.then_inc(turned.sem, 1)

        def back(i, p):
            pe.wait_ge(xT_ready.sem, xT_ready.after(i + 1))
            if later(i, 2):
                pe.wait_ge(l_taken.sem, l_taken.after(i - 1))
            for k in range(KD):
                mm = pe.matmul(pL[p][:, :], xT[p][:, k, :], wr[:, k, :], start=(k == 0), stop=(k == KD - 1))
            mm.then_inc(l_made.sem, 1)

        staggered(pe, TILES, front, back)
        pe.wait_ge(mask_ready.sem, mask_ready.after(1))
        pe.matmul(pP[:, :], net.table["tri"], flat(mask), start=True, stop=True)
        pe.matmul(pN[:, :], net.table["ones"], flat(mask), start=True, stop=True).then_inc(counted.sem, 1)

    @block.scalar
    def _(act):
        def take(i, p):
            act.wait_ge(turned.sem, turned.after(i + 1))
            nc.scalar.activation(xT[p][:, :, :], pX[p][:, :, :], ACT.Copy).then_inc(xT_ready.sem, 1)

        staggered(act, TILES, lambda i, p: None, take)
        act.wait_ge(shifted.sem, shifted.after(1))
        nc.scalar.activation(pr[:, :, :], lg[:, :, :], ACT.Exp).then_inc(exped.sem, 1)

    @block.vector
    def _(dve):
        dve.memset(zeros[:, :], 0.0).then_inc(zero_ready.sem, 1)

        def take(i, p):
            dve.wait_ge(l_made.sem, l_made.after(i + 1))
            dve.tensor_copy(lg[:, bass.ds(i, 1), :].rearrange("p a e -> p (a e)"), pL[p][:, :]).then_inc(l_taken.sem, 1)

        staggered(dve, TILES, lambda i, p: None, take)
        steps = Steps(step.sem)
        dve.wait_ge(l_taken.sem, l_taken.after(TILES))

        def each(x):
            return x[:, :].rearrange("p (t a) -> p t a", a=1).broadcast_to([P, TILES, EXPERTS])

        dve.tensor_reduce(m1[:, :], lg[:, :, :], AX.X, ALU.max).then_inc(steps.sem, 1)
        dve.wait_ge(steps.sem, steps.done(1))
        dve.tensor_tensor(lg[:, :, :], lg[:, :, :], each(m1), ALU.subtract).then_inc(shifted.sem, 1)
        dve.wait_ge(exped.sem, exped.after(1))
        dve.tensor_reduce(m1[:, :], pr[:, :, :], AX.X, ALU.add).then_inc(steps.sem, 1)
        dve.wait_ge(steps.sem, steps.done(1))
        dve.reciprocal(m1[:, :], m1[:, :]).then_inc(steps.sem, 1)
        dve.wait_ge(steps.sem, steps.done(1))
        dve.tensor_tensor(pr[:, :, :], pr[:, :, :], each(m1), ALU.mult).then_inc(steps.sem, 1)
        dve.wait_ge(steps.sem, steps.done(1))
        first = net.table["first"].rearrange("p (a e) -> p a e", a=1).broadcast_to([P, TILES, EXPERTS])
        mview = mask[:, :, :, :, :]
        for k in range(TOPK):
            gate = net.gates[:, k, :]
            dve.tensor_reduce(gate, pr[:, :, :], AX.X, ALU.max).then_inc(steps.sem, 1)
            dve.wait_ge(steps.sem, steps.done(1))
            dve.tensor_tensor(s8[:, :, :], pr[:, :, :], gate.rearrange("p (t a) -> p t a", a=1).broadcast_to([P, TILES, EXPERTS]), ALU.is_equal).then_inc(steps.sem, 1)
            dve.wait_ge(steps.sem, steps.done(1))
            dve.tensor_tensor(s8[:, :, :], s8[:, :, :], first, ALU.mult).then_inc(steps.sem, 1)
            dve.wait_ge(steps.sem, steps.done(1))
            dve.tensor_reduce(m1[:, :], s8[:, :, :], AX.X, ALU.max).then_inc(steps.sem, 1)
            dve.wait_ge(steps.sem, steps.done(1))
            dve.tensor_tensor(tmp[:, :, :], s8[:, :, :], each(m1), ALU.is_equal).then_inc(steps.sem, 1)
            dve.wait_ge(steps.sem, steps.done(1))
            dve.tensor_copy(mview[:, :, k, :, :], tmp[:, :, :].rearrange("p (g t) e -> p g t e", g=MGROUPS)).then_inc(steps.sem, 1)
            dve.wait_ge(steps.sem, steps.done(1))
            dve.scalar_tensor_tensor(out=pr[:, :, :], in0=tmp[:, :, :], scalar=-2.0, in1=pr[:, :, :], op0=ALU.mult, op1=ALU.add).then_inc(steps.sem, 1)
            dve.wait_ge(steps.sem, steps.done(1))
        dve.sem_inc(mask_ready.sem, 1)
        dve.wait_ge(counted.sem, counted.after(1))
        dve.tensor_copy(flat(tot), pN[:, :]).then_inc(steps.sem, 1)
        dve.wait_ge(steps.sem, steps.done(1))
        dve.tensor_copy(flat(acc[0]), flat(tot)).then_inc(steps.sem, 1)
        dve.wait_ge(steps.sem, steps.done(1))
        src, dist = 0, 1
        av = [t[:, :, :, :, :].rearrange("p g k t e -> p g (k t) e") for t in acc]
        while dist < TOPK * TPG:
            dve.tensor_copy(av[1 - src][:, :, 0:dist, :], av[src][:, :, 0:dist, :]).then_inc(steps.sem, 1)
            dve.wait_ge(steps.sem, steps.done(1))
            dve.tensor_tensor(av[1 - src][:, :, dist:, :], av[src][:, :, dist:, :], av[src][:, :, 0:TOPK * TPG - dist, :], ALU.add).then_inc(steps.sem, 1)
            dve.wait_ge(steps.sem, steps.done(1))
            src, dist = 1 - src, 2 * dist
        dve.tensor_tensor(flat(acc[src]), flat(acc[src]), flat(tot), ALU.subtract).then_inc(steps.sem, 1)
        dve.wait_ge(steps.sem, steps.done(1))
        dve.tensor_tensor(flat(pos), pP[:, :], flat(acc[src]), ALU.add).then_inc(steps.sem, 1)
        dve.wait_ge(steps.sem, steps.done(1))
        dve.tensor_tensor(flat(pos), flat(pos), flat(mask), ALU.mult).then_inc(steps.sem, 1)
        dve.wait_ge(steps.sem, steps.done(1))

        def f4(t):
            return t[:, :, :, :].rearrange("p g k t -> p (g k t)")

        def f5(t):
            return t[:, :, :, :, :].rearrange("p g k t e -> p (g k t) e")

        dve.tensor_reduce(f4(posk), f5(pos), AX.X, ALU.add).then_inc(steps.sem, 1)
        dve.wait_ge(steps.sem, steps.done(1))
        base = net.table["base"].rearrange("p (a e) -> p a e", a=1).broadcast_to([P, MGROUPS * TOPK * TPG, EXPERTS])
        dve.tensor_tensor(f5(pos), f5(mask), base, ALU.mult).then_inc(steps.sem, 1)
        dve.wait_ge(steps.sem, steps.done(1))
        dve.tensor_reduce(f4(row), f5(pos), AX.X, ALU.add).then_inc(steps.sem, 1)
        dve.wait_ge(steps.sem, steps.done(1))
        for g in range(MGROUPS):
            r = row[:, g, :, :].rearrange("p k t -> p (k t)")
            dve.scalar_tensor_tensor(out=r, in0=r, scalar=float(g * CAP - 1), in1=posk[:, g, :, :].rearrange("p k t -> p (k t)"),
                               op0=ALU.add, op1=ALU.add).then_inc(steps.sem, 1)
            dve.wait_ge(steps.sem, steps.done(1))
        dve.tensor_scalar(f4(keep), f4(posk), float(CAP), None, ALU.is_le).then_inc(steps.sem, 1)
        dve.wait_ge(steps.sem, steps.done(1))
        dve.tensor_scalar(f4(idxf), f4(row), float(SLOTS), None, ALU.subtract).then_inc(steps.sem, 1)
        dve.wait_ge(steps.sem, steps.done(1))
        dve.tensor_tensor(f4(idxf), f4(idxf), f4(keep), ALU.mult).then_inc(steps.sem, 1)
        dve.wait_ge(steps.sem, steps.done(1))
        dve.tensor_scalar(f4(idxf), f4(idxf), float(SLOTS), None, ALU.add).then_inc(steps.sem, 1)
        dve.wait_ge(steps.sem, steps.done(1))
        dve.tensor_copy(idx_out[:, :, :, :].rearrange("p g k t -> p (g k t)"), f4(idxf)).then_inc(steps.sem, 1)
        dve.wait_ge(steps.sem, steps.done(1))
        dve.tensor_copy(net.idx_back[:, :, :].rearrange("p (g t) k -> p g k t", g=MGROUPS), idxf[:, :, :, :]).then_inc(steps.sem, 1)
        dve.wait_ge(steps.sem, steps.done(1))
        dve.sem_inc(idx_ready.sem, 1)


def experts(net, ctx):
    nc, a = net.nc, net.args
    ph = Phase(net, ctx, "e")
    two = range(2)
    wi = [ph.sb(f"wi{i}", [P, KD, HID]) for i in two]
    wo = [ph.sb(f"wo{i}", [P, NH, DIM]) for i in two]
    xr = [ph.sb(f"xr{i}", [P, 3, DIM]) for i in two]
    xT = [ph.sb(f"xT{i}", [P, KD, ROWS]) for i in two]
    hT = [ph.sb(f"hT{i}", [P, NH, ROWS]) for i in two]
    yo = [ph.sb(f"yo{i}", [P, 3, DIM]) for i in two]
    pX = [ph.ps(f"pX{k}", [P, ROWS]) for k in range(KD)]
    pH = [ph.ps(f"pH{i}", [P, ROWS]) for i in range(4)]
    pD = [ph.ps(f"pD{i}", [P, DIM]) for i in two]
    w_in, x_in, stored = ([ph.sig(f"{n}{i}", h) for i in two] for n, h in (("w_in", 0), ("x_in", 0), ("stored", 48)))
    turned, xT_ready, h_made, h_act, h_dve, d_made, d_act, d_dve = (
        ph.sig(n, 1) for n in ("turned", "xT_ready", "h_made", "h_act", "h_dve", "d_made", "d_act", "d_dve"))

    def later(i, n):
        return not isinstance(i, int) or i >= n

    nc.all_engine_barrier()
    block = ctx.enter_context(nc.Block())

    @block.sync
    def _(sp):

        def front(e, p):
            if later(e, 2):
                sp.wait_ge(d_made.sem, d_made.after(3 * (e - 1)))
            for r, (r0, n) in enumerate(RTILES):
                sp.dma_start(xr[p][0:n, r, :], net.xe_dram[bass.ds(e * ROWS + r0, n), :]).then_inc(x_in[p].sem, 16)
            sp.dma_start(wi[p][:, :, :], a["L1_ffn_wi"][bass.ds(e, 1), :, :].rearrange("a (k p) n -> p (a k) n", p=P)).then_inc(w_in[p].sem, 16)
            sp.dma_start(wo[p][:, :, :], a["L1_ffn_wo"][bass.ds(e, 1), :, :].rearrange("a (k p) n -> p (a k) n", p=P)).then_inc(w_in[p].sem, 16)

        def back(e, p):
            for r, (r0, n) in enumerate(RTILES):
                if r == 0:
                    sp.wait_ge(d_act.sem, d_act.after(2 * e + 1))
                elif r == 1:
                    sp.wait_ge(d_dve.sem, d_dve.after(e + 1))
                else:
                    sp.wait_ge(d_act.sem, d_act.after(2 * e + 2))
                sp.dma_start(net.ye_dram[bass.ds(e * ROWS + r0, n), :], yo[p][0:n, r, :]).then_inc(stored[p].sem, 16)

        staggered(sp, EXPERTS, front, back)
        for p in two:
            sp.wait_ge(stored[p].sem, stored[p].after(48 * EXPERTS // 2))

    @block.tensor
    def _(pe):
        def front(e, p):
            pe.wait_ge(x_in[p].sem, x_in[p].after(48 * (e // 2 + 1) if isinstance(e, int) else 24 * (e - p) + 48))
            if later(e, 1):
                pe.wait_ge(xT_ready.sem, xT_ready.after(e))
            for k in range(KD):
                for r, (r0, n) in enumerate(RTILES):
                    mm = pe.transpose(pX[k][:, r0:r0 + n], xr[p][0:n, r, k * P:(k + 1) * P], net.table["ident"][0:n, 0:n])
            mm.then_inc(turned.sem, 1)

        def back(e, p):
            pe.wait_ge(w_in[p].sem, w_in[p].after(32 * (e // 2 + 1) if isinstance(e, int) else 16 * (e - p) + 32))
            pe.wait_ge(xT_ready.sem, xT_ready.after(e + 1))
            for c in range(NH):
                if later(e, 1) or c >= 4:
                    pe.wait_ge((h_act, h_dve)[c % 2].sem, (h_act, h_dve)[c % 2].after(4 * e + c // 2 - 1))
                for k in range(KD):
                    mm = pe.matmul(pH[c % 4][:, :], wi[p][:, k, c * P:(c + 1) * P], xT[p][:, k, :], start=(k == 0), stop=(k == KD - 1))
                mm.then_inc(h_made.sem, 1)
            pe.wait_ge(h_act.sem, h_act.after(4 * e + 4))
            pe.wait_ge(h_dve.sem, h_dve.after(4 * e + 4))
            for r, (r0, n) in enumerate(RTILES):
                if r == 2:
                    pe.wait_ge(d_act.sem, d_act.after(2 * e + 1))
                elif later(e, 1):
                    pe.wait_ge((d_act if r == 0 else d_dve).sem, (d_act if r == 0 else d_dve).after(2 * e if r == 0 else e))
                for c in range(NH):
                    mm = pe.matmul(pD[r % 2][0:n, :], hT[p][:, c, r0:r0 + n], wo[p][:, c, :], start=(c == 0), stop=(c == NH - 1))
                mm.then_inc(d_made.sem, 1)

        staggered(pe, EXPERTS, front, back)

    @block.scalar
    def _(act):
        def back(e, p):
            for c in range(0, NH, 2):
                act.wait_ge(h_made.sem, h_made.after(NH * e + c + 1))
                nc.scalar.activation(hT[p][:, c, :], pH[c % 4][:, :], ACT.Relu).then_inc(h_act.sem, 1)
            act.wait_ge(stored[p].sem, stored[p].after(48 * (e // 2) if isinstance(e, int) else 24 * (e - p)))
            for r in (0, 2):
                n = RTILES[r][1]
                act.wait_ge(d_made.sem, d_made.after(3 * e + r + 1))
                nc.scalar.activation(yo[p][0:n, r, :], pD[0][0:n, :], ACT.Copy).then_inc(d_act.sem, 1)

        staggered(act, EXPERTS, lambda e, p: None, back)

    @block.vector
    def _(dve):
        def front(e, p):
            dve.wait_ge(turned.sem, turned.after(e + 1))
            for k in range(KD):
                ins = dve.tensor_copy(xT[p][:, k, :], pX[k][:, :])
            ins.then_inc(xT_ready.sem, 1)

        def back(e, p):
            for c in range(1, NH, 2):
                dve.wait_ge(h_made.sem, h_made.after(NH * e + c + 1))
                dve.tensor_scalar(hT[p][:, c, :], pH[c % 4][:, :], 0.0, None, ALU.max).then_inc(h_dve.sem, 1)
            dve.wait_ge(stored[p].sem, stored[p].after(48 * (e // 2) if isinstance(e, int) else 24 * (e - p)))
            dve.wait_ge(d_made.sem, d_made.after(3 * e + 2))
            dve.tensor_copy(yo[p][:, 1, :], pD[1][:, :]).then_inc(d_dve.sem, 1)

        staggered(dve, EXPERTS, front, back)


def combine(net, ctx):
    nc = net.nc
    ph = Phase(net, ctx, "c")
    NB = 4
    idx = [ph.sb(f"idx{i}", [P, TOPK], U32) for i in range(NB)]
    ya = [[ph.sb(f"ya{k}{i}", [P, DIM]) for k in range(TOPK)] for i in range(NB)]
    y, yo = ([ph.sb(f"{n}{i}", [P, DIM]) for i in range(NB)] for n in ("y", "yo"))
    yst, ymv, yrs = ([ph.sb(f"{n}{i}", [P, w]) for i in range(NB)] for n, w in (("yst", 6), ("ymv", 2), ("yrs", 1)))
    gathered = [ph.sig(f"gathered{i}") for i in range(NB)]
    stored = [ph.sig(f"stored{i}", 16) for i in range(NB)]
    ya_used, ymv_ready, yrs_ready, normed, step, pool_step, ones_ready = (
        ph.sig(n, h) for n, h in (("ya_used", NB), ("ymv_ready", 0), ("yrs_ready", 0), ("normed", NB), ("step", 0),
                                  ("pool_step", 0), ("ones_ready", 0)))
    out_rows = net.out.rearrange("b (t p) d -> (b t) p d", p=P)

    nc.all_engine_barrier()
    block = ctx.enter_context(nc.Block())

    @block.gpsimd
    def _(pool):
        steps = Steps(pool_step.sem)
        with pool.Fori(0, TILES // NB) as b:
            steps.enter(b, NB * 2)
            for t in range(NB):
                i = b * NB + t
                pool.wait_ge(ya_used.sem, ya_used.after(i + 1 - NB))
                cols = net.idx_back[:, bass.ds(i, 1), :].rearrange("p a k -> p (a k)")
                pool.tensor_copy(idx[t][:, :], cols).then_inc(steps.sem, 1)
                pool.wait_ge(steps.sem, steps.done(1))
                pool.sem_inc(net.passed_pool, 1)
                for k in range(TOPK):
                    pool.indirect_dma_start(ya[t][k][:, :], None, net.ye_dram[:, :],
                                            bass.IndirectOffsetOnAxis(ap=idx[t][:, k:k + 1], axis=0),
                                            bounds_check=SLOTS, oob_is_err=False).then_inc(gathered[t].sem, 16)
            for t in range(NB):
                i = b * NB + t
                pool.wait_ge(ymv_ready.sem, ymv_ready.after(i + 1))
                rstd_of(pool, steps, yrs[t][:, :], ymv[t][:, 1:2], LN_EPS, net).then_inc(yrs_ready.sem, 1)
            steps.leave(TILES // NB)

    @block.vector
    def _(dve):
        steps = Steps(step.sem)
        with dve.Fori(0, TILES // NB) as b:
            steps.enter(b, 3 * NB)
            for t in range(NB):
                i = b * NB + t
                dve.wait_ge(gathered[t].sem, gathered[t].after(32 * (b + 1)))
                dve.wait_ge(normed.sem, normed.after(i + 1 - NB))
                src = tile_of(net, i)
                for k in range(TOPK):
                    gate = net.gates[:, k, bass.ds(i, 1)]
                    ins = dve.scalar_tensor_tensor(out=y[t][:, :], in0=ya[t][k][:, :], scalar=gate, in1=src, op0=ALU.mult, op1=ALU.add)
                    ins.then_inc(steps.sem, 1)
                    dve.wait_ge(steps.sem, steps.done(1))
                    src = y[t][:, :]
                dve.sem_inc(ya_used.sem, 1)
                dve.bn_stats(yst[t][:, :], y[t][:, :]).then_inc(steps.sem, 1)
                dve.wait_ge(steps.sem, steps.done(1))
                dve.sem_inc(net.passed, 1)
                dve.bn_aggr(ymv[t][:, :], yst[t][:, :]).then_inc(ymv_ready.sem, 1)
            for t in range(NB):
                i = b * NB + t
                dve.wait_ge(yrs_ready.sem, yrs_ready.after(i + 1))
                dve.wait_ge(stored[t].sem, stored[t].after(16 * b))
                dve.tensor_scalar(yo[t][:, :], y[t][:, :], ymv[t][:, 0:1], yrs[t][:, :], ALU.subtract, ALU.mult)\
                    .then_inc(normed.sem, 1)
            steps.leave(TILES // NB)

    @block.sync
    def _(sp):
        with sp.Fori(0, TILES // NB) as b:
            for t in range(NB):
                i = b * NB + t
                sp.wait_ge(normed.sem, normed.after(i + 1))
                sp.dma_start(out_rows[bass.ds(i, 1), :, :].rearrange("a p d -> (a p) d"), yo[t][:, :]).then_inc(stored[t].sem, 16)
        for s in stored:
            sp.wait_ge(s.sem, s.after(16 * TILES // NB))


PHASES = [prepare, retention, ternary_ffn, attention_inputs, per_token_attention, attention_mlp, route, experts, combine]
FINAL = True


def program(nc, args, out, phases=len(PHASES), shown=False):
    with ExitStack() as whole:
        net = Net(nc, whole, args)
        net.out = out
        for phase in PHASES[:phases]:
            net.signals = []
            with ExitStack() as ctx:
                phase(net, ctx)
            for sem in net.signals:
                nc.sync.sem_clear(sem)
        if shown:
            with ExitStack() as ctx:
                done = ctx.enter_context(nc.semaphore("shown"))
                block = ctx.enter_context(nc.Block())
                src = net.att_res if shown == "att" else net.x_res

                @block.sync
                def _(sp):
                    sp.dma_start(out.rearrange("b (t p) d -> p (b t) d", p=P), src[:, :, :]).then_inc(done, 16)
                    sp.wait_ge(done, 16)


NAMES = ["L0_attn_x", "L0_attn_past_kv", "L0_attn_W_qkv", "L0_attn_gn_weight", "L0_attn_gn_bias", "L0_ffn_W_fc",
         "L0_ffn_ln_w", "L0_ffn_ln_b", "L0_ffn_W_proj", "L1_attn_Wq", "L1_attn_Wk", "L1_attn_Wv",
         "L1_attn_lambda_params", "L1_attn_g1", "L1_attn_g2", "L1_attn_g3", "L1_attn_W1", "L1_attn_W2",
         "L1_ffn_w_router", "L1_ffn_wi", "L1_ffn_wo"]


def kernel(**inputs):
    import concourse.bacc as bacc
    from concourse.bass_utils import run_bass_kernel_spmd

    nc = bacc.Bacc("TRN2", target_bir_lowering=False, num_devices=1)
    arrays = {name: np.ascontiguousarray(inputs[name]) for name in NAMES}
    arrays["consts"] = CONSTS
    args = {n: nc.dram_tensor(n, a.shape, mybir.dt.from_np(a.dtype), kind="ExternalInput").ap() for n, a in arrays.items()}
    out = nc.dram_tensor("out", (BATCH, SEQ, DIM), F32, kind="ExternalOutput").ap()
    program(nc, args, out)
    return run_bass_kernel_spmd(nc, [arrays], core_ids=[0]).results[0]["out"]
```

```python
from contextlib import ExitStack

import numpy as np
import concourse.bass as bass
from concourse import mybir

F32 = mybir.dt.float32
F32R = mybir.dt.float32r
BF16 = mybir.dt.bfloat16
I32 = mybir.dt.int32
U32 = mybir.dt.uint32
ALU = mybir.AluOpType
ACT = mybir.ActivationFunctionType
AX = mybir.AxisListType

P = 128
BATCH, SEQ, DIM = 8, 512, 256
TOKENS = BATCH * SEQ
TILES = TOKENS // P
TPB = SEQ // P
KD = DIM // P
HEADS, HD = 16, 16
HPK = P // HD
HID = 1024
NH = HID // P
LN_EPS = 1e-5
ABS_EPS = 1e-6
RMS_EPS = float(np.finfo(np.float32).eps)
LAMBDA_INIT = 0.8 - 0.6 * float(np.exp(-0.3 * 0))
RET_SCALE = 1.0 / float(np.sqrt(DIM // 2))
UNIT = 8 * P
UNITS = TOKENS // UNIT
GROUPS = UNIT // P
HALF = 64
PARTS = 3
TERMS = [(0, 0), (0, 1), (1, 0), (1, 1), (0, 2), (2, 0)]
EXPERTS, CAP, TOPK, MGROUPS = 8, 160, 2, 2
TPG = TILES // MGROUPS
ROWS = MGROUPS * CAP
SLOTS = EXPERTS * ROWS
RTILES = [(0, 128), (128, 128), (256, 64)]



def constant_table(names, of_them):
    gamma = 1.0 - 2.0 ** (-5.0 - np.arange(HEADS, dtype=np.float64))
    p = np.arange(P)
    parts = {}
    parts["ident"] = np.eye(P)
    parts["ones"] = np.ones((P, P))
    parts["tri"] = (p[:, None] <= p[None, :]).astype(np.float64)
    order = [half * HPK + 2 * r + par for r in range(4) for half in range(2) for par in range(2)]
    diff = p[None, :] - p[:, None]
    dec = np.where(diff[None] >= 0, gamma[order][:, None, None] ** np.maximum(diff, 0)[None], 0.0)
    parts["decay"] = dec.transpose(1, 0, 2).reshape(P, -1)
    hrow = np.arange(P) // HD
    qd = np.stack([gamma[half * HPK + hrow][:, None] ** (p[None, :] + 1) for half in range(2)], 1)
    parts["qdecay"] = qd.reshape(P, -1)
    parts["kdecay"] = gamma[np.arange(DIM) // HD][None, :] ** (P - 1 - p)[:, None]
    parts["tiledecay"] = np.stack([gamma[half * HPK + hrow] ** P for half in range(2)], 1)
    parts["block"] = (hrow[:, None] == hrow[None, :]).astype(np.float64)
    parts["even"] = (hrow % 2 == 0).astype(np.float64)[:, None]
    parts["odd"] = (hrow % 2 == 1).astype(np.float64)[:, None]
    parts["first"] = np.tile(EXPERTS - np.arange(EXPERTS), (P, 1))
    parts["base"] = np.tile(np.arange(EXPERTS) * ROWS, (P, 1))
    parts["firsthalf"] = (p % HD < HD // 2).astype(np.float64)[:, None]
    parts["rmseps"] = np.full((P, 1), RMS_EPS)
    parts["minushalf"] = np.full((P, HEADS), -0.5)
    parts = {name: a for name, a in parts.items() if (name in names) == of_them}
    at, where = 0, {}
    for name, a in parts.items():
        where[name] = (at, a.shape[1])
        at += a.shape[1]
    return np.concatenate([a for a in parts.values()], 1).astype(np.float32), where


LAYER0_CONSTS = ("block", "decay", "qdecay", "kdecay", "tiledecay", "even", "odd")
CONSTS, WHERE = constant_table(LAYER0_CONSTS, False)
CONSTS0, WHERE0 = constant_table(LAYER0_CONSTS, True)


class Signal:

    def __init__(self, net, ctx, name, head=0):
        self.sem = ctx.enter_context(net.nc.semaphore(name))
        self.head = head
        net.signals.append(self.sem)
        if head:
            net.nc.sync.sem_inc(self.sem, head)

    def after(self, count):
        return count + self.head


class Steps:

    def __init__(self, sem):
        self.sem, self.base, self.k = sem, 0, 0

    def done(self, more=0):
        self.k += more
        return self.base + self.k

    def enter(self, i, per):
        self.entry, self.per = self.base + self.k, per
        self.base, self.k = self.entry + i * per, 0

    def leave(self, times):
        assert self.k == self.per, (self.k, self.per)
        self.base, self.k = self.entry + times * self.per, 0


class Net:

    def __init__(self, nc, ctx, args):
        self.nc, self.args, self.ctx = nc, args, ctx
        self.sb = lambda name, shape, dt=F32: ctx.enter_context(nc.sbuf_tensor(name, shape, dt))
        self.passed = ctx.enter_context(nc.semaphore("passed"))
        self.passed_act = ctx.enter_context(nc.semaphore("passed_act"))
        self.passed_pool = ctx.enter_context(nc.semaphore("passed_pool"))
        self.x_res = self.sb("x_res", [P, TILES, DIM])
        self.w1T = self.sb("w1T", [P, KD, DIM])
        self.w2T = self.sb("w2T", [P, KD, DIM])
        self.qkv_dram = nc.dram_tensor("qkv_dram", [3, DIM, TILES, 2, PARTS, HALF], BF16).ap()
        self.xe_dram = nc.dram_tensor("xe_dram", [SLOTS, DIM], F32).ap()
        self.ye_dram = nc.dram_tensor("ye_dram", [SLOTS + 1, DIM], F32).ap()
        self.att_res = self.sb("att_res", [P, TILES, DIM])
        self.lg = self.sb("lg", [P, TILES, EXPERTS])
        self.gates = self.sb("gates", [P, TOPK, TILES])
        self.idx_back = self.sb("idx_back", [P, TILES, TOPK], U32)
        self.const = self.sb("const", [P, CONSTS.shape[1]])
        self.table = {}
        for name, (at, n) in WHERE.items():
            self.table[name] = self.const[:, at:at + n]
        self.projections = ExitStack()
        self.wqkvT = self.projections.enter_context(nc.sbuf_tensor("wqkvT", [P, KD, 3 * DIM], F32))
        self.layer0 = ExitStack()
        early = lambda name, shape, dt=F32: self.layer0.enter_context(nc.sbuf_tensor(name, shape, dt))
        self.const0 = early("const0", [P, CONSTS0.shape[1]])
        for name, (at, n) in WHERE0.items():
            self.table[name] = self.const0[:, at:at + n]
        self.wfcT = early("wfcT", [P, KD, HID], F32R)
        self.wpjH = early("wpjH", [P, NH, DIM + 2], F32R)
        self.wpjL = early("wpjL", [P, NH, DIM + 2], F32R)
        self.u0, self.u1 = early("u0", [P, DIM]), early("u1", [P, DIM])


def retention(net, ctx):
    nc, a = net.nc, net.args

    def sb(name, shape, dt=F32):
        return ctx.enter_context(nc.sbuf_tensor("r_" + name, shape, dt))

    def ps(name, shape):
        return ctx.enter_context(nc.psum_tensor("r_" + name, shape, F32))

    def sig(name, head=0):
        return Signal(net, ctx, "r_" + name, head)

    w = sb("w", [P, KD, 3 * DIM])
    pkv = sb("pkv", [P, KD, P])
    pkv_raw = sb("pkv_raw", [P, KD, HD])
    gnw, gnb = sb("gnw", [P, KD]), sb("gnb", [P, KD])
    rT, yT, square = sb("rT", [P, KD, SEQ]), sb("yT", [P, KD, SEQ]), sb("square", [P, P])
    xin = [sb(f"xin{i}", [P, DIM]) for i in range(4)]
    two = range(2)
    xT = [sb(f"xT{i}", [P, KD, P]) for i in two]
    qT = [sb(f"qT{i}", [P, KD, P]) for i in range(TPB)]
    qS = [sb(f"qS{i}", [P, KD, P]) for i in range(TPB)]
    qE = [sb(f"qE{i}", [P, KD, P]) for i in range(TPB)]
    qO = [sb(f"qO{i}", [P, KD, P]) for i in range(TPB)]
    kT = [sb(f"kT{i}", [P, KD, P]) for i in two]
    v = [sb(f"v{i}", [P, DIM]) for i in range(TPB)]
    vE, vO = ([sb(f"v{n}{i}", [P, DIM]) for i in range(TPB)] for n in "EO")
    ks = [sb(f"ks{i}", [P, DIM]) for i in two]
    prob = [sb(f"prob{i}", [P, 4, 4, P]) for i in two]
    state = [sb(f"state{i}", [P, KD, P]) for i in two]
    upd = sb("upd", [P, KD, P])
    gst = sb("gst", [P, 2, TPB, KD])
    gsum = sb("gsum", [P, 4])
    gaff = sb("gaff", [P, 3, KD])
    bst = sb("bst", [P, TPB, 6])
    mv = sb("mv", [P, TPB, 2])
    rstd = sb("rstd", [P, TPB])
    y1 = [sb(f"y1{i}", [P, DIM]) for i in range(TPB)]

    pXR = ps("pXR", [P, 512])
    pX, pR = pXR[:, 0:DIM], pXR[:, DIM:2 * DIM].rearrange("p (k t) -> p k t", k=KD)
    pQV = ps("pQV", [P, 512])
    pQ, pV = pQV[:, 0:DIM].rearrange("p (k t) -> p k t", k=KD), pQV[:, DIM:2 * DIM]
    pKK = ps("pKK", [P, 512])
    pKT, pK = pKK[:, 0:DIM].rearrange("p (k t) -> p k t", k=KD), pKK[:, DIM:2 * DIM]
    pUG = ps("pUG", [P, 512])
    pU, pG = pUG[:, 0:DIM], pUG[:, DIM:DIM + 2 * TPB * KD]
    pS = [ps(f"pS{i}", [P, 4, P]) for i in range(4)]
    pB = [pS[2 + i][:, 0:KD, :].rearrange("p k t -> p (k t)") for i in two]

    w_in = sig("w_in")
    x_in = [sig(f"x_in{i}") for i in range(4)]
    x_kept = sig("x_kept", 4)
    x_turned = sig("x_turned", 4)
    xT_ready = sig("xT_ready")
    kT_made = sig("kT_made")
    qv_made = sig("qv_made")
    q_copied = sig("q_copied")
    qv_taken = sig("qv_taken")
    qS_ready = sig("qS_ready")
    k_taken = sig("k_taken")
    k_turned = sig("k_turned")
    ks_ready = sig("ks_ready")
    s_made = sig("s_made")
    s_taken = sig("s_taken", 4)
    r_made = sig("r_made", 4)
    r_taken = sig("r_taken")
    upd_made = sig("upd_made")
    state_ready = sig("state_ready")
    g_made = sig("g_made")
    g_taken = sig("g_taken")
    pkv_ready = sig("pkv_ready")
    gn_in, cleared = sig("gn_in"), sig("cleared")
    yT_ready = sig("yT_ready")
    square_done = sig("square_done")
    back_made, back_taken = sig("back_made"), sig("back_taken", 4)
    affine = sig("affine")
    gvar_ready = sig("gvar_ready")
    grstd_ready = sig("grstd_ready")
    mv_ready = sig("mv_ready")
    rstd_ready = sig("rstd_ready")
    pool_step = sig("pool_step")
    dve_step = sig("dve_step")

    x_rows = a["L0_attn_x"].rearrange("b (t p) d -> (b t) p d", p=P)

    nc.all_engine_barrier()
    block = ctx.enter_context(nc.Block())

    @block.sync
    def _(sp):
        sp.dma_start(w[:, :, :], a["L0_attn_W_qkv"].rearrange("(k p) n -> p k n", p=P)).then_inc(w_in.sem, 16)
        sp.dma_start(pkv_raw[:, :, :], a["L0_attn_past_kv"].rearrange("(k h) d e -> (h d) k e", k=KD)).then_inc(w_in.sem, 16)
        for dst, src in ((gnw, "L0_attn_gn_weight"), (gnb, "L0_attn_gn_bias")):
            with nc.allow_non_contiguous_dma(reason="1 KB, once"):
                for h in range(HPK):
                    sp.dma_start(dst[h * HD:(h + 1) * HD, :], a[src].rearrange("(k h) -> h k", k=KD)[h:h + 1, :].broadcast_to([HD, KD]))\
                        .then_inc(gn_in.sem, 16)

        with sp.Fori(0, BATCH) as b:
            for t in range(TPB):
                sp.wait_ge(x_turned.sem, x_turned.after(b * TPB + (t + 1 - 4)))
                sp.wait_ge(x_kept.sem, x_kept.after(b * TPB + (t + 1 - 4)))
                sp.dma_start(xin[t][:, :], x_rows[bass.ds(b * TPB + t, 1), :, :].rearrange("a p d -> (a p) d"))\
                    .then_inc(x_in[t].sem, 16)

    @block.gpsimd
    def _(pool):

        def group_pow(b):
            pool.wait_ge(gvar_ready.sem, gvar_ready.after(b + 1))
            rstd_of(pool, steps, gsum[:, 3:4], gsum[:, 2:3], LN_EPS, net).then_inc(grstd_ready.sem, 1)

        def row_pow(b, t):
            i = b * TPB + t
            pool.wait_ge(mv_ready.sem, mv_ready.after(i + 1))
            rstd_of(pool, steps, rstd[:, t:t + 1], mv[:, t, 1:2], LN_EPS, net).then_inc(rstd_ready.sem, 1)

        def keep(b, t):
            pool.wait_ge(x_in[t].sem, x_in[t].after((b + 1) * 16))
            pool.tensor_copy(net.x_res[:, bass.ds(b * TPB + t, 1), :].rearrange("p a d -> p (a d)"), xin[t][:, :])\
                .then_inc(x_kept.sem, 1)

        def decay_queries(b, t):
            i = b * TPB + t
            pool.wait_ge(q_copied.sem, q_copied.after(i + 1))
            pool.wait_ge(r_made.sem, r_made.after(i + 1 - TPB))
            pool.tensor_tensor(qS[t][:, :, :], qT[t][:, :, :], net.table["qdecay"].rearrange("p (k t) -> p k t", k=KD),
                               ALU.mult).then_inc(qS_ready.sem, 1)

        steps = Steps(pool_step.sem)
        for i in range(TPB):
            pool.memset(vE[i][:, :], 0.0)
            ins = pool.memset(vO[i][:, :], 0.0)
        ins.then_inc(cleared.sem, 1)
        for t in range(TPB):
            keep(0, t)
            decay_queries(0, t)
        with pool.Fori(1, BATCH) as b:
            steps.enter(b - 1, 5)
            for t in range(TPB):
                keep(b, t)
                decay_queries(b, t)
                if t == 1:
                    group_pow(b - 1)
            for t in range(TPB):
                row_pow(b - 1, t)
            steps.leave(BATCH - 1)
        group_pow(BATCH - 1)
        for t in range(TPB):
            row_pow(BATCH - 1, t)

    @block.scalar
    def _(act):
        def turn(b, t):
            xT_free = b * TPB + t + 1
            act.wait_ge(x_turned.sem, x_turned.after(xT_free))
            nc.scalar.activation(xT[t % 2][:, :, :], pX.rearrange("p (k t) -> p k t", k=KD), ACT.Copy)\
                .then_inc(xT_ready.sem, 1)

        def take(b, t):
            i = b * TPB + t
            act.wait_ge(qv_made.sem, qv_made.after(i + 1))
            act.wait_ge(r_made.sem, r_made.after(i + 1 - TPB))
            nc.scalar.activation(qT[t][:, :, :], pQ, ACT.Copy).then_inc(q_copied.sem, 1)
            nc.scalar.activation(qE[t][:, :, :], pQ, ACT.Copy, scale=net.table["even"])
            nc.scalar.activation(qO[t][:, :, :], pQ, ACT.Copy, scale=net.table["odd"])
            heads = pV.rearrange("p (g two e) -> p g two e", two=2, e=HD)
            for odd, half in enumerate((vE, vO)):
                nc.scalar.activation(half[t][:, :].rearrange("p (g two e) -> p g two e", two=2, e=HD)[:, :, odd, :],
                                     heads[:, :, odd, :], ACT.Copy)
            nc.scalar.activation(v[t][:, :], pV, ACT.Copy).then_inc(qv_taken.sem, 1)

        def result(b, t):
            i = b * TPB + t
            act.wait_ge(r_made.sem, r_made.after(i + 1))
            if t == 0 and (not isinstance(b, int) or b):
                act.wait_ge(g_made.sem, g_made.after(b))
                act.wait_ge(yT_ready.sem, yT_ready.after(b))
            for k in range(KD):
                nc.scalar.activation(rT[:, k, t * P:(t + 1) * P], pR[:, k, :], ACT.Copy, accum_out=gst[:, 0, t, k:k + 1])
                if k or t or not isinstance(b, int) or b:
                    act.wait_ge(square_done.sem, square_done.after(KD * i + k))
                ins = nc.scalar.activation(square[:, :], pR[:, k, :], ACT.Square, accum_out=gst[:, 1, t, k:k + 1])
                ins.then_inc(square_done.sem, 1)
            act.wait_ge(square_done.sem, square_done.after(KD * (i + 1)))
            act.sem_inc(r_taken.sem, 1)

        def normed(b):
            act.wait_ge(affine.sem, affine.after(b + 1))
            if not isinstance(b, int) or b:
                act.wait_ge(back_made.sem, back_made.after(TPB * b))
            for k in range(KD):
                ins = nc.scalar.activation(yT[:, k, :], rT[:, k, :], ACT.Identity, bias=gaff[:, 1, k:k + 1], scale=gaff[:, 0, k:k + 1])
            ins.then_inc(yT_ready.sem, 1)

        def batch(b, before):
            turn(b, 0)
            turn(b, 1)
            take(b, 0)
            for t in range(TPB):
                if t + 1 < TPB:
                    take(b, t + 1)
                if t + 2 < TPB:
                    turn(b, t + 2)
                if t == 1 and before:
                    normed(b - 1)
                if t:
                    result(b, t - 1)
                elif before:
                    result(b - 1, TPB - 1)

        act.wait_ge(cleared.sem, cleared.after(1))
        batch(0, False)
        with act.Fori(1, BATCH) as b:
            batch(b, True)
        result(BATCH - 1, TPB - 1)
        normed(BATCH - 1)

    @block.tensor
    def _(pe):
        pe.wait_ge(w_in.sem, w_in.after(32))

        def turn(b, t):
            i = b * TPB + t
            pe.wait_ge(x_in[t].sem, x_in[t].after((b + 1) * 16))
            if t:
                pe.wait_ge(xT_ready.sem, xT_ready.after(i))
            if t == 3:
                pe.wait_ge(r_taken.sem, r_taken.after(i - 3))
            elif t == 0 and not isinstance(b, int):
                pe.wait_ge(r_taken.sem, r_taken.after(i - 1))
            for k in range(KD):
                mm = pe.transpose(pX[:, k * P:(k + 1) * P], xin[t][:, k * P:(k + 1) * P], net.table["ident"])
            mm.then_inc(x_turned.sem, 1)

        def project(b, t):
            i = b * TPB + t
            first = isinstance(b, int) and t == 0
            pe.wait_ge(xT_ready.sem, xT_ready.after(i + 1))
            if not first:
                pe.wait_ge(qv_taken.sem, qv_taken.after(i))
            for m in range(2):
                for k in range(KD):
                    pe.matmul(pQ[:, m, :], w[:, k, m * P:(m + 1) * P], xT[t % 2][:, k, :],
                              start=(k == 0), stop=(k == KD - 1))
            for k in range(KD):
                mm = pe.matmul(pV, xT[t % 2][:, k, :], w[:, k, 2 * DIM:], start=(k == 0), stop=(k == KD - 1))
            mm.then_inc(qv_made.sem, 1)
            if not first:
                pe.wait_ge(k_taken.sem, k_taken.after(i))
                pe.wait_ge(ks_ready.sem, ks_ready.after(i if t == 0 else i - 1)) if (t != 1 or not isinstance(b, int)) else None
            for m in range(2):
                for k in range(KD):
                    mm = pe.matmul(pKT[:, m, :], w[:, k, DIM + m * P:DIM + (m + 1) * P], xT[t % 2][:, k, :],
                                   start=(k == 0), stop=(k == KD - 1))
            mm.then_inc(kT_made.sem, 1)

        def scores_of(b, t, r, before):
            i = b * TPB + t
            if r == 0:
                pe.wait_ge(qv_taken.sem, qv_taken.after(i + 1))
                pe.wait_ge(k_taken.sem, k_taken.after(i + 1))
            pe.wait_ge(s_taken.sem, s_taken.after(4 * i + (r + 1 - 4)))
            if r >= 2 and before and t in (0, TPB - 1):
                pe.wait_ge(back_taken.sem, back_taken.after((b - 2) * TPB + r + 1 if t == 0 else (b - 1) * TPB + r - 1))
            rows = slice(32 * r, 32 * r + 32)
            for g in range(4):
                half, q = g // 2, (qE, qO)[g % 2][t]
                mm = pe.matmul(pS[r][:, g, :], kT[t % 2][rows, half, :], q[rows, half, :], start=True, stop=True)
            mm.then_inc(s_made.sem, 1)

        def turn_keys(b, t):
            i = b * TPB + t
            pe.wait_ge(k_taken.sem, k_taken.after(i + (2 if t < TPB - 1 else 1)))
            for k in range(KD):
                mm = pe.transpose(pK[:, k * P:(k + 1) * P], kT[t % 2][:, k, :], net.table["ident"])
            mm.then_inc(k_turned.sem, 1)

        def carry_in(b, t, turned):
            i = b * TPB + t
            pe.wait_ge(xT_ready.sem, xT_ready.after(turned))
            if t or not isinstance(b, int) or b:
                pe.wait_ge(r_taken.sem, r_taken.after(i))
            if t == 0:
                pe.wait_ge(pkv_ready.sem, pkv_ready.after(1))
            for half in range(KD):
                pe.matmul(pR[:, half, :], pkv[:, half, :], qT[t][:, half, :],
                          start=(half == 0), stop=False, skip_group_check=True)
            if t:
                pe.wait_ge(state_ready.sem, state_ready.after(b * (TPB - 1) + t))
                pe.wait_ge(qS_ready.sem, qS_ready.after(i + 1))
                for half in range(KD):
                    pe.matmul(pR[:, half, :], state[t % 2][:, half, :], qS[t][:, half, :],
                              start=False, stop=False, skip_group_check=True)

        def mix_of(b, t, r):
            i = b * TPB + t
            pe.wait_ge(s_taken.sem, s_taken.after(4 * i + r + 1))
            for g in range(4):
                half, rows = g // 2, slice(32 * r, 32 * r + 32)
                cols = slice(half * P + 32 * r, half * P + 32 * r + 32)
                mm = pe.matmul(pR[rows, half, :], (vE, vO)[g % 2][t][:, cols], prob[t % 2][:, r, g, :],
                               start=False, stop=(r == 3 and g == 3), skip_group_check=True)
            if r == 3:
                mm.then_inc(r_made.sem, 1)

        def update(b, t):
            i = b * TPB + t
            if t < TPB - 1:
                pe.wait_ge(ks_ready.sem, ks_ready.after(i + 1))
                if t == 0 and not isinstance(b, int):
                    pe.wait_ge(g_taken.sem, g_taken.after(b))
                for half in range(KD):
                    cols = slice(half * P, (half + 1) * P)
                    mm = pe.matmul(pU[:, cols], ks[t % 2][:, cols], v[t][:, cols], start=True, stop=True)
                mm.then_inc(upd_made.sem, 1)

        def totals(b):
            pe.wait_ge(r_taken.sem, r_taken.after((b + 1) * TPB))
            pe.wait_ge(state_ready.sem, state_ready.after((b + 1) * (TPB - 1)))
            pe.matmul(pG, net.table["ones"], gst[:, :, :, :].rearrange("p s t k -> p (s t k)"), start=True, stop=True)\
                .then_inc(g_made.sem, 1)

        def turn_back(b, t, scores_done):
            pe.wait_ge(yT_ready.sem, yT_ready.after(b + 1))
            pe.wait_ge(s_taken.sem, s_taken.after(scores_done))
            pe.wait_ge(back_taken.sem, back_taken.after(b * TPB + t - 1))
            for k in range(KD):
                mm = pe.transpose(pB[t % 2][:, k * P:(k + 1) * P], yT[:, k, t * P:(t + 1) * P], net.table["ident"])
            mm.then_inc(back_made.sem, 1)

        def batch(b, before):
            turn(b, 0)
            turn(b, 1)
            project(b, 0)
            for t in range(TPB):
                if t + 1 < TPB:
                    project(b, t + 1)
                if t + 2 < TPB:
                    turn(b, t + 2)
                if t == 1 and before:
                    totals(b - 1)
                last = (b, t - 1) if t else (b - 1, TPB - 1) if before else None
                if last:
                    carry_in(*last, b * TPB + min(t + 3, TPB))
                for r in range(4):
                    scores_of(b, t, r, before)
                    if last:
                        mix_of(*last, r)
                if t:
                    update(b, t - 1)
                turn_keys(b, t)
                if t >= 2 and before:
                    for j in (2 * t - 4, 2 * t - 3):
                        turn_back(b - 1, j, 4 * (b * TPB + t + 1))

        batch(0, False)
        with pe.Fori(1, BATCH) as b:
            batch(b, True)
        carry_in(BATCH - 1, TPB - 1, TILES)
        for r in range(4):
            mix_of(BATCH - 1, TPB - 1, r)
        totals(BATCH - 1)
        for t in range(TPB):
            turn_back(BATCH - 1, t, 4 * TILES)

    @block.vector
    def _(dve):
        steps = Steps(dve_step.sem)
        dve.wait_ge(w_in.sem, w_in.after(32))
        blk = net.table["block"].rearrange("p (h e) -> p h e", e=HD)
        for half in range(KD):
            ins = dve.scalar_tensor_tensor(out=pkv[:, half, :].rearrange("p (h e) -> p h e", e=HD),
                                           in0=pkv_raw[:, half:half + 1, :].broadcast_to([P, HPK, HD]),
                                           scalar=float(HEADS * HD), in1=blk, op0=ALU.mult, op1=ALU.mult)
        ins.then_inc(pkv_ready.sem, 1)

        def take(b, t):
            i = b * TPB + t
            dve.wait_ge(kT_made.sem, kT_made.after(i + 1))
            dve.tensor_copy(kT[t % 2][:, :, :], pKT).then_inc(k_taken.sem, 1)

        def decay(b, t):
            i = b * TPB + t
            dec = net.table["decay"].rearrange("p (r g t) -> p r g t", r=4, g=4)
            for r in range(4):
                dve.wait_ge(s_made.sem, s_made.after(4 * i + r + 1))
                if r == 0:
                    dve.wait_ge(r_made.sem, r_made.after(i + 1 - 2))
                dve.tensor_tensor(prob[t % 2][:, r, :, :], pS[r][:, :, :], dec[:, r, :, :], ALU.mult)\
                    .then_inc(s_taken.sem, 1)

        def keys(b, t):
            i = b * TPB + t
            dve.wait_ge(k_turned.sem, k_turned.after(i + 1))
            if t >= 2:
                dve.wait_ge(upd_made.sem, upd_made.after(b * (TPB - 1) + t - 1))
            elif not isinstance(b, int):
                dve.wait_ge(upd_made.sem, upd_made.after(b * (TPB - 1)))
            dve.tensor_tensor(ks[t % 2][:, :], pK, net.table["kdecay"], ALU.mult).then_inc(ks_ready.sem, 1)

        def carry(b, t):
            n = b * (TPB - 1) + t + 1
            dve.wait_ge(upd_made.sem, upd_made.after(n))
            new = state[(t + 1) % 2]
            pu = pU.rearrange("p (k n) -> p k n", k=KD)
            blk2 = net.table["block"].rearrange("p (a n) -> p a n", a=1).broadcast_to([P, KD, P])
            if t == 0:
                dve.tensor_tensor(new[:, :, :], pu, blk2, ALU.mult).then_inc(state_ready.sem, 1)
            else:
                dve.tensor_tensor(upd[:, :, :], pu, blk2, ALU.mult).then_inc(steps.sem, 1)
                dve.wait_ge(steps.sem, steps.done(1))
                dve.wait_ge(state_ready.sem, state_ready.after(n - 1))
                for half in range(KD):
                    ins = dve.scalar_tensor_tensor(out=new[:, half, :], in0=state[t % 2][:, half, :],
                                                   scalar=net.table["tiledecay"][:, half:half + 1], in1=upd[:, half, :],
                                                   op0=ALU.mult, op1=ALU.add)
                ins.then_inc(state_ready.sem, 1)

        mean, ex2, var, rs = (gsum[:, j:j + 1] for j in range(4))
        scale, shift, tmp = (gaff[:, j, :] for j in range(3))

        def group_var(b):
            dve.wait_ge(g_made.sem, g_made.after(b + 1))
            dve.tensor_reduce(gsum[:, 0:2], pG.rearrange("p (s n) -> p s n", s=2), AX.X, ALU.add).then_inc(steps.sem, 1)
            dve.wait_ge(steps.sem, steps.done(1))
            dve.sem_inc(g_taken.sem, 1)
            dve.tensor_scalar(gsum[:, 0:2], gsum[:, 0:2], 1.0 / (SEQ * DIM), None, ALU.mult).then_inc(steps.sem, 1)
            dve.wait_ge(steps.sem, steps.done(1))
            dve.tensor_tensor(var, mean, mean, ALU.mult).then_inc(steps.sem, 1)
            dve.wait_ge(steps.sem, steps.done(1))
            dve.tensor_tensor(var, ex2, var, ALU.subtract).then_inc(gvar_ready.sem, 1)

        def group_affine(b):
            dve.wait_ge(grstd_ready.sem, grstd_ready.after(b + 1))
            if not isinstance(b, int) or b:
                dve.wait_ge(yT_ready.sem, yT_ready.after(b))
            dve.wait_ge(gn_in.sem, gn_in.after(16 * 2 * HPK))
            dve.tensor_scalar(scale, gnw[:, :], rs, None, ALU.mult).then_inc(steps.sem, 1)
            dve.wait_ge(steps.sem, steps.done(1))
            dve.tensor_scalar(tmp, scale, mean, None, ALU.mult).then_inc(steps.sem, 1)
            dve.wait_ge(steps.sem, steps.done(1))
            dve.tensor_tensor(shift, gnb[:, :], tmp, ALU.subtract).then_inc(affine.sem, 1)

        def flat(i):
            return net.x_res[:, bass.ds(i, 1), :].rearrange("p a d -> p (a d)")

        def add_rows(b, t):
            i = b * TPB + t
            dve.wait_ge(back_made.sem, back_made.after(i + 1))
            dve.wait_ge(x_kept.sem, x_kept.after(i + 1))
            dve.tensor_tensor(y1[t][:, :], pB[t % 2], flat(i), ALU.add).then_inc(back_taken.sem, 1)
            dve.wait_ge(back_taken.sem, back_taken.after(i + 1))
            dve.bn_stats(bst[:, t, :], y1[t][:, :]).then_inc(steps.sem, 1)
            dve.wait_ge(steps.sem, steps.done(1))
            dve.sem_inc(net.passed, 1)
            dve.bn_aggr(mv[:, t, :], bst[:, t, :]).then_inc(mv_ready.sem, 1)

        def norm_rows(b, t):
            i = b * TPB + t
            dve.wait_ge(rstd_ready.sem, rstd_ready.after(i + 1))
            dve.tensor_scalar(flat(i), y1[t][:, :], mv[:, t, 0:1], rstd[:, t:t + 1], ALU.subtract, ALU.mult)

        def batch(b, before):
            take(b, 0)
            for t in range(TPB):
                if t + 1 < TPB:
                    take(b, t + 1)
                if t == 1 and before:
                    group_var(b - 1)
                decay(b, t)
                if t == 1 and before:
                    group_affine(b - 1)
                if t:
                    carry(b, t - 1)
                keys(b, t)
                if t >= 2 and before:
                    for j in (2 * t - 4, 2 * t - 3):
                        add_rows(b - 1, j)
                        if j:
                            norm_rows(b - 1, j - 1)
            if before:
                norm_rows(b - 1, TPB - 1)

        batch(0, False)
        with dve.Fori(1, BATCH) as b:
            steps.enter(b - 1, 2 + 3 + 2 + 4)
            batch(b, True)
            steps.leave(BATCH - 1)
        group_var(BATCH - 1)
        group_affine(BATCH - 1)
        for t in range(TPB):
            add_rows(BATCH - 1, t)
            if t:
                norm_rows(BATCH - 1, t - 1)
        norm_rows(BATCH - 1, TPB - 1)


def rstd_of(pool, steps, out, var, eps, net, scale=1.0):
    pool.sem_inc(net.passed_pool, 1)
    pool.tensor_scalar(out, var, scale, eps, ALU.mult, ALU.add).then_inc(steps.sem, 1)
    pool.wait_ge(steps.sem, steps.done(1))
    return pool.tensor_tensor(out, out, net.table["minushalf"][:, 0:out.shape[1]], ALU.pow)


def staggered(eng, count, front, back, steps=None, per=0):
    front(0, 0)
    with eng.Fori(0, count // 2 - 1) as i:
        if steps:
            steps.enter(i, per)
        for p in range(2):
            front(2 * i + p + 1, (p + 1) % 2)
            back(2 * i + p, p)
        if steps:
            steps.leave(count // 2 - 1)
    front(count - 1, 1)
    back(count - 2, 0)
    back(count - 1, 1)


def batches(eng, body, steps=None, per=0):
    body(0, 0, False, True)
    with eng.Fori(0, BATCH // 2 - 1) as i:
        if steps:
            steps.enter(i, 2 * per)
        for p in range(2):
            body(2 * i + 1 + p, 1 - p, True, True)
        if steps:
            steps.leave(BATCH // 2 - 1)
    body(BATCH - 1, 1, True, False)


def tile_of(net, i):
    return net.x_res[:, bass.ds(i, 1), :].rearrange("p a d -> p (a d)")


class Phase:

    def __init__(self, net, ctx, prefix):
        self.net, self.ctx, self.prefix = net, ctx, prefix

    def sb(self, name, shape, dt=F32):
        return self.ctx.enter_context(self.net.nc.sbuf_tensor(f"{self.prefix}_{name}", shape, dt))

    def ps(self, name, shape):
        return self.ctx.enter_context(self.net.nc.psum_tensor(f"{self.prefix}_{name}", shape, F32))

    def sig(self, name, head=0):
        return Signal(self.net, self.ctx, f"{self.prefix}_{name}", head)


def prepare(net, ctx):
    nc, a = net.nc, net.args
    ph = Phase(net, ctx, "w")
    raw_fc = ph.sb("raw_fc", [P, NH, DIM])
    raw_pj = ph.sb("raw_pj", [P, KD, HID])
    neg = ph.sb("neg", [P, 2, NH * DIM])
    sq = [ph.sb(f"sq{i}", [P, KD, DIM]) for i in range(5)]
    absum, thr = ph.sb("absum", [P, 2]), ph.sb("thr", [P, 2, 2])
    pT = [ph.ps(f"pT{i}", [P, 4, P]) for i in range(2)]
    pM = ph.ps("pM", [P, 2])
    pU = [ph.ps(f"pU{i}", [P, DIM]) for i in range(2)]
    tern, full = ph.sb("tern", [P, NH, DIM]), ph.sb("full", [P, NH, DIM + 2])
    lnw, lnb, b_cols = ph.sb("lnw", [P, NH]), ph.sb("lnb", [P, NH]), ph.sb("b_cols", [P, NH, P])
    ln_in, full_ready, u_made = (ph.sig(n) for n in ("ln_in", "full_ready", "u_made"))
    c_in, fc_in, pj_in, sq_in = (ph.sig(n) for n in ("c_in", "fc_in", "pj_in", "sq_in"))
    sums, total, quant, turned, taken, step = (ph.sig(n) for n in ("sums", "total", "quant", "turned", "taken", "step"))

    banks = []
    for k in range(KD):
        for c in range(0, NH, 4):
            banks.append(([(raw_fc, c + j, k) for j in range(4)], net.wfcT[:, k, c * P:(c + 4) * P]))
    for c in range(0, NH, 2):
        banks.append(([(raw_pj, m, c + j) for j in range(2) for m in range(KD)],
                      tern[:, c:c + 2, :].rearrange("p c n -> p (c n)")))
    for n in range(5):
        dst = net.wqkvT[:, :, n * DIM:(n + 1) * DIM] if n < 3 else (net.w1T, net.w2T)[n - 3][:, :, :]
        banks.append(([(sq[n], m, k) for k in range(KD) for m in range(KD)], dst))

    nc.all_engine_barrier()
    block = ctx.enter_context(nc.Block())

    @block.sync
    def _(sp):
        sp.dma_start(net.const[:, :], a["consts"]).then_inc(c_in.sem, 16)
        sp.dma_start(net.const0[:, :], a["consts0"]).then_inc(c_in.sem, 16)
        sp.dma_start(raw_fc[:, :, :], a["L0_ffn_W_fc"].rearrange("(c p) n -> p c n", p=P)).then_inc(fc_in.sem, 16)
        sp.dma_start(raw_pj[:, :, :], a["L0_ffn_W_proj"].rearrange("(c p) n -> p c n", p=P)).then_inc(pj_in.sem, 16)
        with nc.allow_non_contiguous_dma(reason="2 x 4 KB, once"):
            for t, name in ((lnw, "L0_ffn_ln_w"), (lnb, "L0_ffn_ln_b")):
                sp.dma_start(t[:, :], a[name].rearrange("(c p) -> p c", p=P)).then_inc(ln_in.sem, 16)
        for n, name in enumerate(("Wq", "Wk", "Wv", "W1", "W2")):
            sp.dma_start(sq[n][:, :, :], a["L1_attn_" + name].rearrange("(c p) n -> p c n", p=P)).then_inc(sq_in.sem, 16)

    @block.vector
    def _(dve):
        steps = Steps(step.sem)
        dve.wait_ge(fc_in.sem, fc_in.after(16))
        dve.tensor_reduce(absum[:, 0:1], raw_fc[:, :, :].rearrange("p c n -> p (c n)"), AX.X, ALU.add,
                          apply_absolute_value=True)
        dve.wait_ge(pj_in.sem, pj_in.after(16))
        dve.tensor_reduce(absum[:, 1:2], raw_pj[:, :, :].rearrange("p c n -> p (c n)"), AX.X, ALU.add,
                          apply_absolute_value=True).then_inc(sums.sem, 1)
        dve.wait_ge(total.sem, total.after(1))
        n = float(HID * DIM)
        dve.tensor_scalar(thr[:, 0, :], pM[:, :], 1.0 / n, ABS_EPS, ALU.mult, ALU.add).then_inc(steps.sem, 1)
        dve.wait_ge(steps.sem, steps.done(1))
        dve.tensor_scalar(thr[:, 0, :], thr[:, 0, :], 0.5, None, ALU.mult).then_inc(steps.sem, 1)
        dve.wait_ge(steps.sem, steps.done(1))
        dve.tensor_scalar(thr[:, 1, :], thr[:, 0, :], -1.0, None, ALU.mult).then_inc(steps.sem, 1)
        dve.wait_ge(steps.sem, steps.done(1))
        for j, raw in enumerate((raw_fc, raw_pj)):
            flat = raw[:, :, :].rearrange("p c n -> p (c n)")
            dve.tensor_scalar(neg[:, j, :], flat, thr[:, 1, j:j + 1], -1.0, ALU.is_lt, ALU.mult).then_inc(steps.sem, 1)
            dve.wait_ge(steps.sem, steps.done(1))
            dve.scalar_tensor_tensor(out=flat, in0=flat, scalar=thr[:, 0, j:j + 1], in1=neg[:, j, :],
                                     op0=ALU.is_gt, op1=ALU.add).then_inc(quant.sem, 1)
        for n, (_, dst) in enumerate(banks):
            dve.wait_ge(turned.sem, turned.after(n + 1))
            src = pT[n % 2][:, :, :]
            if len(dst.shape) == 3:
                src = src.rearrange("p (k m) n -> p k (m n)", k=KD)
            else:
                src = src.rearrange("p k n -> p (k n)")
            dve.tensor_copy(dst, src).then_inc(taken.sem, 1)
        dve.wait_ge(ln_in.sem, ln_in.after(32))
        dve.wait_ge(taken.sem, taken.after(len(banks)))
        dve.memset(full[:, :, DIM:DIM + 2], 1.0)
        for c in range(NH):
            dve.tensor_scalar(full[:, c, 0:DIM], tern[:, c, :], lnw[:, c:c + 1], None, ALU.mult)
            ins = dve.tensor_scalar(b_cols[:, c, :], net.table["ones"], lnb[:, c:c + 1], None, ALU.mult)
        ins.then_inc(full_ready.sem, 1)
        dve.wait_ge(full_ready.sem, full_ready.after(1))
        dve.tensor_copy(net.wpjH[:, :, :], full[:, :, :]).then_inc(steps.sem, 1)
        dve.wait_ge(steps.sem, steps.done(1))
        dve.tensor_tensor(net.wpjL[:, :, :], full[:, :, :], net.wpjH[:, :, :], ALU.subtract)
        dve.wait_ge(u_made.sem, u_made.after(1))
        dve.tensor_copy(net.u0[:, :], pU[0][:, :])
        dve.tensor_copy(net.u1[:, :], pU[1][:, :])

    @block.tensor
    def _(pe):
        pe.wait_ge(c_in.sem, c_in.after(32))
        pe.wait_ge(sums.sem, sums.after(1))
        pe.matmul(pM[:, :], net.table["ones"], absum[:, :], start=True, stop=True).then_inc(total.sem, 1)
        for n, (blocks, _) in enumerate(banks):
            if n >= 2:
                pe.wait_ge(taken.sem, taken.after(n - 1))
            if blocks[0][0] is raw_fc:
                pe.wait_ge(quant.sem, quant.after(1))
            elif blocks[0][0] is raw_pj:
                pe.wait_ge(quant.sem, quant.after(2))
            else:
                pe.wait_ge(sq_in.sem, sq_in.after(80))
            for j, (src, row, col) in enumerate(blocks):
                mm = pe.transpose(pT[n % 2][:, j, :], src[:, row, col * P:(col + 1) * P], net.table["ident"])
            mm.then_inc(turned.sem, 1)
        pe.wait_ge(full_ready.sem, full_ready.after(1))
        for c in range(NH):
            pe.matmul(pU[0][:, :], b_cols[:, c, :], tern[:, c, :], start=(c == 0), stop=(c == NH - 1))
            mm = pe.matmul(pU[1][:, :], net.table["ones"], full[:, c, 0:DIM], start=(c == 0), stop=(c == NH - 1))
        mm.then_inc(u_made.sem, 1)


def ternary_ffn(net, ctx):
    nc = net.nc
    ph = Phase(net, ctx, "f")
    two, four = range(2), range(4)
    xs = ph.sb("xs", [P, TPB, DIM])
    xh, xl = ([ph.sb(f"{n}{i}", [P, KD, SEQ], F32R) for i in two] for n in ("xh", "xl"))
    g = [ph.sb(f"g{i}", [P, SEQ]) for i in four]
    gh, gl = ([ph.sb(f"{n}{i}", [P, SEQ], F32R) for i in four] for n in ("gh", "gl"))
    g2 = [ph.sb(f"g2{i}", [P, SEQ]) for i in two]
    acc = [ph.sb(f"acc{i}", [P, SEQ]) for i in two]
    y, xb = ph.sb("y", [P, TPB, DIM]), ph.sb("xb", [P, TPB, DIM])
    negmean, meansq, var, rs = (ph.sb(n, [P, TPB]) for n in ("negmean", "meansq", "var", "rs"))
    yst, ymv, yrs = ph.sb("yst", [P, TPB, 6]), ph.sb("ymv", [P, TPB, 2]), ph.sb("yrs", [P, TPB])
    pX = ph.ps("pX", [P, SEQ])
    pH = [ph.ps(f"pH{i}", [P, SEQ]) for i in two]
    pY = ph.ps("pY", [P, TPB, 512])
    pS = ph.ps("pS", [P, TPB])
    x_copied, turned, xh_ready, xl_ready = (ph.sig(n) for n in ("x_copied", "turned", "xh_ready", "xl_ready"))
    up_made, squared, s_made = ph.sig("up_made"), ph.sig("squared"), ph.sig("s_made", 2)
    gelued, split, down_made, added = ph.sig("gelued", 2), ph.sig("split", 4), ph.sig("down_made", 4), ph.sig("added", 2)
    y_taken, var_ready, rs_ready, xb_ready = ph.sig("y_taken", TPB), ph.sig("var_ready"), ph.sig("rs_ready"), ph.sig("xb_ready")
    rows_ready, yrs_ready, step, pool_step = ph.sig("rows_ready", 1), ph.sig("yrs_ready"), ph.sig("step"), ph.sig("pool_step")

    nc.all_engine_barrier()
    block = ctx.enter_context(nc.Block())

    @block.gpsimd
    def _(pool):
        steps = Steps(pool_step.sem)

        def base(b):

            pool.wait_ge(rows_ready.sem, rows_ready.after(b))
            pool.sem_inc(net.passed_pool, 1)
            pool.tensor_tensor(xb[:, :, :], net.x_res[:, bass.ds(b * TPB, TPB), :],
                               net.u0[:, :].rearrange("p (a d) -> p a d", a=1).broadcast_to([P, TPB, DIM]), ALU.add)\
                .then_inc(xb_ready.sem, 1)

        def inner(b):
            pool.wait_ge(var_ready.sem, var_ready.after(b + 1))
            rstd_of(pool, steps, rs[:, :], var[:, :], LN_EPS, net).then_inc(rs_ready.sem, 1)

        def outer(b):
            pool.wait_ge(rows_ready.sem, rows_ready.after(b + 1))
            rstd_of(pool, steps, yrs[:, :], ymv[:, :, 1], LN_EPS, net).then_inc(yrs_ready.sem, 1)

        def add(b, p, c):
            pool.wait_ge(squared.sem, squared.after(8 * b + c + 1))
            if c == 1:
                pool.wait_ge(s_made.sem, s_made.after(b + 1 - 2))
                pool.tensor_tensor(acc[p][:, :], g2[0][:, :], g2[1][:, :], ALU.add).then_inc(added.sem, 1)
            else:
                pool.wait_ge(added.sem, added.after((NH - 1) * b + c - 1))
                pool.tensor_tensor(acc[p][:, :], acc[p][:, :], g2[c % 2][:, :], ALU.add).then_inc(added.sem, 1)

        def body(b, p, before, behind):
            if before:
                base(b - 1)
            for c in range(1, NH):
                if c == 7 and before:
                    outer(b - 1)
                add(b, p, c)
                if c == 1 and before:
                    inner(b - 1)

        batches(pool, body, steps, 2)
        base(BATCH - 1)
        inner(BATCH - 1)
        outer(BATCH - 1)

    @block.scalar
    def _(act):

        def copy(b):
            for t in range(TPB):
                ins = nc.scalar.activation(xs[:, t, :], tile_of(net, b * TPB + t), ACT.Copy)
            ins.then_inc(x_copied.sem, 1)

        def take(b, p, k):
            act.wait_ge(turned.sem, turned.after(2 * b + k + 1))
            nc.scalar.activation(xh[p][:, k, :], pX[:, :], ACT.Copy).then_inc(xh_ready.sem, 1)

        def gelu(b, c):
            n = NH * b + c
            act.wait_ge(up_made.sem, up_made.after(n + 1))
            act.wait_ge(split.sem, split.after(n + 1 - 4))
            nc.scalar.activation(g[c % 4][:, :], pH[c % 2][:, :], ACT.Gelu).then_inc(gelued.sem, 1)

        def square(b, c):
            n = NH * b + c
            act.wait_ge(gelued.sem, gelued.after(n + 1))
            act.wait_ge(added.sem, added.after((NH - 1) * b + (c - 1 if c < 2 else max(c - 2, 1))))
            nc.scalar.activation(g2[c % 2][:, :], g[c % 4][:, :], ACT.Square).then_inc(squared.sem, 1)

        def body(b, p, before, behind):
            for c in range(NH):
                gelu(b, c)
                if c or before:
                    square(b if c else b - 1, (c - 1) % NH)
                if behind:
                    if c == 0:
                        act.sem_inc(net.passed_act, 1)
                        copy(b + 1)
                    if c in (4, 6):
                        take(b + 1, 1 - p, (c - 4) // 2)

        copy(0)
        for k in range(KD):
            take(0, 0, k)
        batches(act, body)
        square(BATCH - 1, NH - 1)

    @block.tensor
    def _(pe):

        def turn(b, p, k):
            pe.wait_ge(x_copied.sem, x_copied.after(b + 1))
            if not isinstance(b, int) or b or k:
                pe.wait_ge(xl_ready.sem, xl_ready.after(2 * b + k))
            for t in range(TPB):
                mm = pe.transpose(pX[:, t * P:(t + 1) * P], xs[:, t, k * P:(k + 1) * P], net.table["ident"])
            mm.then_inc(turned.sem, 1)

        def up(b, p, c):
            n = NH * b + c
            if c == 0:
                pe.wait_ge(xl_ready.sem, xl_ready.after(2 * b + 2))
            pe.wait_ge(gelued.sem, gelued.after(n + 1 - 2))
            for k in range(KD):
                for part in (xh, xl):
                    mm = pe.matmul(pH[c % 2][:, :], net.wfcT[:, k, c * P:(c + 1) * P], part[p][:, k, :],
                                   start=(k == 0 and part is xh), stop=(k == KD - 1 and part is xl))
            mm.then_inc(up_made.sem, 1)

        def down(b, c):
            n = NH * b + c
            pe.wait_ge(split.sem, split.after(n + 1))
            for t in range(TPB):
                if c == 0:
                    pe.wait_ge(y_taken.sem, y_taken.after(TPB * b + t + 1 - TPB))
                out, cols = pY[:, t, 0:DIM + 2], slice(t * P, (t + 1) * P)
                pe.matmul(out, gh[c % 4][:, cols], net.wpjH[:, c, :], start=(c == 0), stop=False)
                pe.matmul(out, gh[c % 4][:, cols], net.wpjL[:, c, :], start=False, stop=False)
                mm = pe.matmul(out, gl[c % 4][:, cols], net.wpjH[:, c, :], start=False, stop=(c == NH - 1))
            mm.then_inc(down_made.sem, 1)

        def sums(b, p):
            pe.wait_ge(added.sem, added.after((NH - 1) * (b + 1)))
            if not isinstance(b, int) or b:
                pe.wait_ge(var_ready.sem, var_ready.after(b))
            for t in range(TPB):
                mm = pe.matmul(pS[:, t:t + 1], acc[p][:, t * P:(t + 1) * P], net.table["ones"][:, 0:1], start=True, stop=True)
            mm.then_inc(s_made.sem, 1)

        def body(b, p, before, behind):
            for c in range(NH):
                up(b, p, c)
                if c >= 2:
                    down(b, c - 2)
                elif before:
                    down(b - 1, c + NH - 2)
                    if c == 1:
                        sums(b - 1, 1 - p)
                if behind and c in (3, 5):
                    turn(b + 1, 1 - p, (c - 3) // 2)

        for k in range(KD):
            turn(0, 0, k)
        batches(pe, body)
        down(BATCH - 1, NH - 2)
        down(BATCH - 1, NH - 1)
        sums(BATCH - 1, 1)

    @block.vector
    def _(dve):
        steps = Steps(step.sem)

        def low(b, p, k):
            dve.wait_ge(xh_ready.sem, xh_ready.after(2 * b + k + 1))
            dve.tensor_tensor(xl[p][:, k, :], pX[:, :], xh[p][:, k, :], ALU.subtract).then_inc(xl_ready.sem, 1)

        def divide(b, c):
            n = NH * b + c
            dve.wait_ge(gelued.sem, gelued.after(n + 1))
            dve.wait_ge(down_made.sem, down_made.after(n + 1 - 4))
            dve.tensor_copy(gh[c % 4][:, :], g[c % 4][:, :]).then_inc(steps.sem, 1)
            dve.wait_ge(steps.sem, steps.done(1))
            dve.tensor_tensor(gl[c % 4][:, :], g[c % 4][:, :], gh[c % 4][:, :], ALU.subtract).then_inc(split.sem, 1)

        def take(b):
            dve.wait_ge(down_made.sem, down_made.after(NH * (b + 1)))
            dve.tensor_scalar(negmean[:, :], pY[:, :, DIM], -1.0 / HID, None, ALU.mult).then_inc(steps.sem, 1)
            dve.wait_ge(steps.sem, steps.done(1))
            if not isinstance(b, int) or b:
                dve.wait_ge(rs_ready.sem, rs_ready.after(b))
            for t in range(TPB):
                dve.scalar_tensor_tensor(out=y[:, t, :], in0=net.u1[:, :], scalar=negmean[:, t:t + 1], in1=pY[:, t, 0:DIM],
                                         op0=ALU.mult, op1=ALU.add).then_inc(y_taken.sem, 1)
            dve.tensor_tensor(meansq[:, :], negmean[:, :], negmean[:, :], ALU.mult).then_inc(steps.sem, 1)
            dve.wait_ge(steps.sem, steps.done(1))
            dve.wait_ge(s_made.sem, s_made.after(b + 1))
            dve.scalar_tensor_tensor(out=var[:, :], in0=pS[:, :], scalar=1.0 / HID, in1=meansq[:, :],
                                     op0=ALU.mult, op1=ALU.subtract).then_inc(var_ready.sem, 1)

        def rows(b, t):
            if t == 0:
                dve.wait_ge(rs_ready.sem, rs_ready.after(b + 1))
                dve.wait_ge(xb_ready.sem, xb_ready.after(b + 1))
            dve.scalar_tensor_tensor(out=y[:, t, :], in0=y[:, t, :], scalar=rs[:, t:t + 1], in1=xb[:, t, :],
                                     op0=ALU.mult, op1=ALU.add).then_inc(steps.sem, 1)
            dve.wait_ge(steps.sem, steps.done(1))
            dve.bn_stats(yst[:, t, :], y[:, t, :]).then_inc(steps.sem, 1)
            dve.wait_ge(steps.sem, steps.done(1))
            dve.sem_inc(net.passed, 1)
            ins = dve.bn_aggr(ymv[:, t, :], yst[:, t, :])
            if t == TPB - 1:
                ins.then_inc(rows_ready.sem, 1)

        def norm(b):
            dve.wait_ge(yrs_ready.sem, yrs_ready.after(b + 1))
            for t in range(TPB):
                dve.tensor_scalar(tile_of(net, b * TPB + t), y[:, t, :], ymv[:, t, 0:1], yrs[:, t:t + 1], ALU.subtract, ALU.mult)\
                    .then_inc(steps.sem, 1)
            dve.wait_ge(steps.sem, steps.done(TPB))

        def body(b, p, before, behind):
            for c in range(NH):
                divide(b, c)
                if before:
                    if c == 1:
                        take(b - 1)
                    if 3 <= c < 7:
                        rows(b - 1, c - 3)
                    if c == 7:
                        norm(b - 1)
                if behind and c in (4, 6):
                    low(b + 1, 1 - p, (c - 4) // 2)

        for k in range(KD):
            low(0, 0, k)
        batches(dve, body, steps, NH + 2 + 2 * TPB + TPB)
        take(BATCH - 1)
        for t in range(TPB):
            rows(BATCH - 1, t)
        norm(BATCH - 1)


def attention_inputs(net, ctx):
    nc, a = net.nc, net.args
    ph = Phase(net, ctx, "q")
    two = range(2)
    g1 = ph.sb("g1", [P, KD])
    lam, lmb = ph.sb("lam", [P, 4]), ph.sb("lmb", [P, 4])
    qscale = ph.sb("qscale", [P, 1])
    sqv = ph.sb("sqv", [P, TPB, DIM])
    ssq = [ph.sb(f"ssq{i}", [P, TPB]) for i in two]
    rs = [ph.sb(f"rs{i}", [P, TPB]) for i in two]
    xn = [ph.sb(f"xn{i}", [P, TPB, DIM]) for i in two]
    xT = [ph.sb(f"xT{i}", [P, KD, SEQ]) for i in two]
    ex = [ph.sb(f"ex{i}", [P, SEQ]) for i in two]
    rl = [ph.sb(f"rl{i}", [P, SEQ]) for i in two]
    full, rest = ([ph.sb(f"{n}{i}", [P, TPB, 2, HALF]) for i in range(3)] for n in ("full", "rest"))
    res = [[ph.sb(f"res{n}{i}", [P, KD, TPB, 2, PARTS, HALF], BF16) for n in range(3)] for i in two]
    pX = [ph.ps(f"pX{k}", [P, SEQ]) for k in range(KD)]
    pE = [ph.ps(f"pE{i}", [P, SEQ]) for i in two]
    pV = [ph.ps(f"pV{i}", [P, SEQ]) for i in two]
    par_in, lam_ready, exp_lam, qs_ready = (ph.sig(n) for n in ("par_in", "lam_ready", "exp_lam", "qs_ready"))
    ssq_ready, rs_ready, xn_ready, turned, xT_ready = (ph.sig(n, 1) for n in ("ssq_ready", "rs_ready", "xn_ready", "turned", "xT_ready"))
    e_made, e_taken, v_made, v_taken, elu_ready = (ph.sig(n, 1) for n in ("e_made", "e_taken", "v_made", "v_taken", "elu_ready"))
    ex_free, stored = ph.sig("ex_free", 2), [ph.sig(f"stored{i}", 16 * 3) for i in two]
    full_ready, rest_ready, second_ready, third_ready = (ph.sig(n, 3) for n in ("full_ready", "rest_ready", "second_ready", "third_ready"))
    step, pool_step = ph.sig("step"), ph.sig("pool_step")

    ITEMS = 3 * KD

    def part(p, n, s):
        return res[p][n // KD][:, n % KD, :, :, s, :]

    nc.all_engine_barrier()
    block = ctx.enter_context(nc.Block())

    @block.sync
    def _(sp):
        with nc.allow_non_contiguous_dma(reason="1 KB, once"):
            sp.dma_start(g1[:, :], a["L1_attn_g1"].rearrange("(c p) -> p c", p=P)).then_inc(par_in.sem, 16)
        sp.dma_start(lam[:, :], a["L1_attn_lambda_params"].rearrange("(a h) -> a h", a=1).broadcast_to([P, 4])).then_inc(par_in.sem, 16)

        def store(b, p):
            sp.wait_ge(third_ready.sem, third_ready.after(ITEMS * b + ITEMS))
            for n in range(3):
                sp.dma_start(net.qkv_dram[n, :, bass.ds(b * TPB, TPB), :, :, :].rearrange("(k p) t g s w -> p k (t g s w)", p=P),
                             res[p][n][:, :, :, :, :, :].rearrange("p k t g s w -> p k (t g s w)"))\
                    .then_inc(stored[p].sem, 16)

        with sp.Fori(0, BATCH // 2) as i:
            for p in two:
                store(2 * i + p, p)
        for p in two:
            sp.wait_ge(stored[p].sem, stored[p].after(48 * BATCH // 2))

    @block.gpsimd
    def _(pool):
        steps = Steps(pool_step.sem)

        def front(b, p):
            pool.wait_ge(ssq_ready.sem, ssq_ready.after(b + 1))
            rstd_of(pool, steps, rs[p][:, :], ssq[p][:, :], RMS_EPS, net, 1.0 / DIM).then_inc(rs_ready.sem, 1)

        def body(b, p, before, behind):
            if behind:
                front(b + 1, 1 - p)
            for n in range(ITEMS):
                m = ITEMS * b + n
                pool.wait_ge(full_ready.sem, full_ready.after(m + 1))
                pool.wait_ge(third_ready.sem, third_ready.after(m + 1 - 3))
                pool.tensor_tensor(rest[n % 3][:, :, :, :], full[n % 3][:, :, :, :], part(p, n, 0), ALU.subtract).then_inc(rest_ready.sem, 1)

        front(0, 0)
        batches(pool, body, steps, 1)

    @block.scalar
    def _(act):
        act.wait_ge(par_in.sem, par_in.after(32))
        act.wait_ge(lam_ready.sem, lam_ready.after(1))
        nc.scalar.activation(lmb[:, 2:4], lmb[:, 0:2], ACT.Exp).then_inc(exp_lam.sem, 1)

        def front(b, p):
            xn_free = b + 1 - 2
            if not isinstance(b, int) or b >= 2:
                act.wait_ge(turned.sem, turned.after(xn_free))
                act.sem_inc(net.passed_act, 1)
            for t in range(TPB):
                ins = nc.scalar.activation(sqv[:, t, :], tile_of(net, b * TPB + t), ACT.Square, accum_out=ssq[p][:, t:t + 1])
            ins.then_inc(ssq_ready.sem, 1)

        def norm(b, p):
            act.wait_ge(rs_ready.sem, rs_ready.after(b + 1))
            act.sem_inc(net.passed_act, 1)
            for t in range(TPB):
                ins = nc.scalar.activation(xn[p][:, t, :], tile_of(net, b * TPB + t), ACT.Copy, scale=rs[p][:, t:t + 1])
            ins.then_inc(xn_ready.sem, 1)

        def second(b, p, n):
            m = ITEMS * b + n
            act.wait_ge(rest_ready.sem, rest_ready.after(m + 1))
            nc.scalar.activation(part(p, n, 1), rest[n % 3][:, :, :, :], ACT.Copy).then_inc(second_ready.sem, 1)

        def body(b, p, before, behind):
            if behind:
                front(b + 1, 1 - p)
            for n in range(4):
                m = 4 * b + n
                act.wait_ge(e_made.sem, e_made.after(m + 1))
                act.wait_ge(ex_free.sem, ex_free.after(m + 1 - 2))
                nc.scalar.activation(ex[n % 2][:, :], pE[n % 2][:, :], ACT.Exp)
                nc.scalar.activation(rl[n % 2][:, :], pE[n % 2][:, :], ACT.Relu).then_inc(e_taken.sem, 1)
                if n >= 2:
                    second(b, p, n - 2)
            if behind:
                norm(b + 1, 1 - p)
            for n in range(2, ITEMS):
                second(b, p, n)

        front(0, 0)
        norm(0, 0)
        batches(act, body)

    @block.tensor
    def _(pe):
        def front(b, p):
            pe.wait_ge(xn_ready.sem, xn_ready.after(b + 1))
            if not (isinstance(b, int) and b == 0):
                pe.wait_ge(xT_ready.sem, xT_ready.after(b))
            for k in range(KD):
                for t in range(TPB):
                    mm = pe.transpose(pX[k][:, t * P:(t + 1) * P], xn[p][:, t, k * P:(k + 1) * P], net.table["ident"])
            mm.then_inc(turned.sem, 1)

        def body(b, p, before, behind):
            first = isinstance(b, int) and b == 0
            pe.wait_ge(xT_ready.sem, xT_ready.after(b + 1))
            for n in range(6):
                if n < 4:
                    if not (first and n < 2):
                        pe.wait_ge(e_taken.sem, e_taken.after(4 * b + n - 1))
                    out, made = pE[n % 2], e_made
                else:
                    if not first:
                        pe.wait_ge(v_taken.sem, v_taken.after(2 * b + n - 4 - 1))
                    out, made = pV[n % 2], v_made
                for k in range(KD):
                    mm = pe.matmul(out[:, :], net.wqkvT[:, k, n * P:(n + 1) * P], xT[p][:, k, :], start=(k == 0), stop=(k == KD - 1))
                mm.then_inc(made.sem, 1)
            if behind:
                front(b + 1, 1 - p)

        front(0, 0)
        batches(pe, body)

    @block.vector
    def _(dve):
        steps = Steps(step.sem)
        dve.wait_ge(par_in.sem, par_in.after(32))
        lv = lam[:, :].rearrange("p (a b) -> p a b", b=2)
        dve.tensor_tensor(lmb[:, 0:2], lv[:, :, 0], lv[:, :, 1], ALU.mult).then_inc(lam_ready.sem, 1)
        dve.wait_ge(exp_lam.sem, exp_lam.after(1))
        dve.tensor_tensor(lmb[:, 0:1], lmb[:, 2:3], lmb[:, 3:4], ALU.subtract).then_inc(steps.sem, 1)
        dve.wait_ge(steps.sem, steps.done(1))
        dve.tensor_scalar(lmb[:, 0:1], lmb[:, 0:1], LAMBDA_INIT, 1.0, ALU.add, ALU.add).then_inc(steps.sem, 1)
        dve.wait_ge(steps.sem, steps.done(1))
        dve.tensor_scalar(lmb[:, 1:2], net.table["firsthalf"], lmb[:, 0:1], 1.0, ALU.mult, ALU.add).then_inc(steps.sem, 1)
        dve.wait_ge(steps.sem, steps.done(1))
        dve.tensor_tensor(lmb[:, 1:2], lmb[:, 1:2], lmb[:, 0:1], ALU.subtract).then_inc(steps.sem, 1)
        dve.wait_ge(steps.sem, steps.done(1))
        dve.tensor_scalar(qscale[:, :], lmb[:, 1:2], RET_SCALE, None, ALU.mult).then_inc(steps.sem, 1)
        dve.wait_ge(steps.sem, steps.done(1))

        def front(b, p):
            dve.wait_ge(turned.sem, turned.after(b + 1))
            for k in range(KD):
                ins = dve.tensor_scalar(xT[p][:, k, :], pX[k][:, :], g1[:, k:k + 1], None, ALU.mult)
            ins.then_inc(xT_ready.sem, 1)

        def third(b, p, n):
            m = ITEMS * b + n
            dve.wait_ge(second_ready.sem, second_ready.after(m + 1))
            dve.tensor_tensor(part(p, n, 2), rest[n % 3][:, :, :, :], part(p, n, 1), ALU.subtract).then_inc(third_ready.sem, 1)

        def body(b, p, before, behind):
            dve.wait_ge(stored[p].sem, stored[p].after(48 * (b // 2) if isinstance(b, int) else 24 * (b - p)))
            for n in range(ITEMS):
                m = ITEMS * b + n
                dst = full[n % 3][:, :, :, :].rearrange("p t g w -> p (t g w)")
                if n < 4:
                    dve.wait_ge(e_taken.sem, e_taken.after(4 * b + n + 1))
                    dve.scalar_tensor_tensor(out=rl[n % 2][:, :], in0=ex[n % 2][:, :], scalar=1.0, in1=rl[n % 2][:, :],
                                             op0=ALU.min, op1=ALU.add).then_inc(steps.sem, 1)
                    dve.wait_ge(steps.sem, steps.done(1))
                else:
                    dve.wait_ge(v_made.sem, v_made.after(2 * b + n - 4 + 1))
                dve.wait_ge(rest_ready.sem, rest_ready.after(m + 1 - 3))
                if n < 2:
                    ins = dve.tensor_scalar(dst, rl[n % 2][:, :], 1.0, qscale[:, :], ALU.subtract, ALU.mult)
                elif n < 4:
                    ins = dve.tensor_scalar(dst, rl[n % 2][:, :], 1.0, None, ALU.subtract)
                else:
                    ins = dve.tensor_copy(dst, pV[n - 4][:, :])
                ins.then_inc(ex_free.sem if n < 4 else v_taken.sem, 1)
                if n < 4:
                    dve.wait_ge(ex_free.sem, ex_free.after(4 * b + n + 1))
                else:
                    dve.wait_ge(v_taken.sem, v_taken.after(2 * b + n - 4 + 1))
                dve.tensor_copy(part(p, n, 0), full[n % 3][:, :, :, :]).then_inc(full_ready.sem, 1)
                if n >= 2:
                    third(b, p, n - 2)
            if behind:
                front(b + 1, 1 - p)
            third(b, p, ITEMS - 2)
            third(b, p, ITEMS - 1)

        front(0, 0)
        batches(dve, body, steps, 4)


def per_token_attention(net, ctx):
    nc, a = net.nc, net.args
    ph = Phase(net, ctx, "t")
    two = range(2)
    CH, STEPS = 4, P // 4
    kb, vb = ph.sb("kb", [P, P, PARTS, HALF], BF16), ph.sb("vb", [P, P, PARTS, HALF], BF16)
    q = [ph.sb(f"q{i}", [P, HEADS, PARTS, HALF], BF16) for i in two]
    rest = [ph.sb(f"rest{i}", [P, STEPS, HEADS]) for i in two]
    at = [ph.sb(f"at{i}", [P, PARTS, STEPS, HEADS], BF16) for i in two]
    ob = ph.sb("ob", [P, HEADS, P])
    g2, g3 = ph.sb("g2", [P, HD]), ph.sb("g3", [P, DIM])
    sqall = ph.sb("sqall", [P, GROUPS * DIM])
    hs, hr, hy = ph.sb("hs", [P, GROUPS * HEADS]), ph.sb("hr", [P, GROUPS * HEADS]), ph.sb("hy", [P, GROUPS * HEADS])
    es, er, ey = ph.sb("es", [P, GROUPS]), ph.sb("er", [P, GROUPS]), ph.sb("ey", [P, GROUPS])
    mrow = sqall[:, :].rearrange("p (j d) -> p j d", j=GROUPS)
    pA = [ph.ps(f"pA{i}", [P, STEPS, HEADS]) for i in two]
    pO = [ph.ps(f"pO{i}", [P, STEPS, HEADS]) for i in two]
    pW = [ph.ps(f"pW{i}", [P, 4, P]) for i in range(4)]
    g_in = ph.sig("g_in")
    k_in, v_in, q_in = ph.sig("k_in"), ph.sig("v_in"), [ph.sig(f"q_in{i}") for i in two]
    cleared_k, cleared_v = ph.sig("cleared_k"), ph.sig("cleared_v")
    a_made, o_made, first_ready, rest_ready, second_ready, third_ready = (
        ph.sig(n, 4) for n in ("a_made", "o_made", "first_ready", "rest_ready", "second_ready", "third_ready"))
    o_taken, w_made, w_act, w_dve = (ph.sig(n, 4) for n in ("o_taken", "w_made", "w_act", "w_dve"))
    squared, sums_ready, root_ready, scaled, es_ready, er_ready = (
        ph.sig(n) for n in ("squared", "sums_ready", "root_ready", "scaled", "es_ready", "er_ready"))
    step = ph.sig("step")
    att = net.att_res

    nc.all_engine_barrier()
    block = ctx.enter_context(nc.Block())

    @block.sync
    def _(sp):
        sp.dma_start(g2[:, :], a["L1_attn_g2"].rearrange("(a h) -> a h", a=1).broadcast_to([P, HD])).then_inc(g_in.sem, 16)
        sp.dma_start(g3[:, :], a["L1_attn_g3"].rearrange("(a h) -> a h", a=1).broadcast_to([P, DIM])).then_inc(g_in.sem, 16)
        q_src = net.qkv_dram[0].rearrange("(h e) t g s w -> e h t g s w", e=HD)
        k_src = net.qkv_dram[1].rearrange("(h e) t g s w -> e h t g s w", e=HD)
        v_src = net.qkv_dram[2].rearrange("(h d) t g s w -> h d t g s w", d=HD)

        def rows(dst, src, u, s, diagonal, sig):
            for j in range(GROUPS):
                to = dst[j * HD:(j + 1) * HD, j * HD:(j + 1) * HD, :, :] if diagonal else dst[j * HD:(j + 1) * HD, :, :, :]
                sp.dma_start(to.rearrange("p h s w -> p h (s w)"),
                             src[:, :, bass.ds(u * GROUPS + j, 1), s, :, :].rearrange("e h t s w -> e (h t) (s w)")).then_inc(sig.sem, 16)

        with sp.Fori(0, UNITS) as u:
            for s in two:
                n = 2 * u + s
                sp.wait_ge(a_made.sem, a_made.after(2 * n - 2))
                rows(q[s], q_src, u, s, False, q_in[s])
                if s == 0:
                    sp.wait_ge(cleared_k.sem, cleared_k.after(1))
                sp.wait_ge(a_made.sem, a_made.after(2 * n))
                rows(kb, k_src, u, s, True, k_in)
                if s == 0:
                    sp.wait_ge(cleared_v.sem, cleared_v.after(1))
                sp.wait_ge(o_made.sem, o_made.after(2 * n))
                rows(vb, v_src, u, s, True, v_in)

    @block.gpsimd
    def _(pool):
        pool.memset(vb[:, :, :, :].rearrange("p a s b -> p (a s b)"), 0.0).then_inc(cleared_v.sem, 1)

        def split(u, c):
            n = CH * u + c
            pool.wait_ge(first_ready.sem, first_ready.after(n + 1))
            pool.wait_ge(third_ready.sem, third_ready.after(n + 1 - 2))
            pool.tensor_tensor(rest[c % 2][:, :, :], rest[c % 2][:, :, :], at[c % 2][:, 0, :, :], ALU.subtract).then_inc(rest_ready.sem, 1)
            pool.wait_ge(second_ready.sem, second_ready.after(n + 1))
            pool.tensor_tensor(at[c % 2][:, 2, :, :], rest[c % 2][:, :, :], at[c % 2][:, 1, :, :], ALU.subtract).then_inc(third_ready.sem, 1)

        with pool.Fori(0, UNITS) as u:
            for c in range(CH):
                split(u, c)

    @block.tensor
    def _(pe):

        def scores(u, c):
            n = CH * u + c
            pe.wait_ge(first_ready.sem, first_ready.after(n - 1))
            for s in range(STEPS):
                at0 = (c % 2) * STEPS + s
                for k, (kp, qp) in enumerate(TERMS):
                    mm = pe.matmul(pA[c % 2][:, s, :], kb[:, :, kp, at0], q[c // 2][:, :, qp, at0],
                                   start=(k == 0), stop=(k == len(TERMS) - 1))
            mm.then_inc(a_made.sem, 1)

        def mix(u, c):
            n = CH * u + c
            pe.wait_ge(third_ready.sem, third_ready.after(n + 1))
            pe.wait_ge(o_taken.sem, o_taken.after(n - 1))
            for s in range(STEPS):
                at0 = (c % 2) * STEPS + s
                for k, (vp, ap) in enumerate(TERMS):
                    mm = pe.matmul(pO[c % 2][:, s, :], vb[:, :, vp, at0], at[c % 2][:, ap, s, :],
                                   start=(k == 0), stop=(k == len(TERMS) - 1))
            mm.then_inc(o_made.sem, 1)

        def turn(u):
            pe.wait_ge(o_taken.sem, o_taken.after(CH * (u + 1)))
            for r in range(4):
                done = (w_act, w_dve)[r // 2]
                pe.wait_ge(done.sem, done.after(2 * u + r % 2 - 1))
                for g in range(4):
                    mm = pe.transpose(pW[r][:, g, :], ob[:, 4 * r + g, :], net.table["ident"])
                mm.then_inc(w_made.sem, 1)

        def unit(u, before):
            for s in two:
                pe.wait_ge(k_in.sem, k_in.after(128 * (2 * u + s + 1)))
                pe.wait_ge(q_in[s].sem, q_in[s].after(128 * (u + 1)))
                scores(u, 2 * s)
                scores(u, 2 * s + 1)
                if s == 0 and before:
                    turn(u - 1)
                pe.wait_ge(v_in.sem, v_in.after(128 * (2 * u + s + 1)))
                mix(u, 2 * s)
                mix(u, 2 * s + 1)

        unit(0, False)
        with pe.Fori(1, UNITS) as u:
            unit(u, True)
        turn(UNITS - 1)

    def heads_of(u, r):
        return att[:, bass.ds(u * GROUPS, GROUPS), 4 * r * HD:4 * (r + 1) * HD].rearrange("p j (g d) -> p g j d", d=HD)

    def unit_rows(u):
        return att[:, bass.ds(u * GROUPS, GROUPS), :]

    def token_rows(u, j):
        return att[:, bass.ds(u * GROUPS + j, 1), :].rearrange("p a d -> p (a d)")

    @block.scalar
    def _(act):

        def take(u, c):
            n = CH * u + c
            act.wait_ge(a_made.sem, a_made.after(n + 1))
            act.wait_ge(o_made.sem, o_made.after(n - 1))
            nc.scalar.activation(at[c % 2][:, 0, :, :], pA[c % 2][:, :, :], ACT.Copy)
            nc.scalar.activation(rest[c % 2][:, :, :], pA[c % 2][:, :, :], ACT.Copy).then_inc(first_ready.sem, 1)

        def second(u, c):
            n = CH * u + c
            act.wait_ge(rest_ready.sem, rest_ready.after(n + 1))
            nc.scalar.activation(at[c % 2][:, 1, :, :], rest[c % 2][:, :, :], ACT.Copy).then_inc(second_ready.sem, 1)

        def heads(u):
            for r in two:
                act.wait_ge(w_made.sem, w_made.after(4 * u + r + 1))
                act.sem_inc(net.passed_act, 1)
                ins = nc.scalar.activation(heads_of(u, r), pW[r][:, :, :].rearrange("p g (j d) -> p g j d", d=HD), ACT.Copy)
                ins.then_inc(w_act.sem, 1)

        def squares(u):
            act.wait_ge(w_act.sem, w_act.after(2 * u + 2))
            act.wait_ge(w_dve.sem, w_dve.after(2 * u + 2))
            act.sem_inc(net.passed_act, 1)
            ins = nc.scalar.activation(sqall[:, :].rearrange("p (j d) -> p j d", j=GROUPS), unit_rows(u), ACT.Square)
            ins.then_inc(squared.sem, 1)

        def head_roots(u):
            act.wait_ge(sums_ready.sem, sums_ready.after(u + 1))
            nc.scalar.activation(hr[:, :], hs[:, :], ACT.Sqrt, bias=net.table["rmseps"], scale=1.0 / HD).then_inc(root_ready.sem, 1)

        def row_roots(u):
            act.wait_ge(scaled.sem, scaled.after(u + 1))
            act.sem_inc(net.passed_act, 1)
            for j in range(GROUPS):
                ins = nc.scalar.activation(sqall[:, j * DIM:(j + 1) * DIM], token_rows(u, j), ACT.Square, accum_out=es[:, j:j + 1])
            ins.then_inc(es_ready.sem, 1)
            act.wait_ge(es_ready.sem, es_ready.after(u + 1))
            nc.scalar.activation(er[:, :], es[:, :], ACT.Sqrt, bias=net.table["rmseps"], scale=1.0 / DIM).then_inc(er_ready.sem, 1)

        def unit(u, before):
            for c in range(CH):
                take(u, c)
                second(u, c)
                if before and c % 2:
                    for piece in (heads, squares, head_roots, row_roots)[c - 1:c + 1]:
                        piece(u - 1)

        unit(0, False)
        with act.Fori(1, UNITS) as u:
            unit(u, True)
        heads(UNITS - 1)
        squares(UNITS - 1)
        head_roots(UNITS - 1)
        row_roots(UNITS - 1)

    @block.vector
    def _(dve):
        steps = Steps(step.sem)

        def take(u, c):
            n = CH * u + c
            dve.wait_ge(o_made.sem, o_made.after(n + 1))
            if c == 0:
                dve.wait_ge(w_made.sem, w_made.after(4 * u))
            dve.tensor_copy(ob[:, :, c * STEPS:(c + 1) * STEPS].rearrange("p h t -> p t h"), pO[c % 2][:, :, :]).then_inc(o_taken.sem, 1)

        def inverse(root, mean_sq_scale, sums, out):
            dve.reciprocal(out, root).then_inc(steps.sem, 1)
            dve.wait_ge(steps.sem, steps.done(1))
            dve.tensor_scalar(root, sums, mean_sq_scale, RMS_EPS, ALU.mult, ALU.add).then_inc(steps.sem, 1)
            dve.wait_ge(steps.sem, steps.done(1))
            dve.tensor_tensor(root, root, out, ALU.mult).then_inc(steps.sem, 1)
            dve.wait_ge(steps.sem, steps.done(1))
            dve.tensor_tensor(root, root, out, ALU.mult).then_inc(steps.sem, 1)
            dve.wait_ge(steps.sem, steps.done(1))
            dve.tensor_scalar(root, root, -0.5, 1.5, ALU.mult, ALU.add).then_inc(steps.sem, 1)
            dve.wait_ge(steps.sem, steps.done(1))
            dve.tensor_tensor(out, out, root, ALU.mult).then_inc(steps.sem, 1)
            dve.wait_ge(steps.sem, steps.done(1))

        def heads(u):
            for r in (2, 3):
                dve.wait_ge(w_made.sem, w_made.after(4 * u + r + 1))
                ins = dve.tensor_copy(heads_of(u, r), pW[r][:, :, :].rearrange("p g (j d) -> p g j d", d=HD))
                ins.then_inc(w_dve.sem, 1)

        def head_sums(u):
            dve.wait_ge(squared.sem, squared.after(u + 1))
            dve.tensor_reduce(hs[:, :], sqall[:, :].rearrange("p (g d) -> p g d", d=HD), AX.X, ALU.add).then_inc(sums_ready.sem, 1)

        def head_norm(u):
            per_head = unit_rows(u).rearrange("p j (h d) -> p (j h) d", d=HD)
            dve.wait_ge(root_ready.sem, root_ready.after(u + 1))
            inverse(hr[:, :], 1.0 / HD, hs[:, :], hy[:, :])
            dve.tensor_tensor(per_head, per_head, hy[:, :].rearrange("p (g a) -> p g a", a=1).broadcast_to([P, GROUPS * HEADS, HD]), ALU.mult)\
                .then_inc(steps.sem, 1)
            dve.wait_ge(steps.sem, steps.done(1))
            dve.tensor_tensor(per_head, per_head, g2[:, :].rearrange("p (a d) -> p a d", a=1).broadcast_to([P, GROUPS * HEADS, HD]), ALU.mult)\
                .then_inc(scaled.sem, 1)

        def row_norm(u):
            dve.wait_ge(er_ready.sem, er_ready.after(u + 1))
            inverse(er[:, :], 1.0 / DIM, es[:, :], ey[:, :])
            for j in range(GROUPS):
                dve.tensor_scalar(mrow[:, j, :], g3[:, :], ey[:, j:j + 1], 1.0, ALU.mult, ALU.add).then_inc(steps.sem, 1)
            dve.wait_ge(steps.sem, steps.done(GROUPS))
            dve.tensor_tensor(unit_rows(u), unit_rows(u), mrow, ALU.mult).then_inc(steps.sem, 1)
            dve.wait_ge(steps.sem, steps.done(1))

        def unit(u, before):
            for c in range(CH):
                if c % 2 == 0 and before:
                    for piece in (heads, head_sums, head_norm, row_norm)[c:c + 2]:
                        piece(u - 1)
                take(u, c)

        dve.memset(kb[:, :, :, :].rearrange("p a s b -> p (a s b)"), 0.0).then_inc(cleared_k.sem, 1)
        dve.wait_ge(g_in.sem, g_in.after(32))
        dve.tensor_scalar(g2[:, :], g2[:, :], 1.0 - LAMBDA_INIT, None, ALU.mult).then_inc(steps.sem, 1)
        dve.wait_ge(steps.sem, steps.done(1))
        unit(0, False)
        with dve.Fori(1, UNITS) as u:
            steps.enter(u - 1, 6 + 1 + 6 + GROUPS + 1)
            unit(u, True)
            steps.leave(UNITS - 1)
        heads(UNITS - 1)
        head_sums(UNITS - 1)
        head_norm(UNITS - 1)
        row_norm(UNITS - 1)


def attention_mlp(net, ctx):
    nc, a = net.nc, net.args
    ph = Phase(net, ctx, "m")
    two = range(2)
    wr = ph.sb("wr", [P, KD, EXPERTS])
    ac = ph.sb("ac", [P, TPB, DIM])
    aT = ph.sb("aT", [P, KD, SEQ])
    hT = ph.sb("hT", [P, KD, SEQ])
    s = [ph.sb(f"s{i}", [P, TPB, DIM]) for i in two]
    y, xn = ph.sb("y", [P, TPB, DIM]), ph.sb("xn", [P, TPB, DIM])
    xT = ph.sb("xT", [P, KD, SEQ])
    yst, ymv, yrs = ph.sb("yst", [P, TPB, 6]), ph.sb("ymv", [P, TPB, 2]), ph.sb("yrs", [P, TPB])
    pX = ph.ps("pX", [P, KD, SEQ])
    pH = [ph.ps(f"pH{i}", [P, SEQ]) for i in two]
    pY = [ph.ps(f"pY{i}", [P, 2, DIM]) for i in two]
    pZ, pL = ph.ps("pZ", [P, SEQ]), ph.ps("pL", [P, TPB, EXPERTS])
    w_in, copied, turned, aT_ready = (ph.sig(n) for n in ("w_in", "copied", "turned", "aT_ready"))
    h_made, gelued, y_made, y_taken = ph.sig("h_made"), ph.sig("gelued"), ph.sig("y_made", 2), ph.sig("y_taken", 2)
    s_ready, mv_ready, yrs_ready, xn_ready = (ph.sig(n) for n in ("s_ready", "mv_ready", "yrs_ready", "xn_ready"))
    z_turned, xT_ready, l_made, l_taken = ph.sig("z_turned", 2), ph.sig("xT_ready", 1), ph.sig("l_made", 1), ph.sig("l_taken", 1)
    step, pool_step = ph.sig("step"), ph.sig("pool_step")

    nc.all_engine_barrier()
    block = ctx.enter_context(nc.Block())

    @block.sync
    def _(sp):
        sp.dma_start(wr[:, :, :], a["L1_ffn_w_router"].rearrange("(k p) n -> p k n", p=P)).then_inc(w_in.sem, 16)
        sp.wait_ge(w_in.sem, w_in.after(16))

    @block.gpsimd
    def _(pool):
        steps = Steps(pool_step.sem)

        def base(b, p):
            pool.wait_ge(y_taken.sem, y_taken.after(2 * b - 2))
            pool.sem_inc(net.passed_pool, 1)
            pool.tensor_tensor(s[p][:, :, :], net.x_res[:, bass.ds(b * TPB, TPB), :], net.att_res[:, bass.ds(b * TPB, TPB), :], ALU.add)\
                .then_inc(s_ready.sem, 1)

        def body(b, p, before, behind):
            if behind:
                base(b + 1, 1 - p)
            pool.wait_ge(mv_ready.sem, mv_ready.after(b + 1))
            rstd_of(pool, steps, yrs[:, :], ymv[:, :, 1], LN_EPS, net).then_inc(yrs_ready.sem, 1)

        base(0, 0)
        batches(pool, body, steps, 1)

    @block.tensor
    def _(pe):
        pe.wait_ge(w_in.sem, w_in.after(16))

        def turn(b):
            pe.wait_ge(copied.sem, copied.after(b + 1))
            if not isinstance(b, int) or b:
                pe.wait_ge(aT_ready.sem, aT_ready.after(b))
            for k in range(KD):
                for t in range(TPB):
                    mm = pe.transpose(pX[:, k, t * P:(t + 1) * P], ac[:, t, k * P:(k + 1) * P], net.table["ident"])
            mm.then_inc(turned.sem, 1)

        def up(b):
            pe.wait_ge(aT_ready.sem, aT_ready.after(b + 1))
            if not isinstance(b, int) or b:
                pe.wait_ge(gelued.sem, gelued.after(2 * b))
            for m in two:
                for k in range(KD):
                    mm = pe.matmul(pH[m][:, :], net.w1T[:, k, m * P:(m + 1) * P], aT[:, k, :], start=(k == 0), stop=(k == KD - 1))
                mm.then_inc(h_made.sem, 1)

        def down(b):
            pe.wait_ge(gelued.sem, gelued.after(2 * b + 2))
            for h in two:
                pe.wait_ge(y_taken.sem, y_taken.after(2 * b + h + 1 - 2))
                for t in (2 * h, 2 * h + 1):
                    for k in range(KD):
                        mm = pe.matmul(pY[h][:, t % 2, :], hT[:, k, t * P:(t + 1) * P], net.w2T[:, k, :],
                                       start=(k == 0), stop=(k == KD - 1))
                mm.then_inc(y_made.sem, 1)

        def turn_x(b, k):
            if k == 0:
                pe.wait_ge(xn_ready.sem, xn_ready.after(b + 1))
            pe.wait_ge(xT_ready.sem, xT_ready.after(2 * b + k))
            for t in range(TPB):
                mm = pe.transpose(pZ[:, t * P:(t + 1) * P], xn[:, t, k * P:(k + 1) * P], net.table["ident"])
            mm.then_inc(z_turned.sem, 1)

        def logits(b):
            pe.wait_ge(xT_ready.sem, xT_ready.after(2 * b + 2))
            pe.wait_ge(l_taken.sem, l_taken.after(b))
            for t in range(TPB):
                for k in range(KD):
                    mm = pe.matmul(pL[:, t, :], xT[:, k, t * P:(t + 1) * P], wr[:, k, :], start=(k == 0), stop=(k == KD - 1))
            mm.then_inc(l_made.sem, 1)

        def body(b, p, before, behind):
            if before:
                turn_x(b - 1, 0)
            if behind:
                turn(b + 1)
            down(b)
            if before:
                turn_x(b - 1, 1)
            if behind:
                up(b + 1)
            if before:
                logits(b - 1)

        turn(0)
        up(0)
        batches(pe, body)
        turn_x(BATCH - 1, 0)
        turn_x(BATCH - 1, 1)
        logits(BATCH - 1)

    @block.scalar
    def _(act):
        def copy(b):
            act.sem_inc(net.passed_act, 1)
            for t in range(TPB):
                att = net.att_res[:, bass.ds(b * TPB + t, 1), :].rearrange("p a d -> p (a d)")
                ins = nc.scalar.activation(ac[:, t, :], att, ACT.Copy)
            ins.then_inc(copied.sem, 1)

        def take(b):
            act.wait_ge(turned.sem, turned.after(b + 1))
            nc.scalar.activation(aT[:, :, :], pX[:, :, :], ACT.Copy).then_inc(aT_ready.sem, 1)

        def gelu(b):
            for m in two:
                act.wait_ge(h_made.sem, h_made.after(2 * b + m + 1))
                if m == 0 and (not isinstance(b, int) or b):
                    act.wait_ge(y_made.sem, y_made.after(2 * b))
                nc.scalar.activation(hT[:, m, :], pH[m][:, :], ACT.Gelu).then_inc(gelued.sem, 1)

        def take_x(b, k):
            act.wait_ge(z_turned.sem, z_turned.after(2 * b + k + 1))
            act.wait_ge(l_made.sem, l_made.after(b))
            nc.scalar.activation(xT[:, k, :], pZ[:, :], ACT.Copy).then_inc(xT_ready.sem, 1)

        def body(b, p, before, behind):
            if behind:
                copy(b + 1)
            if before:
                take_x(b - 1, 0)
            if behind:
                take(b + 1)
            if before:
                take_x(b - 1, 1)
            if behind:
                gelu(b + 1)

        copy(0)
        take(0)
        gelu(0)
        batches(act, body)
        take_x(BATCH - 1, 0)
        take_x(BATCH - 1, 1)

    @block.vector
    def _(dve):
        steps = Steps(step.sem)

        def rows(b, p):
            dve.wait_ge(s_ready.sem, s_ready.after(b + 1))
            for h in two:
                dve.wait_ge(y_made.sem, y_made.after(2 * b + h + 1))
                dve.tensor_tensor(y[:, 2 * h:2 * h + 2, :], pY[h][:, :, :], s[p][:, 2 * h:2 * h + 2, :], ALU.add).then_inc(y_taken.sem, 1)
            for t in range(TPB):
                if t % 2 == 0:
                    dve.wait_ge(y_taken.sem, y_taken.after(2 * b + t // 2 + 1))
                ins = dve.bn_stats(yst[:, t, :], y[:, t, :])
            ins.then_inc(steps.sem, 1)
            dve.wait_ge(steps.sem, steps.done(1))
            dve.sem_inc(net.passed, 1)
            for t in range(TPB):
                ins = dve.bn_aggr(ymv[:, t, :], yst[:, t, :])
            ins.then_inc(mv_ready.sem, 1)

        def norm(b):
            dve.wait_ge(yrs_ready.sem, yrs_ready.after(b + 1))
            dve.wait_ge(z_turned.sem, z_turned.after(2 * b))
            for t in range(TPB):
                ins = dve.tensor_scalar(xn[:, t, :], y[:, t, :], ymv[:, t, 0:1], yrs[:, t:t + 1], ALU.subtract, ALU.mult)
            ins.then_inc(xn_ready.sem, 1)
            for t in range(TPB):
                ins = dve.tensor_scalar(tile_of(net, b * TPB + t), y[:, t, :], ymv[:, t, 0:1], yrs[:, t:t + 1], ALU.subtract, ALU.mult)
            ins.then_inc(steps.sem, 1)
            dve.wait_ge(steps.sem, steps.done(1))

        def keep_logits(b):
            dve.wait_ge(l_made.sem, l_made.after(b + 1))
            dve.tensor_copy(net.lg[:, bass.ds(b * TPB, TPB), :], pL[:, :, :]).then_inc(l_taken.sem, 1)

        def body(b, p, before, behind):
            rows(b, p)
            norm(b)
            if before:
                keep_logits(b - 1)

        batches(dve, body, steps, 2)
        keep_logits(BATCH - 1)


def route(net, ctx):
    nc, a = net.nc, net.args
    ph = Phase(net, ctx, "g")
    net.wi = [net.sb(f"wi{i}", [P, KD, HID]) for i in range(2)]
    net.wo = [net.sb(f"wo{i}", [P, NH, DIM]) for i in range(2)]
    own, net.signals = net.signals, []
    net.w_in = [Signal(net, net.ctx, f"w_in{i}") for i in range(2)]
    net.signals = own
    two = range(2)
    lg = net.lg
    pr, s8, tmp = ph.sb("pr", [P, TILES, EXPERTS]), ph.sb("s8", [P, TILES, EXPERTS]), ph.sb("tmp", [P, TILES, EXPERTS])
    m1 = ph.sb("m1", [P, TILES])
    big = [P, MGROUPS, TOPK, TPG, EXPERTS]
    mask, pos, tot = ph.sb("mask", big), ph.sb("pos", big), ph.sb("tot", big)
    acc = [ph.sb(f"acc{i}", big) for i in two]
    posk, row, keep, idxf = (ph.sb(n, big[:-1]) for n in ("posk", "row", "keep", "idxf"))
    idx_out = ph.sb("idx_out", big[:-1], U32)
    zeros = ph.sb("zeros", [P, SLOTS // P * DIM])
    pP, pN = ph.ps("pP", [P, 512]), ph.ps("pN", [P, 512])
    shifted, exped, mask_ready, counted, idx_ready, step, cleared = (
        ph.sig(n) for n in ("shifted", "exped", "mask_ready", "counted", "idx_ready", "step", "cleared"))
    zero_ready, sent = ph.sig("zero_ready"), ph.sig("sent")

    def flat(t):
        return t[:, :, :, :, :].rearrange("p g k t e -> p (g k t e)")

    nc.all_engine_barrier()
    block = ctx.enter_context(nc.Block())

    @block.sync
    def _(sp):
        for e in range(2):
            load_expert(net, sp, e, e)
        sp.wait_ge(zero_ready.sem, zero_ready.after(1))
        sp.dma_start(net.xe_dram.rearrange("(p r) d -> p (r d)", p=P), zeros[:, :]).then_inc(cleared.sem, 16)
        sp.dma_start(net.ye_dram[SLOTS:SLOTS + 1, :], zeros[0:1, 0:DIM]).then_inc(cleared.sem, 16)
        sp.wait_ge(cleared.sem, cleared.after(32))

    @block.gpsimd
    def _(pool):
        pool.wait_ge(idx_ready.sem, idx_ready.after(1))
        pool.wait_ge(cleared.sem, cleared.after(32))
        for g in range(MGROUPS):
            for k in range(TOPK):
                for t in range(TPG):
                    pool.indirect_dma_start(net.xe_dram[:, :], bass.IndirectOffsetOnAxis(ap=idx_out[:, g, k, t:t + 1], axis=0),
                                            net.x_res[:, g * TPG + t, :], None, bounds_check=SLOTS - 1, oob_is_err=False)\
                        .then_inc(sent.sem, 16)
        pool.wait_ge(sent.sem, sent.after(16 * MGROUPS * TOPK * TPG))

    @block.tensor
    def _(pe):
        pe.wait_ge(mask_ready.sem, mask_ready.after(1))
        pe.matmul(pP[:, :], net.table["tri"], flat(mask), start=True, stop=True)
        pe.matmul(pN[:, :], net.table["ones"], flat(mask), start=True, stop=True).then_inc(counted.sem, 1)

    @block.scalar
    def _(act):
        act.wait_ge(shifted.sem, shifted.after(1))
        nc.scalar.activation(pr[:, :, :], lg[:, :, :], ACT.Exp).then_inc(exped.sem, 1)

    @block.vector
    def _(dve):
        dve.memset(zeros[:, :], 0.0).then_inc(zero_ready.sem, 1)
        steps = Steps(step.sem)

        def each(x):
            return x[:, :].rearrange("p (t a) -> p t a", a=1).broadcast_to([P, TILES, EXPERTS])

        dve.tensor_reduce(m1[:, :], lg[:, :, :], AX.X, ALU.max).then_inc(steps.sem, 1)
        dve.wait_ge(steps.sem, steps.done(1))
        dve.tensor_tensor(lg[:, :, :], lg[:, :, :], each(m1), ALU.subtract).then_inc(shifted.sem, 1)
        dve.wait_ge(exped.sem, exped.after(1))
        dve.tensor_reduce(m1[:, :], pr[:, :, :], AX.X, ALU.add).then_inc(steps.sem, 1)
        dve.wait_ge(steps.sem, steps.done(1))
        dve.reciprocal(m1[:, :], m1[:, :]).then_inc(steps.sem, 1)
        dve.wait_ge(steps.sem, steps.done(1))
        dve.tensor_tensor(pr[:, :, :], pr[:, :, :], each(m1), ALU.mult).then_inc(steps.sem, 1)
        dve.wait_ge(steps.sem, steps.done(1))
        first = net.table["first"].rearrange("p (a e) -> p a e", a=1).broadcast_to([P, TILES, EXPERTS])
        mview = mask[:, :, :, :, :]
        for k in range(TOPK):
            gate = net.gates[:, k, :]
            dve.tensor_reduce(gate, pr[:, :, :], AX.X, ALU.max).then_inc(steps.sem, 1)
            dve.wait_ge(steps.sem, steps.done(1))
            dve.tensor_tensor(s8[:, :, :], pr[:, :, :], gate.rearrange("p (t a) -> p t a", a=1).broadcast_to([P, TILES, EXPERTS]), ALU.is_equal).then_inc(steps.sem, 1)
            dve.wait_ge(steps.sem, steps.done(1))
            dve.tensor_tensor(s8[:, :, :], s8[:, :, :], first, ALU.mult).then_inc(steps.sem, 1)
            dve.wait_ge(steps.sem, steps.done(1))
            dve.tensor_reduce(m1[:, :], s8[:, :, :], AX.X, ALU.max).then_inc(steps.sem, 1)
            dve.wait_ge(steps.sem, steps.done(1))
            dve.tensor_tensor(tmp[:, :, :], s8[:, :, :], each(m1), ALU.is_equal).then_inc(steps.sem, 1)
            dve.wait_ge(steps.sem, steps.done(1))
            dve.tensor_copy(mview[:, :, k, :, :], tmp[:, :, :].rearrange("p (g t) e -> p g t e", g=MGROUPS)).then_inc(steps.sem, 1)
            dve.wait_ge(steps.sem, steps.done(1))
            dve.scalar_tensor_tensor(out=pr[:, :, :], in0=tmp[:, :, :], scalar=-2.0, in1=pr[:, :, :], op0=ALU.mult, op1=ALU.add).then_inc(steps.sem, 1)
            dve.wait_ge(steps.sem, steps.done(1))
        dve.sem_inc(mask_ready.sem, 1)
        dve.wait_ge(counted.sem, counted.after(1))
        dve.tensor_copy(flat(tot), pN[:, :]).then_inc(steps.sem, 1)
        dve.wait_ge(steps.sem, steps.done(1))
        dve.tensor_copy(flat(acc[0]), flat(tot)).then_inc(steps.sem, 1)
        dve.wait_ge(steps.sem, steps.done(1))
        src, dist = 0, 1
        av = [t[:, :, :, :, :].rearrange("p g k t e -> p g (k t) e") for t in acc]
        while dist < TOPK * TPG:
            dve.tensor_copy(av[1 - src][:, :, 0:dist, :], av[src][:, :, 0:dist, :]).then_inc(steps.sem, 1)
            dve.wait_ge(steps.sem, steps.done(1))
            dve.tensor_tensor(av[1 - src][:, :, dist:, :], av[src][:, :, dist:, :], av[src][:, :, 0:TOPK * TPG - dist, :], ALU.add).then_inc(steps.sem, 1)
            dve.wait_ge(steps.sem, steps.done(1))
            src, dist = 1 - src, 2 * dist
        dve.tensor_tensor(flat(acc[src]), flat(acc[src]), flat(tot), ALU.subtract).then_inc(steps.sem, 1)
        dve.wait_ge(steps.sem, steps.done(1))
        dve.tensor_tensor(flat(pos), pP[:, :], flat(acc[src]), ALU.add).then_inc(steps.sem, 1)
        dve.wait_ge(steps.sem, steps.done(1))
        dve.tensor_tensor(flat(pos), flat(pos), flat(mask), ALU.mult).then_inc(steps.sem, 1)
        dve.wait_ge(steps.sem, steps.done(1))

        def f4(t):
            return t[:, :, :, :].rearrange("p g k t -> p (g k t)")

        def f5(t):
            return t[:, :, :, :, :].rearrange("p g k t e -> p (g k t) e")

        dve.tensor_reduce(f4(posk), f5(pos), AX.X, ALU.add).then_inc(steps.sem, 1)
        dve.wait_ge(steps.sem, steps.done(1))
        base = net.table["base"].rearrange("p (a e) -> p a e", a=1).broadcast_to([P, MGROUPS * TOPK * TPG, EXPERTS])
        dve.tensor_tensor(f5(pos), f5(mask), base, ALU.mult).then_inc(steps.sem, 1)
        dve.wait_ge(steps.sem, steps.done(1))
        dve.tensor_reduce(f4(row), f5(pos), AX.X, ALU.add).then_inc(steps.sem, 1)
        dve.wait_ge(steps.sem, steps.done(1))
        for g in range(MGROUPS):
            r = row[:, g, :, :].rearrange("p k t -> p (k t)")
            dve.scalar_tensor_tensor(out=r, in0=r, scalar=float(g * CAP - 1), in1=posk[:, g, :, :].rearrange("p k t -> p (k t)"),
                               op0=ALU.add, op1=ALU.add).then_inc(steps.sem, 1)
            dve.wait_ge(steps.sem, steps.done(1))
        dve.tensor_scalar(f4(keep), f4(posk), float(CAP), None, ALU.is_le).then_inc(steps.sem, 1)
        dve.wait_ge(steps.sem, steps.done(1))
        dve.tensor_scalar(f4(idxf), f4(row), float(SLOTS), None, ALU.subtract).then_inc(steps.sem, 1)
        dve.wait_ge(steps.sem, steps.done(1))
        dve.tensor_tensor(f4(idxf), f4(idxf), f4(keep), ALU.mult).then_inc(steps.sem, 1)
        dve.wait_ge(steps.sem, steps.done(1))
        dve.tensor_scalar(f4(idxf), f4(idxf), float(SLOTS), None, ALU.add).then_inc(steps.sem, 1)
        dve.wait_ge(steps.sem, steps.done(1))
        dve.tensor_copy(idx_out[:, :, :, :].rearrange("p g k t -> p (g k t)"), f4(idxf)).then_inc(steps.sem, 1)
        dve.wait_ge(steps.sem, steps.done(1))
        dve.tensor_copy(net.idx_back[:, :, :].rearrange("p (g t) k -> p g k t", g=MGROUPS), idxf[:, :, :, :]).then_inc(steps.sem, 1)
        dve.wait_ge(steps.sem, steps.done(1))
        dve.sem_inc(idx_ready.sem, 1)


def load_expert(net, sp, e, p):
    a = net.args
    sp.dma_start(net.wi[p][:, :, :], a["L1_ffn_wi"][bass.ds(e, 1), :, :].rearrange("a (k p) n -> p (a k) n", p=P)).then_inc(net.w_in[p].sem, 16)
    sp.dma_start(net.wo[p][:, :, :], a["L1_ffn_wo"][bass.ds(e, 1), :, :].rearrange("a (k p) n -> p (a k) n", p=P)).then_inc(net.w_in[p].sem, 16)


def experts(net, ctx):
    nc, a = net.nc, net.args
    ph = Phase(net, ctx, "e")
    two = range(2)
    wi, wo, w_in = net.wi, net.wo, net.w_in
    xr = [ph.sb(f"xr{i}", [P, 3, DIM]) for i in two]
    xT = [ph.sb(f"xT{i}", [P, KD, ROWS]) for i in two]
    hT = [ph.sb(f"hT{i}", [P, NH, ROWS]) for i in two]
    yo = [ph.sb(f"yo{i}", [P, 3, DIM]) for i in two]
    pX = [ph.ps(f"pX{k}", [P, ROWS]) for k in range(KD)]
    pH = [ph.ps(f"pH{i}", [P, ROWS]) for i in range(4)]
    pD = [ph.ps(f"pD{i}", [P, DIM]) for i in two]
    x_in, stored = ([ph.sig(f"{n}{i}", h) for i in two] for n, h in (("x_in", 0), ("stored", 48)))
    turned, xT_ready, h_made, h_act, h_dve, d_made, d_act, d_dve = (
        ph.sig(n, 1) for n in ("turned", "xT_ready", "h_made", "h_act", "h_dve", "d_made", "d_act", "d_dve"))

    def later(i, n):
        return not isinstance(i, int) or i >= n

    def in_pairs(eng, body):
        with eng.Fori(0, EXPERTS // 2 - 1) as i:
            for p in two:
                body(2 * i + p, p, True)
        body(EXPERTS - 2, 0, True)
        body(EXPERTS - 1, 1, False)

    nc.all_engine_barrier()
    block = ctx.enter_context(nc.Block())

    @block.sync
    def _(sp):

        def front(e, p):
            if later(e, 2):
                sp.wait_ge(d_made.sem, d_made.after(3 * (e - 1)))
            for r, (r0, n) in enumerate(RTILES):
                sp.dma_start(xr[p][0:n, r, :], net.xe_dram[bass.ds(e * ROWS + r0, n), :]).then_inc(x_in[p].sem, 16)
            if later(e, 2):
                load_expert(net, sp, e, p)

        def back(e, p):
            for r, (r0, n) in enumerate(RTILES):
                if r == 0:
                    sp.wait_ge(d_act.sem, d_act.after(2 * e + 1))
                elif r == 1:
                    sp.wait_ge(d_dve.sem, d_dve.after(e + 1))
                else:
                    sp.wait_ge(d_act.sem, d_act.after(2 * e + 2))
                sp.dma_start(net.ye_dram[bass.ds(e * ROWS + r0, n), :], yo[p][0:n, r, :]).then_inc(stored[p].sem, 16)

        front(0, 0)
        front(1, 1)
        back(0, 0)
        with sp.Fori(0, EXPERTS // 2 - 1) as i:
            for p in two:
                front(2 * i + 2 + p, p)
                back(2 * i + 1 + p, 1 - p)
        back(EXPERTS - 1, 1)
        for p in two:
            sp.wait_ge(stored[p].sem, stored[p].after(48 * EXPERTS // 2))

    @block.tensor
    def _(pe):
        def front(e, p):
            pe.wait_ge(x_in[p].sem, x_in[p].after(48 * (e // 2 + 1) if isinstance(e, int) else 24 * (e - p) + 48))
            if later(e, 1):
                pe.wait_ge(xT_ready.sem, xT_ready.after(e))
            for k in range(KD):
                for r, (r0, n) in enumerate(RTILES):
                    mm = pe.transpose(pX[k][:, r0:r0 + n], xr[p][0:n, r, k * P:(k + 1) * P], net.table["ident"][0:n, 0:n])
            mm.then_inc(turned.sem, 1)

        def body(e, p, behind):
            pe.wait_ge(w_in[p].sem, w_in[p].after(32 * (e // 2 + 1) if isinstance(e, int) else 16 * (e - p) + 32))
            pe.wait_ge(xT_ready.sem, xT_ready.after(e + 1))
            for c in range(NH):
                if later(e, 1) or c >= 4:
                    pe.wait_ge((h_act, h_dve)[c % 2].sem, (h_act, h_dve)[c % 2].after(4 * e + c // 2 - 1))
                for k in range(KD):
                    mm = pe.matmul(pH[c % 4][:, :], wi[p][:, k, c * P:(c + 1) * P], xT[p][:, k, :], start=(k == 0), stop=(k == KD - 1))
                mm.then_inc(h_made.sem, 1)
            if behind:
                front(e + 1, 1 - p)
            pe.wait_ge(h_act.sem, h_act.after(4 * e + 4))
            pe.wait_ge(h_dve.sem, h_dve.after(4 * e + 4))
            for r, (r0, n) in enumerate(RTILES):
                if r == 2:
                    pe.wait_ge(d_act.sem, d_act.after(2 * e + 1))
                elif later(e, 1):
                    pe.wait_ge((d_act if r == 0 else d_dve).sem, (d_act if r == 0 else d_dve).after(2 * e if r == 0 else e))
                for c in range(NH):
                    mm = pe.matmul(pD[r % 2][0:n, :], hT[p][:, c, r0:r0 + n], wo[p][:, c, :], start=(c == 0), stop=(c == NH - 1))
                mm.then_inc(d_made.sem, 1)

        front(0, 0)
        in_pairs(pe, body)

    @block.scalar
    def _(act):
        def back(e, p):
            for c in range(0, NH, 2):
                act.wait_ge(h_made.sem, h_made.after(NH * e + c + 1))
                nc.scalar.activation(hT[p][:, c, :], pH[c % 4][:, :], ACT.Relu).then_inc(h_act.sem, 1)
            act.wait_ge(stored[p].sem, stored[p].after(48 * (e // 2) if isinstance(e, int) else 24 * (e - p)))
            for r in (0, 2):
                n = RTILES[r][1]
                act.wait_ge(d_made.sem, d_made.after(3 * e + r + 1))
                nc.scalar.activation(yo[p][0:n, r, :], pD[0][0:n, :], ACT.Copy).then_inc(d_act.sem, 1)

        staggered(act, EXPERTS, lambda e, p: None, back)

    @block.vector
    def _(dve):
        def front(e, p):
            dve.wait_ge(turned.sem, turned.after(e + 1))
            for k in range(KD):
                ins = dve.tensor_copy(xT[p][:, k, :], pX[k][:, :])
            ins.then_inc(xT_ready.sem, 1)

        def body(e, p, behind):
            for c in range(1, NH, 2):
                dve.wait_ge(h_made.sem, h_made.after(NH * e + c + 1))
                dve.tensor_scalar(hT[p][:, c, :], pH[c % 4][:, :], 0.0, None, ALU.max).then_inc(h_dve.sem, 1)
            if behind:
                front(e + 1, 1 - p)
            dve.wait_ge(stored[p].sem, stored[p].after(48 * (e // 2) if isinstance(e, int) else 24 * (e - p)))
            dve.wait_ge(d_made.sem, d_made.after(3 * e + 2))
            dve.tensor_copy(yo[p][:, 1, :], pD[1][:, :]).then_inc(d_dve.sem, 1)

        front(0, 0)
        in_pairs(dve, body)


def combine(net, ctx):
    nc = net.nc
    ph = Phase(net, ctx, "c")
    NB = 8
    NG = 4
    idx = [ph.sb(f"idx{i}", [P, NG, TOPK], U32) for i in range(NB // NG)]
    ya = [[ph.sb(f"ya{k}{i}", [P, DIM]) for k in range(TOPK)] for i in range(NB)]
    y, yo = ([ph.sb(f"{n}{i}", [P, DIM]) for i in range(NB)] for n in ("y", "yo"))
    yst, ymv, yrs = ([ph.sb(f"{n}{i}", [P, NG, w]) for i in range(NB // NG)] for n, w in (("yst", 6), ("ymv", 2), ("yrs", 1)))
    gathered = [ph.sig(f"gathered{i}") for i in range(NB)]
    stored = [ph.sig(f"stored{i}", 16) for i in range(NB)]
    ya_used, ymv_ready, yrs_ready, normed, step, pool_step, ones_ready = (
        ph.sig(n, h) for n, h in (("ya_used", NB), ("ymv_ready", 0), ("yrs_ready", 0), ("normed", NB), ("step", 0),
                                  ("pool_step", 0), ("ones_ready", 0)))
    out_rows = net.out.rearrange("b (t p) d -> (b t) p d", p=P)

    nc.all_engine_barrier()
    block = ctx.enter_context(nc.Block())

    @block.gpsimd
    def _(pool):
        steps = Steps(pool_step.sem)
        def gather(b, g):
            n = b * NB + g * NG
            pool.wait_ge(ya_used.sem, ya_used.after(n + NG - NB))
            pool.tensor_copy(idx[g][:, :, :], net.idx_back[:, bass.ds(n, NG), :]).then_inc(steps.sem, 1)
            pool.wait_ge(steps.sem, steps.done(1))
            pool.sem_inc(net.passed_pool, 1)
            for t in range(NG):
                for k in range(TOPK):
                    pool.indirect_dma_start(ya[g * NG + t][k][:, :], None, net.ye_dram[:, :],
                                            bass.IndirectOffsetOnAxis(ap=idx[g][:, t, k:k + 1], axis=0),
                                            bounds_check=SLOTS, oob_is_err=False).then_inc(gathered[g * NG + t].sem, 16)

        def roots(m, g):
            pool.wait_ge(ymv_ready.sem, ymv_ready.after(m + 1))
            rstd_of(pool, steps, yrs[g][:, :, 0], ymv[g][:, :, 1], LN_EPS, net).then_inc(yrs_ready.sem, 1)

        gather(0, 0)
        gather(0, 1)
        roots(0, 0)
        with pool.Fori(1, TILES // NB) as b:
            steps.enter(b - 1, 4)
            gather(b, 0)
            roots(2 * b - 1, 1)
            gather(b, 1)
            roots(2 * b, 0)
            steps.leave(TILES // NB - 1)
        roots(2 * (TILES // NB) - 1, 1)

    @block.vector
    def _(dve):
        steps = Steps(step.sem)

        def add_rows(b, g):
            for t in range(g * NG, (g + 1) * NG):
                i = b * NB + t
                dve.wait_ge(gathered[t].sem, gathered[t].after(32 * (b + 1)))
                dve.wait_ge(normed.sem, normed.after(i + 1 - NB))
                src = tile_of(net, i)
                for k in range(TOPK):
                    gate = net.gates[:, k, bass.ds(i, 1)]
                    dve.scalar_tensor_tensor(out=y[t][:, :], in0=ya[t][k][:, :], scalar=gate, in1=src, op0=ALU.mult, op1=ALU.add)\
                        .then_inc(steps.sem, 1)
                    dve.wait_ge(steps.sem, steps.done(1))
                    src = y[t][:, :]
                dve.sem_inc(ya_used.sem, 1)
                dve.bn_stats(yst[g][:, t % NG, :], y[t][:, :]).then_inc(steps.sem, 1)
                dve.wait_ge(steps.sem, steps.done(1))
                dve.sem_inc(net.passed, 1)
                ins = dve.bn_aggr(ymv[g][:, t % NG, :], yst[g][:, t % NG, :])
            ins.then_inc(ymv_ready.sem, 1)

        def norm_rows(m, g):
            dve.wait_ge(yrs_ready.sem, yrs_ready.after(m + 1))
            for t in range(NG):
                dve.wait_ge(stored[g * NG + t].sem, stored[g * NG + t].after(8 * (m - g)))
                dve.tensor_scalar(yo[g * NG + t][:, :], y[g * NG + t][:, :], ymv[g][:, t, 0:1], yrs[g][:, t, :], ALU.subtract, ALU.mult)\
                    .then_inc(normed.sem, 1)

        add_rows(0, 0)
        add_rows(0, 1)
        norm_rows(0, 0)
        with dve.Fori(1, TILES // NB) as b:
            steps.enter(b - 1, 3 * NB)
            add_rows(b, 0)
            norm_rows(2 * b - 1, 1)
            add_rows(b, 1)
            norm_rows(2 * b, 0)
            steps.leave(TILES // NB - 1)
        norm_rows(2 * (TILES // NB) - 1, 1)

    @block.sync
    def _(sp):
        with sp.Fori(0, TILES // NB) as b:
            for t in range(NB):
                i = b * NB + t
                sp.wait_ge(normed.sem, normed.after(i + 1))
                sp.dma_start(out_rows[bass.ds(i, 1), :, :].rearrange("a p d -> (a p) d"), yo[t][:, :]).then_inc(stored[t].sem, 16)
        for s in stored:
            sp.wait_ge(s.sem, s.after(16 * TILES // NB))


PHASES = [prepare, retention, ternary_ffn, attention_inputs, per_token_attention, attention_mlp, route, experts, combine]
FINAL = True


def program(nc, args, out, phases=len(PHASES), shown=False):
    with ExitStack() as whole:
        net = Net(nc, whole, args)
        net.out = out
        for phase in PHASES[:phases]:
            net.signals = []
            with ExitStack() as ctx:
                phase(net, ctx)
            if phase is ternary_ffn:
                net.layer0.close()
            if phase is attention_inputs:
                net.projections.close()
            for sem in net.signals:
                nc.sync.sem_clear(sem)
        net.layer0.close()
        net.projections.close()
        if shown:
            with ExitStack() as ctx:
                done = ctx.enter_context(nc.semaphore("shown"))
                block = ctx.enter_context(nc.Block())
                src = net.att_res if shown == "att" else net.x_res

                @block.sync
                def _(sp):
                    sp.dma_start(out.rearrange("b (t p) d -> p (b t) d", p=P), src[:, :, :]).then_inc(done, 16)
                    sp.wait_ge(done, 16)


NAMES = ["L0_attn_x", "L0_attn_past_kv", "L0_attn_W_qkv", "L0_attn_gn_weight", "L0_attn_gn_bias", "L0_ffn_W_fc",
         "L0_ffn_ln_w", "L0_ffn_ln_b", "L0_ffn_W_proj", "L1_attn_Wq", "L1_attn_Wk", "L1_attn_Wv",
         "L1_attn_lambda_params", "L1_attn_g1", "L1_attn_g2", "L1_attn_g3", "L1_attn_W1", "L1_attn_W2",
         "L1_ffn_w_router", "L1_ffn_wi", "L1_ffn_wo"]


def kernel(**inputs):
    import concourse.bacc as bacc
    from concourse.bass_utils import run_bass_kernel_spmd

    nc = bacc.Bacc("TRN2", target_bir_lowering=False, num_devices=1)
    arrays = {name: np.ascontiguousarray(inputs[name]) for name in NAMES}
    arrays["consts"], arrays["consts0"] = CONSTS, CONSTS0
    args = {n: nc.dram_tensor(n, a.shape, mybir.dt.from_np(a.dtype), kind="ExternalInput").ap() for n, a in arrays.items()}
    out = nc.dram_tensor("out", (BATCH, SEQ, DIM), F32, kind="ExternalOutput").ap()
    program(nc, args, out)
    return run_bass_kernel_spmd(nc, [arrays], core_ids=[0]).results[0]["out"]
```

```python
from contextlib import ExitStack

import numpy as np
import concourse.bass as bass
from concourse import mybir

F32 = mybir.dt.float32
F32R = mybir.dt.float32r
BF16 = mybir.dt.bfloat16
I32 = mybir.dt.int32
U32 = mybir.dt.uint32
ALU = mybir.AluOpType
ACT = mybir.ActivationFunctionType
AX = mybir.AxisListType

P = 128
BATCH, SEQ, DIM = 8, 512, 256
TOKENS = BATCH * SEQ
TILES = TOKENS // P
TPB = SEQ // P
KD = DIM // P
HEADS, HD = 16, 16
HPK = P // HD
HID = 1024
NH = HID // P
LN_EPS = 1e-5
ABS_EPS = 1e-6
RMS_EPS = float(np.finfo(np.float32).eps)
LAMBDA_INIT = 0.8 - 0.6 * float(np.exp(-0.3 * 0))
RET_SCALE = 1.0 / float(np.sqrt(DIM // 2))
UNIT = 8 * P
UNITS = TOKENS // UNIT
GROUPS = UNIT // P
HALF = 64
PARTS = 3
TERMS = [(0, 0), (0, 1), (1, 0), (1, 1), (0, 2), (2, 0)]
EXPERTS, CAP, TOPK, MGROUPS = 8, 160, 2, 2
TPG = TILES // MGROUPS
ROWS = MGROUPS * CAP
SLOTS = EXPERTS * ROWS
RTILES = [(0, 128), (128, 128), (256, 64)]



def constant_table(names, of_them):
    gamma = 1.0 - 2.0 ** (-5.0 - np.arange(HEADS, dtype=np.float64))
    p = np.arange(P)
    parts = {}
    parts["ident"] = np.eye(P)
    parts["ones"] = np.ones((P, P))
    parts["tri"] = (p[:, None] <= p[None, :]).astype(np.float64)
    order = [half * HPK + 2 * r + par for r in range(4) for half in range(2) for par in range(2)]
    diff = p[None, :] - p[:, None]
    dec = np.where(diff[None] >= 0, gamma[order][:, None, None] ** np.maximum(diff, 0)[None], 0.0)
    parts["decay"] = dec.transpose(1, 0, 2).reshape(P, -1)
    hrow = np.arange(P) // HD
    qd = np.stack([gamma[half * HPK + hrow][:, None] ** (p[None, :] + 1) for half in range(2)], 1)
    parts["qdecay"] = qd.reshape(P, -1)
    parts["kdecay"] = gamma[np.arange(DIM) // HD][None, :] ** (P - 1 - p)[:, None]
    parts["tiledecay"] = np.stack([gamma[half * HPK + hrow] ** P for half in range(2)], 1)
    parts["block"] = (hrow[:, None] == hrow[None, :]).astype(np.float64)
    parts["even"] = (hrow % 2 == 0).astype(np.float64)[:, None]
    parts["odd"] = (hrow % 2 == 1).astype(np.float64)[:, None]
    parts["first"] = np.tile(EXPERTS - np.arange(EXPERTS), (P, 1))
    parts["base"] = np.tile(np.arange(EXPERTS) * ROWS, (P, 1))
    parts["firsthalf"] = (p % HD < HD // 2).astype(np.float64)[:, None]
    parts["rmseps"] = np.full((P, 1), RMS_EPS)
    parts["minushalf"] = np.full((P, HEADS), -0.5)
    parts = {name: a for name, a in parts.items() if (name in names) == of_them}
    at, where = 0, {}
    for name, a in parts.items():
        where[name] = (at, a.shape[1])
        at += a.shape[1]
    return np.concatenate([a for a in parts.values()], 1).astype(np.float32), where


LAYER0_CONSTS = ("block", "decay", "qdecay", "kdecay", "tiledecay", "even", "odd")
CONSTS, WHERE = constant_table(LAYER0_CONSTS, False)
CONSTS0, WHERE0 = constant_table(LAYER0_CONSTS, True)


class Signal:

    def __init__(self, net, ctx, name, head=0):
        self.sem = ctx.enter_context(net.nc.semaphore(name))
        self.head = head
        net.signals.append(self.sem)
        if head:
            net.nc.sync.sem_inc(self.sem, head)

    def after(self, count):
        return count + self.head


class Steps:

    def __init__(self, sem):
        self.sem, self.base, self.k = sem, 0, 0

    def done(self, more=0):
        self.k += more
        return self.base + self.k

    def enter(self, i, per):
        self.entry, self.per = self.base + self.k, per
        self.base, self.k = self.entry + i * per, 0

    def leave(self, times):
        assert self.k == self.per, (self.k, self.per)
        self.base, self.k = self.entry + times * self.per, 0


class Net:

    def __init__(self, nc, ctx, args):
        self.nc, self.args, self.ctx = nc, args, ctx
        self.sb = lambda name, shape, dt=F32: ctx.enter_context(nc.sbuf_tensor(name, shape, dt))
        self.passed = ctx.enter_context(nc.semaphore("passed"))
        self.passed_act = ctx.enter_context(nc.semaphore("passed_act"))
        self.passed_pool = ctx.enter_context(nc.semaphore("passed_pool"))
        self.x_res = self.sb("x_res", [P, TILES, DIM])
        self.w1T = self.sb("w1T", [P, KD, DIM])
        self.w2T = self.sb("w2T", [P, KD, DIM])
        self.qkv_dram = nc.dram_tensor("qkv_dram", [3, DIM, TILES, 2, PARTS, HALF], BF16).ap()
        self.xe_dram = nc.dram_tensor("xe_dram", [SLOTS, DIM], F32).ap()
        self.ye_dram = nc.dram_tensor("ye_dram", [SLOTS + 1, DIM], F32).ap()
        self.att_res = self.sb("att_res", [P, TILES, DIM])
        self.lg = self.sb("lg", [P, TILES, EXPERTS])
        self.gates = self.sb("gates", [P, TOPK, TILES])
        self.idx_back = self.sb("idx_back", [P, TILES, TOPK], U32)
        self.const = self.sb("const", [P, CONSTS.shape[1]])
        self.table = {}
        for name, (at, n) in WHERE.items():
            self.table[name] = self.const[:, at:at + n]
        self.projections = ExitStack()
        self.wqkvT = self.projections.enter_context(nc.sbuf_tensor("wqkvT", [P, KD, 3 * DIM], F32))
        self.layer0 = ExitStack()
        early = lambda name, shape, dt=F32: self.layer0.enter_context(nc.sbuf_tensor(name, shape, dt))
        self.const0 = early("const0", [P, CONSTS0.shape[1]])
        for name, (at, n) in WHERE0.items():
            self.table[name] = self.const0[:, at:at + n]
        self.wfcT = early("wfcT", [P, KD, HID], F32R)
        self.wpjH = early("wpjH", [P, NH, DIM + 2], F32R)
        self.wpjL = early("wpjL", [P, NH, DIM + 2], F32R)
        self.w, self.pkv_raw = early("w", [P, KD, 3 * DIM]), early("pkv_raw", [P, KD, HD])
        self.signals = []
        self.gnw, self.gnb = early("gnw", [P, KD]), early("gnb", [P, KD])
        self.w0_in, self.gn_in = Signal(self, ctx, "w0_in"), Signal(self, ctx, "gn_in")
        self.u0, self.u1 = early("u0", [P, DIM]), early("u1", [P, DIM])


def retention(net, ctx):
    nc, a = net.nc, net.args

    def sb(name, shape, dt=F32):
        return ctx.enter_context(nc.sbuf_tensor("r_" + name, shape, dt))

    def ps(name, shape):
        return ctx.enter_context(nc.psum_tensor("r_" + name, shape, F32))

    def sig(name, head=0):
        return Signal(net, ctx, "r_" + name, head)

    w, pkv_raw, w_in = net.w, net.pkv_raw, net.w0_in
    pkv = sb("pkv", [P, KD, P])
    gnw, gnb, gn_in = net.gnw, net.gnb, net.gn_in
    rT, yT, square = sb("rT", [P, KD, SEQ]), sb("yT", [P, KD, SEQ]), sb("square", [P, P])
    xin = [sb(f"xin{i}", [P, DIM]) for i in range(4)]
    two = range(2)
    xT = [sb(f"xT{i}", [P, KD, P]) for i in two]
    qT = [sb(f"qT{i}", [P, KD, P]) for i in range(TPB)]
    qS = [sb(f"qS{i}", [P, KD, P]) for i in range(TPB)]
    qE = [sb(f"qE{i}", [P, KD, P]) for i in range(TPB)]
    qO = [sb(f"qO{i}", [P, KD, P]) for i in range(TPB)]
    kT = [sb(f"kT{i}", [P, KD, P]) for i in two]
    v = [sb(f"v{i}", [P, DIM]) for i in range(TPB)]
    vE, vO = ([sb(f"v{n}{i}", [P, DIM]) for i in range(TPB)] for n in "EO")
    ks = [sb(f"ks{i}", [P, DIM]) for i in two]
    prob = [sb(f"prob{i}", [P, 4, 4, P]) for i in two]
    state = [sb(f"state{i}", [P, KD, P]) for i in two]
    upd = sb("upd", [P, KD, P])
    gst = sb("gst", [P, 2, TPB, KD])
    gsum = sb("gsum", [P, 4])
    gaff = sb("gaff", [P, 3, KD])
    bst = sb("bst", [P, TPB, 6])
    mv = sb("mv", [P, TPB, 2])
    rstd = sb("rstd", [P, TPB])
    y1 = [sb(f"y1{i}", [P, DIM]) for i in range(TPB)]

    pXR = ps("pXR", [P, 512])
    pX, pR = pXR[:, 0:DIM], pXR[:, DIM:2 * DIM].rearrange("p (k t) -> p k t", k=KD)
    pQV = ps("pQV", [P, 512])
    pQ, pV = pQV[:, 0:DIM].rearrange("p (k t) -> p k t", k=KD), pQV[:, DIM:2 * DIM]
    pKK = ps("pKK", [P, 512])
    pKT, pK = pKK[:, 0:DIM].rearrange("p (k t) -> p k t", k=KD), pKK[:, DIM:2 * DIM]
    pUG = ps("pUG", [P, 512])
    pU, pG = pUG[:, 0:DIM], pUG[:, DIM:DIM + 2 * TPB * KD]
    pS = [ps(f"pS{i}", [P, 4, P]) for i in range(4)]
    pB = [pS[2 + i][:, 0:KD, :].rearrange("p k t -> p (k t)") for i in two]

    x_in = [sig(f"x_in{i}") for i in range(4)]
    x_kept = sig("x_kept", 4)
    x_turned = sig("x_turned", 4)
    xT_ready = sig("xT_ready")
    kT_made = sig("kT_made")
    qv_made = sig("qv_made")
    q_copied = sig("q_copied")
    qv_taken = sig("qv_taken")
    qS_ready = sig("qS_ready")
    k_taken = sig("k_taken")
    k_turned = sig("k_turned")
    ks_ready = sig("ks_ready")
    s_made = sig("s_made")
    s_taken = sig("s_taken", 4)
    r_made = sig("r_made", 4)
    r_taken = sig("r_taken")
    upd_made = sig("upd_made")
    state_ready = sig("state_ready")
    g_made = sig("g_made")
    g_taken = sig("g_taken")
    pkv_ready = sig("pkv_ready")
    cleared = sig("cleared")
    yT_ready = sig("yT_ready")
    square_done = sig("square_done")
    back_made, back_taken = sig("back_made"), sig("back_taken", 4)
    affine = sig("affine")
    gvar_ready = sig("gvar_ready")
    grstd_ready = sig("grstd_ready")
    mv_ready = sig("mv_ready")
    rstd_ready = sig("rstd_ready")
    pool_step = sig("pool_step")
    dve_step = sig("dve_step")

    x_rows = a["L0_attn_x"].rearrange("b (t p) d -> (b t) p d", p=P)

    nc.all_engine_barrier()
    block = ctx.enter_context(nc.Block())

    @block.sync
    def _(sp):
        with sp.Fori(0, BATCH) as b:
            for t in range(TPB):
                sp.wait_ge(x_turned.sem, x_turned.after(b * TPB + (t + 1 - 4)))
                sp.wait_ge(x_kept.sem, x_kept.after(b * TPB + (t + 1 - 4)))
                sp.dma_start(xin[t][:, :], x_rows[bass.ds(b * TPB + t, 1), :, :].rearrange("a p d -> (a p) d"))\
                    .then_inc(x_in[t].sem, 16)

    @block.gpsimd
    def _(pool):

        def group_pow(b):
            pool.wait_ge(gvar_ready.sem, gvar_ready.after(b + 1))
            rstd_of(pool, steps, gsum[:, 3:4], gsum[:, 2:3], LN_EPS, net).then_inc(grstd_ready.sem, 1)

        def row_pow(b, t):
            i = b * TPB + t
            pool.wait_ge(mv_ready.sem, mv_ready.after(i + 1))
            rstd_of(pool, steps, rstd[:, t:t + 1], mv[:, t, 1:2], LN_EPS, net).then_inc(rstd_ready.sem, 1)

        def keep(b, t):
            pool.wait_ge(x_in[t].sem, x_in[t].after((b + 1) * 16))
            pool.tensor_copy(net.x_res[:, bass.ds(b * TPB + t, 1), :].rearrange("p a d -> p (a d)"), xin[t][:, :])\
                .then_inc(x_kept.sem, 1)

        def decay_queries(b, t):
            i = b * TPB + t
            pool.wait_ge(q_copied.sem, q_copied.after(i + 1))
            pool.wait_ge(r_made.sem, r_made.after(i + 1 - TPB))
            pool.tensor_tensor(qS[t][:, :, :], qT[t][:, :, :], net.table["qdecay"].rearrange("p (k t) -> p k t", k=KD),
                               ALU.mult).then_inc(qS_ready.sem, 1)

        steps = Steps(pool_step.sem)
        for i in range(TPB):
            pool.memset(vE[i][:, :], 0.0)
            ins = pool.memset(vO[i][:, :], 0.0)
        ins.then_inc(cleared.sem, 1)
        for t in range(TPB):
            keep(0, t)
            decay_queries(0, t)
        with pool.Fori(1, BATCH) as b:
            steps.enter(b - 1, 5)
            for t in range(TPB):
                keep(b, t)
                decay_queries(b, t)
                if t == 1:
                    group_pow(b - 1)
            for t in range(TPB):
                row_pow(b - 1, t)
            steps.leave(BATCH - 1)
        group_pow(BATCH - 1)
        for t in range(TPB):
            row_pow(BATCH - 1, t)

    @block.scalar
    def _(act):
        def turn(b, t):
            act.wait_ge(x_turned.sem, x_turned.after(b * TPB + t + 1))
            nc.scalar.activation(xT[t % 2][:, :, :], pX.rearrange("p (k t) -> p k t", k=KD), ACT.Copy)\
                .then_inc(xT_ready.sem, 1)

        def take(b, t):
            i = b * TPB + t
            act.wait_ge(qv_made.sem, qv_made.after(i + 1))
            act.wait_ge(r_made.sem, r_made.after(i + 1 - TPB))
            nc.scalar.activation(qT[t][:, :, :], pQ, ACT.Copy).then_inc(q_copied.sem, 1)
            nc.scalar.activation(qE[t][:, :, :], pQ, ACT.Copy, scale=net.table["even"])
            nc.scalar.activation(qO[t][:, :, :], pQ, ACT.Copy, scale=net.table["odd"])
            heads = pV.rearrange("p (g two e) -> p g two e", two=2, e=HD)
            for odd, half in enumerate((vE, vO)):
                nc.scalar.activation(half[t][:, :].rearrange("p (g two e) -> p g two e", two=2, e=HD)[:, :, odd, :],
                                     heads[:, :, odd, :], ACT.Copy)
            nc.scalar.activation(v[t][:, :], pV, ACT.Copy).then_inc(qv_taken.sem, 1)

        def result(b, t):
            i = b * TPB + t
            act.wait_ge(r_made.sem, r_made.after(i + 1))
            if t == 0 and (not isinstance(b, int) or b):
                act.wait_ge(g_made.sem, g_made.after(b))
                act.wait_ge(yT_ready.sem, yT_ready.after(b))
            for k in range(KD):
                nc.scalar.activation(rT[:, k, t * P:(t + 1) * P], pR[:, k, :], ACT.Copy, accum_out=gst[:, 0, t, k:k + 1])
                if k or t or not isinstance(b, int) or b:
                    act.wait_ge(square_done.sem, square_done.after(KD * i + k))
                ins = nc.scalar.activation(square[:, :], pR[:, k, :], ACT.Square, accum_out=gst[:, 1, t, k:k + 1])
                ins.then_inc(square_done.sem, 1)
            act.wait_ge(square_done.sem, square_done.after(KD * (i + 1)))
            act.sem_inc(r_taken.sem, 1)

        def normed(b):
            act.wait_ge(affine.sem, affine.after(b + 1))
            if not isinstance(b, int) or b:
                act.wait_ge(back_made.sem, back_made.after(TPB * b))
            for k in range(KD):
                ins = nc.scalar.activation(yT[:, k, :], rT[:, k, :], ACT.Identity, bias=gaff[:, 1, k:k + 1], scale=gaff[:, 0, k:k + 1])
            ins.then_inc(yT_ready.sem, 1)

        def batch(b, before):
            turn(b, 0)
            turn(b, 1)
            take(b, 0)
            for t in range(TPB):
                if t + 2 < TPB:
                    turn(b, t + 2)
                if t + 1 < TPB:
                    take(b, t + 1)
                if t == 1 and before:
                    normed(b - 1)
                if t:
                    result(b, t - 1)
                elif before:
                    result(b - 1, TPB - 1)

        act.wait_ge(cleared.sem, cleared.after(1))
        batch(0, False)
        with act.Fori(1, BATCH) as b:
            batch(b, True)
        result(BATCH - 1, TPB - 1)
        normed(BATCH - 1)

    @block.tensor
    def _(pe):
        pe.wait_ge(w_in.sem, w_in.after(32))

        def turn(b, t):
            i = b * TPB + t
            pe.wait_ge(x_in[t].sem, x_in[t].after((b + 1) * 16))
            if t:
                pe.wait_ge(xT_ready.sem, xT_ready.after(i))
            if t == 3:
                pe.wait_ge(r_taken.sem, r_taken.after(i - 3))
            elif t == 0 and not isinstance(b, int):
                pe.wait_ge(r_taken.sem, r_taken.after(i - 1))
            for k in range(KD):
                mm = pe.transpose(pX[:, k * P:(k + 1) * P], xin[t][:, k * P:(k + 1) * P], net.table["ident"])
            mm.then_inc(x_turned.sem, 1)

        def project(b, t):
            i = b * TPB + t
            first = isinstance(b, int) and t == 0
            pe.wait_ge(xT_ready.sem, xT_ready.after(i + 1))
            if not first:
                pe.wait_ge(qv_taken.sem, qv_taken.after(i))
            for m in range(2):
                for k in range(KD):
                    pe.matmul(pQ[:, m, :], w[:, k, m * P:(m + 1) * P], xT[t % 2][:, k, :],
                              start=(k == 0), stop=(k == KD - 1))
            for k in range(KD):
                mm = pe.matmul(pV, xT[t % 2][:, k, :], w[:, k, 2 * DIM:], start=(k == 0), stop=(k == KD - 1))
            mm.then_inc(qv_made.sem, 1)
            if not first:
                pe.wait_ge(k_taken.sem, k_taken.after(i))
                pe.wait_ge(ks_ready.sem, ks_ready.after(i if t == 0 else i - 1)) if (t != 1 or not isinstance(b, int)) else None
            for m in range(2):
                for k in range(KD):
                    mm = pe.matmul(pKT[:, m, :], w[:, k, DIM + m * P:DIM + (m + 1) * P], xT[t % 2][:, k, :],
                                   start=(k == 0), stop=(k == KD - 1))
            mm.then_inc(kT_made.sem, 1)

        def scores_of(b, t, r, before):
            i = b * TPB + t
            if r == 0:
                pe.wait_ge(qv_taken.sem, qv_taken.after(i + 1))
                pe.wait_ge(k_taken.sem, k_taken.after(i + 1))
            pe.wait_ge(s_taken.sem, s_taken.after(4 * i + (r + 1 - 4)))
            if r >= 2 and before and t in (0, TPB - 1):
                pe.wait_ge(back_taken.sem, back_taken.after((b - 2) * TPB + r + 1 if t == 0 else (b - 1) * TPB + r - 1))
            rows = slice(32 * r, 32 * r + 32)
            for g in range(4):
                half, q = g // 2, (qE, qO)[g % 2][t]
                mm = pe.matmul(pS[r][:, g, :], kT[t % 2][rows, half, :], q[rows, half, :], start=True, stop=True)
            mm.then_inc(s_made.sem, 1)

        def turn_keys(b, t):
            i = b * TPB + t
            pe.wait_ge(k_taken.sem, k_taken.after(i + (2 if t < TPB - 1 else 1)))
            for k in range(KD):
                mm = pe.transpose(pK[:, k * P:(k + 1) * P], kT[t % 2][:, k, :], net.table["ident"])
            mm.then_inc(k_turned.sem, 1)

        def carry_in(b, t, turned):
            i = b * TPB + t
            pe.wait_ge(xT_ready.sem, xT_ready.after(turned))
            if t or not isinstance(b, int) or b:
                pe.wait_ge(r_taken.sem, r_taken.after(i))
            if t == 0:
                pe.wait_ge(pkv_ready.sem, pkv_ready.after(1))
            for half in range(KD):
                pe.matmul(pR[:, half, :], pkv[:, half, :], qT[t][:, half, :],
                          start=(half == 0), stop=False, skip_group_check=True)
            if t:
                pe.wait_ge(state_ready.sem, state_ready.after(b * (TPB - 1) + t))
                pe.wait_ge(qS_ready.sem, qS_ready.after(i + 1))
                for half in range(KD):
                    pe.matmul(pR[:, half, :], state[t % 2][:, half, :], qS[t][:, half, :],
                              start=False, stop=False, skip_group_check=True)

        def mix_of(b, t, r):
            i = b * TPB + t
            pe.wait_ge(s_taken.sem, s_taken.after(4 * i + r + 1))
            for g in range(4):
                half, rows = g // 2, slice(32 * r, 32 * r + 32)
                cols = slice(half * P + 32 * r, half * P + 32 * r + 32)
                mm = pe.matmul(pR[rows, half, :], (vE, vO)[g % 2][t][:, cols], prob[t % 2][:, r, g, :],
                               start=False, stop=(r == 3 and g == 3), skip_group_check=True)
            if r == 3:
                mm.then_inc(r_made.sem, 1)

        def update(b, t):
            i = b * TPB + t
            if t < TPB - 1:
                pe.wait_ge(ks_ready.sem, ks_ready.after(i + 1))
                if t == 0 and not isinstance(b, int):
                    pe.wait_ge(g_taken.sem, g_taken.after(b))
                for half in range(KD):
                    cols = slice(half * P, (half + 1) * P)
                    mm = pe.matmul(pU[:, cols], ks[t % 2][:, cols], v[t][:, cols], start=True, stop=True)
                mm.then_inc(upd_made.sem, 1)

        def totals(b):
            pe.wait_ge(r_taken.sem, r_taken.after((b + 1) * TPB))
            pe.wait_ge(state_ready.sem, state_ready.after((b + 1) * (TPB - 1)))
            pe.matmul(pG, net.table["ones"], gst[:, :, :, :].rearrange("p s t k -> p (s t k)"), start=True, stop=True)\
                .then_inc(g_made.sem, 1)

        def turn_back(b, t, scores_done):
            pe.wait_ge(yT_ready.sem, yT_ready.after(b + 1))
            pe.wait_ge(s_taken.sem, s_taken.after(scores_done))
            pe.wait_ge(back_taken.sem, back_taken.after(b * TPB + t - 1))
            for k in range(KD):
                mm = pe.transpose(pB[t % 2][:, k * P:(k + 1) * P], yT[:, k, t * P:(t + 1) * P], net.table["ident"])
            mm.then_inc(back_made.sem, 1)

        def batch(b, before):
            turn(b, 0)
            turn(b, 1)
            project(b, 0)
            for t in range(TPB):
                if t + 2 < TPB:
                    turn(b, t + 2)
                if t + 1 < TPB:
                    project(b, t + 1)
                if t == 1 and before:
                    totals(b - 1)
                last = (b, t - 1) if t else (b - 1, TPB - 1) if before else None
                if last:
                    carry_in(*last, b * TPB + min(t + 3, TPB))
                for r in range(4):
                    scores_of(b, t, r, before)
                    if last:
                        mix_of(*last, r)
                if t:
                    update(b, t - 1)
                turn_keys(b, t)
                if t >= 2 and before:
                    for j in (2 * t - 4, 2 * t - 3):
                        turn_back(b - 1, j, 4 * (b * TPB + t + 1))

        batch(0, False)
        with pe.Fori(1, BATCH) as b:
            batch(b, True)
        carry_in(BATCH - 1, TPB - 1, TILES)
        for r in range(4):
            mix_of(BATCH - 1, TPB - 1, r)
        totals(BATCH - 1)
        for t in range(TPB):
            turn_back(BATCH - 1, t, 4 * TILES)

    @block.vector
    def _(dve):
        steps = Steps(dve_step.sem)
        dve.wait_ge(w_in.sem, w_in.after(32))
        blk = net.table["block"].rearrange("p (h e) -> p h e", e=HD)
        for half in range(KD):
            ins = dve.scalar_tensor_tensor(out=pkv[:, half, :].rearrange("p (h e) -> p h e", e=HD),
                                           in0=pkv_raw[:, half:half + 1, :].broadcast_to([P, HPK, HD]),
                                           scalar=float(HEADS * HD), in1=blk, op0=ALU.mult, op1=ALU.mult)
        ins.then_inc(pkv_ready.sem, 1)

        def take(b, t):
            i = b * TPB + t
            dve.wait_ge(kT_made.sem, kT_made.after(i + 1))
            dve.tensor_copy(kT[t % 2][:, :, :], pKT).then_inc(k_taken.sem, 1)

        def decay(b, t):
            i = b * TPB + t
            dec = net.table["decay"].rearrange("p (r g t) -> p r g t", r=4, g=4)
            for r in range(4):
                dve.wait_ge(s_made.sem, s_made.after(4 * i + r + 1))
                if r == 0:
                    dve.wait_ge(r_made.sem, r_made.after(i + 1 - 2))
                dve.tensor_tensor(prob[t % 2][:, r, :, :], pS[r][:, :, :], dec[:, r, :, :], ALU.mult)\
                    .then_inc(s_taken.sem, 1)

        def keys(b, t):
            i = b * TPB + t
            dve.wait_ge(k_turned.sem, k_turned.after(i + 1))
            if t >= 2:
                dve.wait_ge(upd_made.sem, upd_made.after(b * (TPB - 1) + t - 1))
            elif not isinstance(b, int):
                dve.wait_ge(upd_made.sem, upd_made.after(b * (TPB - 1)))
            dve.tensor_tensor(ks[t % 2][:, :], pK, net.table["kdecay"], ALU.mult).then_inc(ks_ready.sem, 1)

        def carry(b, t):
            n = b * (TPB - 1) + t + 1
            dve.wait_ge(upd_made.sem, upd_made.after(n))
            new = state[(t + 1) % 2]
            pu = pU.rearrange("p (k n) -> p k n", k=KD)
            blk2 = net.table["block"].rearrange("p (a n) -> p a n", a=1).broadcast_to([P, KD, P])
            if t == 0:
                dve.tensor_tensor(new[:, :, :], pu, blk2, ALU.mult).then_inc(state_ready.sem, 1)
            else:
                dve.tensor_tensor(upd[:, :, :], pu, blk2, ALU.mult).then_inc(steps.sem, 1)
                dve.wait_ge(steps.sem, steps.done(1))
                dve.wait_ge(state_ready.sem, state_ready.after(n - 1))
                for half in range(KD):
                    ins = dve.scalar_tensor_tensor(out=new[:, half, :], in0=state[t % 2][:, half, :],
                                                   scalar=net.table["tiledecay"][:, half:half + 1], in1=upd[:, half, :],
                                                   op0=ALU.mult, op1=ALU.add)
                ins.then_inc(state_ready.sem, 1)

        mean, ex2, var, rs = (gsum[:, j:j + 1] for j in range(4))
        scale, shift, tmp = (gaff[:, j, :] for j in range(3))

        def group_var(b):
            dve.wait_ge(g_made.sem, g_made.after(b + 1))
            dve.tensor_reduce(gsum[:, 0:2], pG.rearrange("p (s n) -> p s n", s=2), AX.X, ALU.add).then_inc(steps.sem, 1)
            dve.wait_ge(steps.sem, steps.done(1))
            dve.sem_inc(g_taken.sem, 1)
            dve.tensor_scalar(gsum[:, 0:2], gsum[:, 0:2], 1.0 / (SEQ * DIM), None, ALU.mult).then_inc(steps.sem, 1)
            dve.wait_ge(steps.sem, steps.done(1))
            dve.tensor_tensor(var, mean, mean, ALU.mult).then_inc(steps.sem, 1)
            dve.wait_ge(steps.sem, steps.done(1))
            dve.tensor_tensor(var, ex2, var, ALU.subtract).then_inc(gvar_ready.sem, 1)

        def group_affine(b):
            dve.wait_ge(grstd_ready.sem, grstd_ready.after(b + 1))
            if not isinstance(b, int) or b:
                dve.wait_ge(yT_ready.sem, yT_ready.after(b))
            dve.wait_ge(gn_in.sem, gn_in.after(16 * 2 * HPK))
            dve.tensor_scalar(scale, gnw[:, :], rs, None, ALU.mult).then_inc(steps.sem, 1)
            dve.wait_ge(steps.sem, steps.done(1))
            dve.tensor_scalar(tmp, scale, mean, None, ALU.mult).then_inc(steps.sem, 1)
            dve.wait_ge(steps.sem, steps.done(1))
            dve.tensor_tensor(shift, gnb[:, :], tmp, ALU.subtract).then_inc(affine.sem, 1)

        def flat(i):
            return net.x_res[:, bass.ds(i, 1), :].rearrange("p a d -> p (a d)")

        def add_rows(b, t):
            i = b * TPB + t
            dve.wait_ge(back_made.sem, back_made.after(i + 1))
            dve.wait_ge(x_kept.sem, x_kept.after(i + 1))
            dve.tensor_tensor(y1[t][:, :], pB[t % 2], flat(i), ALU.add).then_inc(back_taken.sem, 1)
            dve.wait_ge(back_taken.sem, back_taken.after(i + 1))
            dve.bn_stats(bst[:, t, :], y1[t][:, :]).then_inc(steps.sem, 1)
            dve.wait_ge(steps.sem, steps.done(1))
            dve.sem_inc(net.passed, 1)
            dve.bn_aggr(mv[:, t, :], bst[:, t, :]).then_inc(mv_ready.sem, 1)

        def norm_rows(b, t):
            i = b * TPB + t
            dve.wait_ge(rstd_ready.sem, rstd_ready.after(i + 1))
            dve.tensor_scalar(flat(i), y1[t][:, :], mv[:, t, 0:1], rstd[:, t:t + 1], ALU.subtract, ALU.mult)

        def batch(b, before):
            take(b, 0)
            for t in range(TPB):
                if t + 1 < TPB:
                    take(b, t + 1)
                if t == 1 and before:
                    group_var(b - 1)
                decay(b, t)
                if t == 1 and before:
                    group_affine(b - 1)
                if t:
                    carry(b, t - 1)
                keys(b, t)
                if t >= 2 and before:
                    for j in (2 * t - 4, 2 * t - 3):
                        add_rows(b - 1, j)
                        if j:
                            norm_rows(b - 1, j - 1)
            if before:
                norm_rows(b - 1, TPB - 1)

        batch(0, False)
        with dve.Fori(1, BATCH) as b:
            steps.enter(b - 1, 2 + 3 + 2 + 4)
            batch(b, True)
            steps.leave(BATCH - 1)
        group_var(BATCH - 1)
        group_affine(BATCH - 1)
        for t in range(TPB):
            add_rows(BATCH - 1, t)
            if t:
                norm_rows(BATCH - 1, t - 1)
        norm_rows(BATCH - 1, TPB - 1)


def rstd_of(pool, steps, out, var, eps, net, scale=1.0):
    pool.sem_inc(net.passed_pool, 1)
    pool.tensor_scalar(out, var, scale, eps, ALU.mult, ALU.add).then_inc(steps.sem, 1)
    pool.wait_ge(steps.sem, steps.done(1))
    return pool.tensor_tensor(out, out, net.table["minushalf"][:, 0:out.shape[1]], ALU.pow)


def batches(eng, body, steps=None, per=0):
    body(0, 0, False, True)
    with eng.Fori(0, BATCH // 2 - 1) as i:
        if steps:
            steps.enter(i, 2 * per)
        for p in range(2):
            body(2 * i + 1 + p, 1 - p, True, True)
        if steps:
            steps.leave(BATCH // 2 - 1)
    body(BATCH - 1, 1, True, False)


def tile_of(net, i):
    return net.x_res[:, bass.ds(i, 1), :].rearrange("p a d -> p (a d)")


class Phase:

    def __init__(self, net, ctx, prefix):
        self.net, self.ctx, self.prefix = net, ctx, prefix

    def sb(self, name, shape, dt=F32):
        return self.ctx.enter_context(self.net.nc.sbuf_tensor(f"{self.prefix}_{name}", shape, dt))

    def ps(self, name, shape):
        return self.ctx.enter_context(self.net.nc.psum_tensor(f"{self.prefix}_{name}", shape, F32))

    def sig(self, name, head=0):
        return Signal(self.net, self.ctx, f"{self.prefix}_{name}", head)


def prepare(net, ctx):
    nc, a = net.nc, net.args
    ph = Phase(net, ctx, "w")
    raw_fc = ph.sb("raw_fc", [P, NH, DIM])
    raw_pj = ph.sb("raw_pj", [P, KD, HID])
    neg = ph.sb("neg", [P, 2, NH * DIM])
    sq = [ph.sb(f"sq{i}", [P, KD, DIM]) for i in range(5)]
    absum, thr = ph.sb("absum", [P, 2]), ph.sb("thr", [P, 2, 2])
    pT = [ph.ps(f"pT{i}", [P, 4, P]) for i in range(2)]
    pQ = [ph.ps(f"pQ{i}", [P, 4, P]) for i in range(2)]
    pM = ph.ps("pM", [P, 2])
    pU = [ph.ps(f"pU{i}", [P, DIM]) for i in range(2)]
    tern, full = ph.sb("tern", [P, NH, DIM]), ph.sb("full", [P, NH, DIM + 2])
    lnw, lnb, b_cols = ph.sb("lnw", [P, NH]), ph.sb("lnb", [P, NH]), ph.sb("b_cols", [P, NH, P])
    ln_in, full_ready, u_made = (ph.sig(n) for n in ("ln_in", "full_ready", "u_made"))
    c_in, c0_in, fc_in, pj_in, sq_in = (ph.sig(n) for n in ("c_in", "c0_in", "fc_in", "pj_in", "sq_in"))
    taken_act = ph.sig("taken_act")
    sums, total, quant, turned, taken, step = (ph.sig(n) for n in ("sums", "total", "quant", "turned", "taken", "step"))

    banks = []
    for n in range(5):
        dst = net.wqkvT[:, :, n * DIM:(n + 1) * DIM] if n < 3 else (net.w1T, net.w2T)[n - 3][:, :, :]
        banks.append(([(sq[n], m, k) for k in range(KD) for m in range(KD)], dst))
    SQUARES = len(banks)
    for k in range(KD):
        for c in range(0, NH, 4):
            banks.append(([(raw_fc, c + j, k) for j in range(4)], net.wfcT[:, k, c * P:(c + 4) * P]))
    for c in range(0, NH, 2):
        banks.append(([(raw_pj, m, c + j) for j in range(2) for m in range(KD)],
                      tern[:, c:c + 2, :].rearrange("p c n -> p (c n)")))

    def bank_of(n):
        return (pQ if n < SQUARES else pT)[n % 2][:, :, :]

    def shaped(src, dst):
        if len(dst.shape) == 3:
            return src.rearrange("p (k m) n -> p k (m n)", k=KD)
        return src.rearrange("p k n -> p (k n)")

    nc.all_engine_barrier()
    block = ctx.enter_context(nc.Block())

    @block.sync
    def _(sp):
        sp.dma_start(raw_fc[:, :, :], a["L0_ffn_W_fc"].rearrange("(c p) n -> p c n", p=P)).then_inc(fc_in.sem, 16)
        sp.dma_start(raw_pj[:, :, :], a["L0_ffn_W_proj"].rearrange("(c p) n -> p c n", p=P)).then_inc(pj_in.sem, 16)
        sp.dma_start(net.const[:, :], a["consts"]).then_inc(c_in.sem, 16)
        for n, name in enumerate(("Wq", "Wk", "Wv", "W1", "W2")):
            sp.dma_start(sq[n][:, :, :], a["L1_attn_" + name].rearrange("(c p) n -> p c n", p=P)).then_inc(sq_in.sem, 16)
        with nc.allow_non_contiguous_dma(reason="2 x 4 KB, once"):
            for t, name in ((lnw, "L0_ffn_ln_w"), (lnb, "L0_ffn_ln_b")):
                sp.dma_start(t[:, :], a[name].rearrange("(c p) -> p c", p=P)).then_inc(ln_in.sem, 16)
        sp.dma_start(net.const0[:, :], a["consts0"]).then_inc(c0_in.sem, 16)
        sp.dma_start(net.w[:, :, :], a["L0_attn_W_qkv"].rearrange("(k p) n -> p k n", p=P)).then_inc(net.w0_in.sem, 16)
        sp.dma_start(net.pkv_raw[:, :, :], a["L0_attn_past_kv"].rearrange("(k h) d e -> (h d) k e", k=KD)).then_inc(net.w0_in.sem, 16)
        for dst, src in ((net.gnw, "L0_attn_gn_weight"), (net.gnb, "L0_attn_gn_bias")):
            with nc.allow_non_contiguous_dma(reason="1 KB, once"):
                for h in range(HPK):
                    sp.dma_start(dst[h * HD:(h + 1) * HD, :], a[src].rearrange("(k h) -> h k", k=KD)[h:h + 1, :].broadcast_to([HD, KD]))\
                        .then_inc(net.gn_in.sem, 16)
        sp.wait_ge(c0_in.sem, c0_in.after(16))

    @block.scalar
    def _(act):
        for n in range(SQUARES):
            dst = banks[n][1]
            act.wait_ge(turned.sem, turned.after(n + 1))
            nc.scalar.activation(dst, shaped(bank_of(n), dst), ACT.Copy).then_inc(taken_act.sem, 1)

    @block.vector
    def _(dve):
        steps = Steps(step.sem)
        dve.wait_ge(fc_in.sem, fc_in.after(16))
        dve.tensor_reduce(absum[:, 0:1], raw_fc[:, :, :].rearrange("p c n -> p (c n)"), AX.X, ALU.add,
                          apply_absolute_value=True)
        dve.wait_ge(pj_in.sem, pj_in.after(16))
        dve.tensor_reduce(absum[:, 1:2], raw_pj[:, :, :].rearrange("p c n -> p (c n)"), AX.X, ALU.add,
                          apply_absolute_value=True).then_inc(sums.sem, 1)
        dve.wait_ge(total.sem, total.after(1))
        n = float(HID * DIM)
        dve.tensor_scalar(thr[:, 0, :], pM[:, :], 1.0 / n, ABS_EPS, ALU.mult, ALU.add).then_inc(steps.sem, 1)
        dve.wait_ge(steps.sem, steps.done(1))
        dve.tensor_scalar(thr[:, 0, :], thr[:, 0, :], 0.5, None, ALU.mult).then_inc(steps.sem, 1)
        dve.wait_ge(steps.sem, steps.done(1))
        dve.tensor_scalar(thr[:, 1, :], thr[:, 0, :], -1.0, None, ALU.mult).then_inc(steps.sem, 1)
        dve.wait_ge(steps.sem, steps.done(1))
        for j, raw in enumerate((raw_fc, raw_pj)):
            flat = raw[:, :, :].rearrange("p c n -> p (c n)")
            dve.tensor_scalar(neg[:, j, :], flat, thr[:, 1, j:j + 1], -1.0, ALU.is_lt, ALU.mult).then_inc(steps.sem, 1)
            dve.wait_ge(steps.sem, steps.done(1))
            dve.scalar_tensor_tensor(out=flat, in0=flat, scalar=thr[:, 0, j:j + 1], in1=neg[:, j, :],
                                     op0=ALU.is_gt, op1=ALU.add).then_inc(quant.sem, 1)
        dve.wait_ge(c_in.sem, c_in.after(16))
        for n in range(SQUARES, len(banks)):
            dst = banks[n][1]
            dve.wait_ge(turned.sem, turned.after(n + 1))
            dve.tensor_copy(dst, shaped(bank_of(n), dst)).then_inc(taken.sem, 1)
        dve.wait_ge(ln_in.sem, ln_in.after(32))
        dve.wait_ge(taken.sem, taken.after(len(banks) - SQUARES))
        dve.memset(full[:, :, DIM:DIM + 2], 1.0)
        for c in range(NH):
            dve.tensor_scalar(full[:, c, 0:DIM], tern[:, c, :], lnw[:, c:c + 1], None, ALU.mult)
            ins = dve.tensor_scalar(b_cols[:, c, :], net.table["ones"], lnb[:, c:c + 1], None, ALU.mult)
        ins.then_inc(full_ready.sem, 1)
        dve.wait_ge(full_ready.sem, full_ready.after(1))
        dve.tensor_copy(net.wpjH[:, :, :], full[:, :, :]).then_inc(steps.sem, 1)
        dve.wait_ge(steps.sem, steps.done(1))
        dve.tensor_tensor(net.wpjL[:, :, :], full[:, :, :], net.wpjH[:, :, :], ALU.subtract)
        dve.wait_ge(u_made.sem, u_made.after(1))
        dve.tensor_copy(net.u0[:, :], pU[0][:, :])
        dve.tensor_copy(net.u1[:, :], pU[1][:, :])

    @block.tensor
    def _(pe):
        pe.wait_ge(c_in.sem, c_in.after(16))
        pe.wait_ge(sums.sem, sums.after(1))
        pe.matmul(pM[:, :], net.table["ones"], absum[:, :], start=True, stop=True).then_inc(total.sem, 1)
        for n, (blocks, _) in enumerate(banks):
            if n >= SQUARES + 2:
                pe.wait_ge(taken.sem, taken.after(n - SQUARES - 1))
            elif 2 <= n < SQUARES:
                pe.wait_ge(taken_act.sem, taken_act.after(n - 1))
            if blocks[0][0] is raw_fc:
                pe.wait_ge(quant.sem, quant.after(1))
            elif blocks[0][0] is raw_pj:
                pe.wait_ge(quant.sem, quant.after(2))
            else:
                pe.wait_ge(sq_in.sem, sq_in.after(80))
            for j, (src, row, col) in enumerate(blocks):
                mm = pe.transpose(bank_of(n)[:, j, :], src[:, row, col * P:(col + 1) * P], net.table["ident"])
            mm.then_inc(turned.sem, 1)
        pe.wait_ge(full_ready.sem, full_ready.after(1))
        for c in range(NH):
            pe.matmul(pU[0][:, :], b_cols[:, c, :], tern[:, c, :], start=(c == 0), stop=(c == NH - 1))
            mm = pe.matmul(pU[1][:, :], net.table["ones"], full[:, c, 0:DIM], start=(c == 0), stop=(c == NH - 1))
        mm.then_inc(u_made.sem, 1)


def ternary_ffn(net, ctx):
    nc = net.nc
    ph = Phase(net, ctx, "f")
    two, four = range(2), range(4)
    xs = ph.sb("xs", [P, TPB, DIM])
    xh, xl = ([ph.sb(f"{n}{i}", [P, KD, SEQ], F32R) for i in two] for n in ("xh", "xl"))
    g = [ph.sb(f"g{i}", [P, SEQ]) for i in four]
    gh, gl = ([ph.sb(f"{n}{i}", [P, SEQ], F32R) for i in four] for n in ("gh", "gl"))
    g2 = [ph.sb(f"g2{i}", [P, SEQ]) for i in two]
    acc = [ph.sb(f"acc{i}", [P, SEQ]) for i in two]
    y, xb = ph.sb("y", [P, TPB, DIM]), ph.sb("xb", [P, TPB, DIM])
    negmean, meansq, var, rs = (ph.sb(n, [P, TPB]) for n in ("negmean", "meansq", "var", "rs"))
    yst, ymv, yrs = ph.sb("yst", [P, TPB, 6]), ph.sb("ymv", [P, TPB, 2]), ph.sb("yrs", [P, TPB])
    pX = ph.ps("pX", [P, SEQ])
    pH = [ph.ps(f"pH{i}", [P, SEQ]) for i in two]
    pY = ph.ps("pY", [P, TPB, 512])
    pS = ph.ps("pS", [P, TPB])
    x_copied, turned, xh_ready, xl_ready = (ph.sig(n) for n in ("x_copied", "turned", "xh_ready", "xl_ready"))
    up_made, squared, s_made = ph.sig("up_made"), ph.sig("squared"), ph.sig("s_made", 2)
    gelued, split, down_made, added = ph.sig("gelued", 2), ph.sig("split", 4), ph.sig("down_made", 4), ph.sig("added", 2)
    y_taken, var_ready, rs_ready, xb_ready = ph.sig("y_taken", TPB), ph.sig("var_ready"), ph.sig("rs_ready"), ph.sig("xb_ready")
    rows_ready, yrs_ready, step, pool_step = ph.sig("rows_ready", 1), ph.sig("yrs_ready"), ph.sig("step"), ph.sig("pool_step")

    nc.all_engine_barrier()
    block = ctx.enter_context(nc.Block())

    @block.gpsimd
    def _(pool):
        steps = Steps(pool_step.sem)

        def base(b):

            pool.wait_ge(rows_ready.sem, rows_ready.after(b))
            pool.sem_inc(net.passed_pool, 1)
            pool.tensor_tensor(xb[:, :, :], net.x_res[:, bass.ds(b * TPB, TPB), :],
                               net.u0[:, :].rearrange("p (a d) -> p a d", a=1).broadcast_to([P, TPB, DIM]), ALU.add)\
                .then_inc(xb_ready.sem, 1)

        def inner(b):
            pool.wait_ge(var_ready.sem, var_ready.after(b + 1))
            rstd_of(pool, steps, rs[:, :], var[:, :], LN_EPS, net).then_inc(rs_ready.sem, 1)

        def outer(b):
            pool.wait_ge(rows_ready.sem, rows_ready.after(b + 1))
            rstd_of(pool, steps, yrs[:, :], ymv[:, :, 1], LN_EPS, net).then_inc(yrs_ready.sem, 1)

        def add(b, p, c):
            pool.wait_ge(squared.sem, squared.after(8 * b + c + 1))
            if c == 1:
                pool.wait_ge(s_made.sem, s_made.after(b + 1 - 2))
                pool.tensor_tensor(acc[p][:, :], g2[0][:, :], g2[1][:, :], ALU.add).then_inc(added.sem, 1)
            else:
                pool.wait_ge(added.sem, added.after((NH - 1) * b + c - 1))
                pool.tensor_tensor(acc[p][:, :], acc[p][:, :], g2[c % 2][:, :], ALU.add).then_inc(added.sem, 1)

        def body(b, p, before, behind):
            if before:
                base(b - 1)
            for c in range(1, NH):
                if c == 7 and before:
                    outer(b - 1)
                add(b, p, c)
                if c == 1 and before:
                    inner(b - 1)

        batches(pool, body, steps, 2)
        base(BATCH - 1)
        inner(BATCH - 1)
        outer(BATCH - 1)

    @block.scalar
    def _(act):

        def copy(b):
            for t in range(TPB):
                ins = nc.scalar.activation(xs[:, t, :], tile_of(net, b * TPB + t), ACT.Copy)
            ins.then_inc(x_copied.sem, 1)

        def take(b, p, k):
            act.wait_ge(turned.sem, turned.after(2 * b + k + 1))
            nc.scalar.activation(xh[p][:, k, :], pX[:, :], ACT.Copy).then_inc(xh_ready.sem, 1)

        def gelu(b, c):
            n = NH * b + c
            act.wait_ge(up_made.sem, up_made.after(n + 1))
            act.wait_ge(split.sem, split.after(n + 1 - 4))
            nc.scalar.activation(g[c % 4][:, :], pH[c % 2][:, :], ACT.Gelu).then_inc(gelued.sem, 1)

        def square(b, c):
            n = NH * b + c
            act.wait_ge(gelued.sem, gelued.after(n + 1))
            act.wait_ge(added.sem, added.after((NH - 1) * b + (c - 1 if c < 2 else max(c - 2, 1))))
            nc.scalar.activation(g2[c % 2][:, :], g[c % 4][:, :], ACT.Square).then_inc(squared.sem, 1)

        def body(b, p, before, behind):
            for c in range(NH):
                gelu(b, c)
                if c or before:
                    square(b if c else b - 1, (c - 1) % NH)
                if behind:
                    if c == 0:
                        act.sem_inc(net.passed_act, 1)
                        copy(b + 1)
                    if c in (4, 6):
                        take(b + 1, 1 - p, (c - 4) // 2)

        copy(0)
        for k in range(KD):
            take(0, 0, k)
        batches(act, body)
        square(BATCH - 1, NH - 1)

    @block.tensor
    def _(pe):

        def turn(b, p, k):
            pe.wait_ge(x_copied.sem, x_copied.after(b + 1))
            if not isinstance(b, int) or b or k:
                pe.wait_ge(xl_ready.sem, xl_ready.after(2 * b + k))
            for t in range(TPB):
                mm = pe.transpose(pX[:, t * P:(t + 1) * P], xs[:, t, k * P:(k + 1) * P], net.table["ident"])
            mm.then_inc(turned.sem, 1)

        def up(b, p, c):
            n = NH * b + c
            if c == 0:
                pe.wait_ge(xl_ready.sem, xl_ready.after(2 * b + 2))
            pe.wait_ge(gelued.sem, gelued.after(n + 1 - 2))
            for k in range(KD):
                for part in (xh, xl):
                    mm = pe.matmul(pH[c % 2][:, :], net.wfcT[:, k, c * P:(c + 1) * P], part[p][:, k, :],
                                   start=(k == 0 and part is xh), stop=(k == KD - 1 and part is xl))
            mm.then_inc(up_made.sem, 1)

        def down(b, c):
            n = NH * b + c
            pe.wait_ge(split.sem, split.after(n + 1))
            for t in range(TPB):
                if c == 0:
                    pe.wait_ge(y_taken.sem, y_taken.after(TPB * b + t + 1 - TPB))
                out, cols = pY[:, t, 0:DIM + 2], slice(t * P, (t + 1) * P)
                pe.matmul(out, gh[c % 4][:, cols], net.wpjH[:, c, :], start=(c == 0), stop=False)
                pe.matmul(out, gh[c % 4][:, cols], net.wpjL[:, c, :], start=False, stop=False)
                mm = pe.matmul(out, gl[c % 4][:, cols], net.wpjH[:, c, :], start=False, stop=(c == NH - 1))
            mm.then_inc(down_made.sem, 1)

        def sums(b, p):
            pe.wait_ge(added.sem, added.after((NH - 1) * (b + 1)))
            if not isinstance(b, int) or b:
                pe.wait_ge(var_ready.sem, var_ready.after(b))
            for t in range(TPB):
                mm = pe.matmul(pS[:, t:t + 1], acc[p][:, t * P:(t + 1) * P], net.table["ones"][:, 0:1], start=True, stop=True)
            mm.then_inc(s_made.sem, 1)

        def body(b, p, before, behind):
            for c in range(NH):
                up(b, p, c)
                if c >= 2:
                    down(b, c - 2)
                elif before:
                    down(b - 1, c + NH - 2)
                    if c == 1:
                        sums(b - 1, 1 - p)
                if behind and c in (3, 5):
                    turn(b + 1, 1 - p, (c - 3) // 2)

        for k in range(KD):
            turn(0, 0, k)
        batches(pe, body)
        down(BATCH - 1, NH - 2)
        down(BATCH - 1, NH - 1)
        sums(BATCH - 1, 1)

    @block.vector
    def _(dve):
        steps = Steps(step.sem)

        def low(b, p, k):
            dve.wait_ge(xh_ready.sem, xh_ready.after(2 * b + k + 1))
            dve.tensor_tensor(xl[p][:, k, :], pX[:, :], xh[p][:, k, :], ALU.subtract).then_inc(xl_ready.sem, 1)

        def divide(b, c):
            n = NH * b + c
            dve.wait_ge(gelued.sem, gelued.after(n + 1))
            dve.wait_ge(down_made.sem, down_made.after(n + 1 - 4))
            dve.tensor_copy(gh[c % 4][:, :], g[c % 4][:, :]).then_inc(steps.sem, 1)
            dve.wait_ge(steps.sem, steps.done(1))
            dve.tensor_tensor(gl[c % 4][:, :], g[c % 4][:, :], gh[c % 4][:, :], ALU.subtract).then_inc(split.sem, 1)

        def take(b):
            dve.wait_ge(down_made.sem, down_made.after(NH * (b + 1)))
            dve.tensor_scalar(negmean[:, :], pY[:, :, DIM], -1.0 / HID, None, ALU.mult).then_inc(steps.sem, 1)
            dve.wait_ge(steps.sem, steps.done(1))
            if not isinstance(b, int) or b:
                dve.wait_ge(rs_ready.sem, rs_ready.after(b))
            for t in range(TPB):
                dve.scalar_tensor_tensor(out=y[:, t, :], in0=net.u1[:, :], scalar=negmean[:, t:t + 1], in1=pY[:, t, 0:DIM],
                                         op0=ALU.mult, op1=ALU.add).then_inc(y_taken.sem, 1)
            dve.tensor_tensor(meansq[:, :], negmean[:, :], negmean[:, :], ALU.mult).then_inc(steps.sem, 1)
            dve.wait_ge(steps.sem, steps.done(1))
            dve.wait_ge(s_made.sem, s_made.after(b + 1))
            dve.scalar_tensor_tensor(out=var[:, :], in0=pS[:, :], scalar=1.0 / HID, in1=meansq[:, :],
                                     op0=ALU.mult, op1=ALU.subtract).then_inc(var_ready.sem, 1)

        def rows(b, t):
            if t == 0:
                dve.wait_ge(rs_ready.sem, rs_ready.after(b + 1))
                dve.wait_ge(xb_ready.sem, xb_ready.after(b + 1))
            dve.scalar_tensor_tensor(out=y[:, t, :], in0=y[:, t, :], scalar=rs[:, t:t + 1], in1=xb[:, t, :],
                                     op0=ALU.mult, op1=ALU.add).then_inc(steps.sem, 1)
            dve.wait_ge(steps.sem, steps.done(1))
            dve.bn_stats(yst[:, t, :], y[:, t, :]).then_inc(steps.sem, 1)
            dve.wait_ge(steps.sem, steps.done(1))
            dve.sem_inc(net.passed, 1)
            ins = dve.bn_aggr(ymv[:, t, :], yst[:, t, :])
            if t == TPB - 1:
                ins.then_inc(rows_ready.sem, 1)

        def norm(b):
            dve.wait_ge(yrs_ready.sem, yrs_ready.after(b + 1))
            for t in range(TPB):
                dve.tensor_scalar(tile_of(net, b * TPB + t), y[:, t, :], ymv[:, t, 0:1], yrs[:, t:t + 1], ALU.subtract, ALU.mult)\
                    .then_inc(steps.sem, 1)
            dve.wait_ge(steps.sem, steps.done(TPB))

        def body(b, p, before, behind):
            for c in range(NH):
                divide(b, c)
                if before:
                    if c == 1:
                        take(b - 1)
                    if 3 <= c < 7:
                        rows(b - 1, c - 3)
                    if c == 7:
                        norm(b - 1)
                if behind and c in (4, 6):
                    low(b + 1, 1 - p, (c - 4) // 2)

        for k in range(KD):
            low(0, 0, k)
        batches(dve, body, steps, NH + 2 + 2 * TPB + TPB)
        take(BATCH - 1)
        for t in range(TPB):
            rows(BATCH - 1, t)
        norm(BATCH - 1)


def attention_inputs(net, ctx):
    nc, a = net.nc, net.args
    ph = Phase(net, ctx, "q")
    two = range(2)
    g1 = ph.sb("g1", [P, KD])
    lam, lmb = ph.sb("lam", [P, 4]), ph.sb("lmb", [P, 4])
    qscale = ph.sb("qscale", [P, 1])
    sqv = ph.sb("sqv", [P, TPB, DIM])
    ssq = [ph.sb(f"ssq{i}", [P, TPB]) for i in two]
    rs = [ph.sb(f"rs{i}", [P, TPB]) for i in two]
    xn = [ph.sb(f"xn{i}", [P, TPB, DIM]) for i in two]
    xT = [ph.sb(f"xT{i}", [P, KD, SEQ]) for i in two]
    ex = [ph.sb(f"ex{i}", [P, SEQ]) for i in two]
    rl = [ph.sb(f"rl{i}", [P, SEQ]) for i in two]
    full, rest = ([ph.sb(f"{n}{i}", [P, TPB, 2, HALF]) for i in range(3)] for n in ("full", "rest"))
    res = [[ph.sb(f"res{n}{i}", [P, KD, TPB, 2, PARTS, HALF], BF16) for n in range(3)] for i in two]
    pX = [ph.ps(f"pX{k}", [P, SEQ]) for k in range(KD)]
    pE = [ph.ps(f"pE{i}", [P, SEQ]) for i in two]
    pV = [ph.ps(f"pV{i}", [P, SEQ]) for i in two]
    par_in, lam_ready, exp_lam = (ph.sig(n) for n in ("par_in", "lam_ready", "exp_lam"))
    ssq_ready, rs_ready, xn_ready, turned, xT_ready = (ph.sig(n, 1) for n in ("ssq_ready", "rs_ready", "xn_ready", "turned", "xT_ready"))
    e_made, e_taken, v_made, v_taken = (ph.sig(n, 1) for n in ("e_made", "e_taken", "v_made", "v_taken"))
    ex_free, stored = ph.sig("ex_free", 2), [ph.sig(f"stored{i}", 16 * 3) for i in two]
    full_ready, rest_ready, second_ready, third_ready = (ph.sig(n, 3) for n in ("full_ready", "rest_ready", "second_ready", "third_ready"))
    step, pool_step = ph.sig("step"), ph.sig("pool_step")

    ITEMS = 3 * KD

    def part(p, n, s):
        return res[p][n // KD][:, n % KD, :, :, s, :]

    nc.all_engine_barrier()
    block = ctx.enter_context(nc.Block())

    @block.sync
    def _(sp):
        with nc.allow_non_contiguous_dma(reason="1 KB, once"):
            sp.dma_start(g1[:, :], a["L1_attn_g1"].rearrange("(c p) -> p c", p=P)).then_inc(par_in.sem, 16)
        sp.dma_start(lam[:, :], a["L1_attn_lambda_params"].rearrange("(a h) -> a h", a=1).broadcast_to([P, 4])).then_inc(par_in.sem, 16)

        def store(b, p):
            sp.wait_ge(third_ready.sem, third_ready.after(ITEMS * b + ITEMS))
            for n in range(3):
                sp.dma_start(net.qkv_dram[n, :, bass.ds(b * TPB, TPB), :, :, :].rearrange("(k p) t g s w -> p k (t g s w)", p=P),
                             res[p][n][:, :, :, :, :, :].rearrange("p k t g s w -> p k (t g s w)"))\
                    .then_inc(stored[p].sem, 16)

        with sp.Fori(0, BATCH // 2) as i:
            for p in two:
                store(2 * i + p, p)
        for p in two:
            sp.wait_ge(stored[p].sem, stored[p].after(48 * BATCH // 2))

    @block.gpsimd
    def _(pool):
        steps = Steps(pool_step.sem)

        def front(b, p):
            pool.wait_ge(ssq_ready.sem, ssq_ready.after(b + 1))
            rstd_of(pool, steps, rs[p][:, :], ssq[p][:, :], RMS_EPS, net, 1.0 / DIM).then_inc(rs_ready.sem, 1)

        def body(b, p, before, behind):
            if behind:
                front(b + 1, 1 - p)
            for n in range(ITEMS):
                m = ITEMS * b + n
                pool.wait_ge(full_ready.sem, full_ready.after(m + 1))
                pool.wait_ge(third_ready.sem, third_ready.after(m + 1 - 3))
                pool.tensor_tensor(rest[n % 3][:, :, :, :], full[n % 3][:, :, :, :], part(p, n, 0), ALU.subtract).then_inc(rest_ready.sem, 1)

        front(0, 0)
        batches(pool, body, steps, 1)

    @block.scalar
    def _(act):
        act.wait_ge(par_in.sem, par_in.after(32))
        act.wait_ge(lam_ready.sem, lam_ready.after(1))
        nc.scalar.activation(lmb[:, 2:4], lmb[:, 0:2], ACT.Exp).then_inc(exp_lam.sem, 1)

        def front(b, p):
            if not isinstance(b, int) or b >= 2:
                act.wait_ge(turned.sem, turned.after(b - 1))
                act.sem_inc(net.passed_act, 1)
            for t in range(TPB):
                ins = nc.scalar.activation(sqv[:, t, :], tile_of(net, b * TPB + t), ACT.Square, accum_out=ssq[p][:, t:t + 1])
            ins.then_inc(ssq_ready.sem, 1)

        def take(b, p):
            act.wait_ge(turned.sem, turned.after(b + 1))
            for k in range(KD):
                ins = nc.scalar.activation(xT[p][:, k, :], pX[k][:, :], ACT.Copy, scale=g1[:, k:k + 1])
            ins.then_inc(xT_ready.sem, 1)

        def norm(b, p):
            act.wait_ge(rs_ready.sem, rs_ready.after(b + 1))
            act.sem_inc(net.passed_act, 1)
            for t in range(TPB):
                ins = nc.scalar.activation(xn[p][:, t, :], tile_of(net, b * TPB + t), ACT.Copy, scale=rs[p][:, t:t + 1])
            ins.then_inc(xn_ready.sem, 1)

        def second(b, p, n):
            m = ITEMS * b + n
            act.wait_ge(rest_ready.sem, rest_ready.after(m + 1))
            nc.scalar.activation(part(p, n, 1), rest[n % 3][:, :, :, :], ACT.Copy).then_inc(second_ready.sem, 1)

        def body(b, p, before, behind):
            if behind:
                front(b + 1, 1 - p)
            for n in range(4):
                m = 4 * b + n
                act.wait_ge(e_made.sem, e_made.after(m + 1))
                act.wait_ge(ex_free.sem, ex_free.after(m + 1 - 2))
                nc.scalar.activation(ex[n % 2][:, :], pE[n % 2][:, :], ACT.Exp)
                nc.scalar.activation(rl[n % 2][:, :], pE[n % 2][:, :], ACT.Relu).then_inc(e_taken.sem, 1)
                if n >= 2:
                    second(b, p, n - 2)
            if behind:
                norm(b + 1, 1 - p)
            for n in range(2, ITEMS):
                if n == 3 and behind:
                    take(b + 1, 1 - p)
                second(b, p, n)

        front(0, 0)
        norm(0, 0)
        take(0, 0)
        batches(act, body)

    @block.tensor
    def _(pe):
        def front(b, p):
            pe.wait_ge(xn_ready.sem, xn_ready.after(b + 1))
            if not (isinstance(b, int) and b == 0):
                pe.wait_ge(xT_ready.sem, xT_ready.after(b))
            for k in range(KD):
                for t in range(TPB):
                    mm = pe.transpose(pX[k][:, t * P:(t + 1) * P], xn[p][:, t, k * P:(k + 1) * P], net.table["ident"])
            mm.then_inc(turned.sem, 1)

        def body(b, p, before, behind):
            first = isinstance(b, int) and b == 0
            pe.wait_ge(xT_ready.sem, xT_ready.after(b + 1))
            for n in range(6):
                if n < 4:
                    if not (first and n < 2):
                        pe.wait_ge(e_taken.sem, e_taken.after(4 * b + n - 1))
                    out, made = pE[n % 2], e_made
                else:
                    if not first:
                        pe.wait_ge(v_taken.sem, v_taken.after(2 * b + n - 4 - 1))
                    out, made = pV[n % 2], v_made
                for k in range(KD):
                    mm = pe.matmul(out[:, :], net.wqkvT[:, k, n * P:(n + 1) * P], xT[p][:, k, :], start=(k == 0), stop=(k == KD - 1))
                mm.then_inc(made.sem, 1)
            if behind:
                front(b + 1, 1 - p)

        front(0, 0)
        batches(pe, body)

    @block.vector
    def _(dve):
        steps = Steps(step.sem)
        dve.wait_ge(par_in.sem, par_in.after(32))
        lv = lam[:, :].rearrange("p (a b) -> p a b", b=2)
        dve.tensor_tensor(lmb[:, 0:2], lv[:, :, 0], lv[:, :, 1], ALU.mult).then_inc(lam_ready.sem, 1)
        dve.wait_ge(exp_lam.sem, exp_lam.after(1))
        dve.tensor_tensor(lmb[:, 0:1], lmb[:, 2:3], lmb[:, 3:4], ALU.subtract).then_inc(steps.sem, 1)
        dve.wait_ge(steps.sem, steps.done(1))
        dve.tensor_scalar(lmb[:, 0:1], lmb[:, 0:1], LAMBDA_INIT, 1.0, ALU.add, ALU.add).then_inc(steps.sem, 1)
        dve.wait_ge(steps.sem, steps.done(1))
        dve.tensor_scalar(lmb[:, 1:2], net.table["firsthalf"], lmb[:, 0:1], 1.0, ALU.mult, ALU.add).then_inc(steps.sem, 1)
        dve.wait_ge(steps.sem, steps.done(1))
        dve.tensor_tensor(lmb[:, 1:2], lmb[:, 1:2], lmb[:, 0:1], ALU.subtract).then_inc(steps.sem, 1)
        dve.wait_ge(steps.sem, steps.done(1))
        dve.tensor_scalar(qscale[:, :], lmb[:, 1:2], RET_SCALE, None, ALU.mult).then_inc(steps.sem, 1)
        dve.wait_ge(steps.sem, steps.done(1))

        def third(b, p, n):
            m = ITEMS * b + n
            dve.wait_ge(second_ready.sem, second_ready.after(m + 1))
            dve.tensor_tensor(part(p, n, 2), rest[n % 3][:, :, :, :], part(p, n, 1), ALU.subtract).then_inc(third_ready.sem, 1)

        def body(b, p, before, behind):
            dve.wait_ge(stored[p].sem, stored[p].after(48 * (b // 2) if isinstance(b, int) else 24 * (b - p)))
            for n in range(ITEMS):
                m = ITEMS * b + n
                dst = full[n % 3][:, :, :, :].rearrange("p t g w -> p (t g w)")
                if n < 4:
                    dve.wait_ge(e_taken.sem, e_taken.after(4 * b + n + 1))
                    dve.scalar_tensor_tensor(out=rl[n % 2][:, :], in0=ex[n % 2][:, :], scalar=1.0, in1=rl[n % 2][:, :],
                                             op0=ALU.min, op1=ALU.add).then_inc(steps.sem, 1)
                    dve.wait_ge(steps.sem, steps.done(1))
                else:
                    dve.wait_ge(v_made.sem, v_made.after(2 * b + n - 4 + 1))
                dve.wait_ge(rest_ready.sem, rest_ready.after(m + 1 - 3))
                if n < 2:
                    ins = dve.tensor_scalar(dst, rl[n % 2][:, :], 1.0, qscale[:, :], ALU.subtract, ALU.mult)
                elif n < 4:
                    ins = dve.tensor_scalar(dst, rl[n % 2][:, :], 1.0, None, ALU.subtract)
                else:
                    ins = dve.tensor_copy(dst, pV[n - 4][:, :])
                ins.then_inc(ex_free.sem if n < 4 else v_taken.sem, 1)
                if n < 4:
                    dve.wait_ge(ex_free.sem, ex_free.after(4 * b + n + 1))
                else:
                    dve.wait_ge(v_taken.sem, v_taken.after(2 * b + n - 4 + 1))
                dve.tensor_copy(part(p, n, 0), full[n % 3][:, :, :, :]).then_inc(full_ready.sem, 1)
                if n >= 2:
                    third(b, p, n - 2)
            third(b, p, ITEMS - 2)
            third(b, p, ITEMS - 1)

        batches(dve, body, steps, 4)


def per_token_attention(net, ctx):
    nc, a = net.nc, net.args
    ph = Phase(net, ctx, "t")
    two = range(2)
    CH, STEPS = 4, P // 4
    kb, vb = ph.sb("kb", [P, P, PARTS, HALF], BF16), ph.sb("vb", [P, P, PARTS, HALF], BF16)
    q = [ph.sb(f"q{i}", [P, HEADS, PARTS, HALF], BF16) for i in two]
    rest = [ph.sb(f"rest{i}", [P, STEPS, HEADS]) for i in two]
    at = [ph.sb(f"at{i}", [P, PARTS, STEPS, HEADS], BF16) for i in two]
    ob = ph.sb("ob", [P, HEADS, P])
    g2, g3 = ph.sb("g2", [P, HD]), ph.sb("g3", [P, DIM])
    sqall = ph.sb("sqall", [P, GROUPS * DIM])
    hs, hr, hy = ph.sb("hs", [P, GROUPS * HEADS]), ph.sb("hr", [P, GROUPS * HEADS]), ph.sb("hy", [P, GROUPS * HEADS])
    es, er, ey = ph.sb("es", [P, GROUPS]), ph.sb("er", [P, GROUPS]), ph.sb("ey", [P, GROUPS])
    mrow = sqall[:, :].rearrange("p (j d) -> p j d", j=GROUPS)
    pA = [ph.ps(f"pA{i}", [P, STEPS, HEADS]) for i in two]
    pO = [ph.ps(f"pO{i}", [P, STEPS, HEADS]) for i in two]
    pW = [ph.ps(f"pW{i}", [P, 4, P]) for i in range(4)]
    g_in = ph.sig("g_in")
    k_in, v_in, q_in = ph.sig("k_in"), ph.sig("v_in"), [ph.sig(f"q_in{i}") for i in two]
    cleared_k, cleared_v = ph.sig("cleared_k"), ph.sig("cleared_v")
    a_made, o_made, first_ready, rest_ready, second_ready, third_ready = (
        ph.sig(n, 4) for n in ("a_made", "o_made", "first_ready", "rest_ready", "second_ready", "third_ready"))
    o_taken, w_made, w_act, w_dve = (ph.sig(n, 4) for n in ("o_taken", "w_made", "w_act", "w_dve"))
    squared, sums_ready, root_ready, scaled, es_ready, er_ready = (
        ph.sig(n) for n in ("squared", "sums_ready", "root_ready", "scaled", "es_ready", "er_ready"))
    step = ph.sig("step")
    att = net.att_res

    def zeroed(t, half):
        return t[:, half * HALF:(half + 1) * HALF, :, :].rearrange("p a s b -> p (a s b)").bitcast(F32)

    nc.all_engine_barrier()
    block = ctx.enter_context(nc.Block())

    @block.sync
    def _(sp):
        sp.dma_start(g2[:, :], a["L1_attn_g2"].rearrange("(a h) -> a h", a=1).broadcast_to([P, HD])).then_inc(g_in.sem, 16)
        sp.dma_start(g3[:, :], a["L1_attn_g3"].rearrange("(a h) -> a h", a=1).broadcast_to([P, DIM])).then_inc(g_in.sem, 16)
        q_src = net.qkv_dram[0].rearrange("(h e) t g s w -> e h t g s w", e=HD)
        k_src = net.qkv_dram[1].rearrange("(h e) t g s w -> e h t g s w", e=HD)
        v_src = net.qkv_dram[2].rearrange("(h d) t g s w -> h d t g s w", d=HD)

        def rows(dst, src, u, s, diagonal, sig):
            for j in range(GROUPS):
                to = dst[j * HD:(j + 1) * HD, j * HD:(j + 1) * HD, :, :] if diagonal else dst[j * HD:(j + 1) * HD, :, :, :]
                sp.dma_start(to.rearrange("p h s w -> p h (s w)"),
                             src[:, :, bass.ds(u * GROUPS + j, 1), s, :, :].rearrange("e h t s w -> e (h t) (s w)")).then_inc(sig.sem, 16)

        with sp.Fori(0, UNITS) as u:
            for s in two:
                n = 2 * u + s
                sp.wait_ge(a_made.sem, a_made.after(2 * n - 2))
                rows(q[s], q_src, u, s, False, q_in[s])
                if s == 0:
                    sp.wait_ge(cleared_k.sem, cleared_k.after(2))
                sp.wait_ge(a_made.sem, a_made.after(2 * n))
                rows(kb, k_src, u, s, True, k_in)
                if s == 0:
                    sp.wait_ge(cleared_v.sem, cleared_v.after(2))
                sp.wait_ge(o_made.sem, o_made.after(2 * n))
                rows(vb, v_src, u, s, True, v_in)

    @block.gpsimd
    def _(pool):
        pool.memset(zeroed(kb, 1), 0.0).then_inc(cleared_k.sem, 1)
        pool.memset(zeroed(vb, 1), 0.0).then_inc(cleared_v.sem, 1)

        def split(u, c):
            n = CH * u + c
            pool.wait_ge(first_ready.sem, first_ready.after(n + 1))
            pool.wait_ge(third_ready.sem, third_ready.after(n + 1 - 2))
            pool.tensor_tensor(rest[c % 2][:, :, :], rest[c % 2][:, :, :], at[c % 2][:, 0, :, :], ALU.subtract).then_inc(rest_ready.sem, 1)
            pool.wait_ge(second_ready.sem, second_ready.after(n + 1))
            pool.tensor_tensor(at[c % 2][:, 2, :, :], rest[c % 2][:, :, :], at[c % 2][:, 1, :, :], ALU.subtract).then_inc(third_ready.sem, 1)

        with pool.Fori(0, UNITS) as u:
            for c in range(CH):
                split(u, c)

    @block.tensor
    def _(pe):

        def scores(u, c):
            n = CH * u + c
            pe.wait_ge(first_ready.sem, first_ready.after(n - 1))
            for s in range(STEPS):
                at0 = (c % 2) * STEPS + s
                for k, (kp, qp) in enumerate(TERMS):
                    mm = pe.matmul(pA[c % 2][:, s, :], kb[:, :, kp, at0], q[c // 2][:, :, qp, at0],
                                   start=(k == 0), stop=(k == len(TERMS) - 1))
            mm.then_inc(a_made.sem, 1)

        def mix(u, c):
            n = CH * u + c
            pe.wait_ge(third_ready.sem, third_ready.after(n + 1))
            pe.wait_ge(o_taken.sem, o_taken.after(n - 1))
            for s in range(STEPS):
                at0 = (c % 2) * STEPS + s
                for k, (vp, ap) in enumerate(TERMS):
                    mm = pe.matmul(pO[c % 2][:, s, :], vb[:, :, vp, at0], at[c % 2][:, ap, s, :],
                                   start=(k == 0), stop=(k == len(TERMS) - 1))
            mm.then_inc(o_made.sem, 1)

        def turn(u):
            pe.wait_ge(o_taken.sem, o_taken.after(CH * (u + 1)))
            for r in range(4):
                done = (w_act, w_dve)[r // 2]
                pe.wait_ge(done.sem, done.after(2 * u + r % 2 - 1))
                for g in range(4):
                    mm = pe.transpose(pW[r][:, g, :], ob[:, 4 * r + g, :], net.table["ident"])
                mm.then_inc(w_made.sem, 1)

        def unit(u, before):
            for s in two:
                pe.wait_ge(k_in.sem, k_in.after(128 * (2 * u + s + 1)))
                pe.wait_ge(q_in[s].sem, q_in[s].after(128 * (u + 1)))
                scores(u, 2 * s)
                scores(u, 2 * s + 1)
                if s == 0 and before:
                    turn(u - 1)
                pe.wait_ge(v_in.sem, v_in.after(128 * (2 * u + s + 1)))
                mix(u, 2 * s)
                mix(u, 2 * s + 1)

        unit(0, False)
        with pe.Fori(1, UNITS) as u:
            unit(u, True)
        turn(UNITS - 1)

    def heads_of(u, r):
        return att[:, bass.ds(u * GROUPS, GROUPS), 4 * r * HD:4 * (r + 1) * HD].rearrange("p j (g d) -> p g j d", d=HD)

    def unit_rows(u):
        return att[:, bass.ds(u * GROUPS, GROUPS), :]

    def token_rows(u, j):
        return att[:, bass.ds(u * GROUPS + j, 1), :].rearrange("p a d -> p (a d)")

    @block.scalar
    def _(act):

        def take(u, c):
            n = CH * u + c
            act.wait_ge(a_made.sem, a_made.after(n + 1))
            act.wait_ge(o_made.sem, o_made.after(n - 1))
            nc.scalar.activation(at[c % 2][:, 0, :, :], pA[c % 2][:, :, :], ACT.Copy)
            nc.scalar.activation(rest[c % 2][:, :, :], pA[c % 2][:, :, :], ACT.Copy).then_inc(first_ready.sem, 1)

        def second(u, c):
            n = CH * u + c
            act.wait_ge(rest_ready.sem, rest_ready.after(n + 1))
            nc.scalar.activation(at[c % 2][:, 1, :, :], rest[c % 2][:, :, :], ACT.Copy).then_inc(second_ready.sem, 1)

        def heads(u):
            for r in two:
                act.wait_ge(w_made.sem, w_made.after(4 * u + r + 1))
                act.sem_inc(net.passed_act, 1)
                ins = nc.scalar.activation(heads_of(u, r), pW[r][:, :, :].rearrange("p g (j d) -> p g j d", d=HD), ACT.Copy)
                ins.then_inc(w_act.sem, 1)

        def squares(u):
            act.wait_ge(w_act.sem, w_act.after(2 * u + 2))
            act.wait_ge(w_dve.sem, w_dve.after(2 * u + 2))
            act.sem_inc(net.passed_act, 1)
            ins = nc.scalar.activation(sqall[:, :].rearrange("p (j d) -> p j d", j=GROUPS), unit_rows(u), ACT.Square)
            ins.then_inc(squared.sem, 1)

        def head_roots(u):
            act.wait_ge(sums_ready.sem, sums_ready.after(u + 1))
            nc.scalar.activation(hr[:, :], hs[:, :], ACT.Sqrt, bias=net.table["rmseps"], scale=1.0 / HD).then_inc(root_ready.sem, 1)

        def row_roots(u):
            act.wait_ge(scaled.sem, scaled.after(u + 1))
            act.sem_inc(net.passed_act, 1)
            for j in range(GROUPS):
                ins = nc.scalar.activation(sqall[:, j * DIM:(j + 1) * DIM], token_rows(u, j), ACT.Square, accum_out=es[:, j:j + 1])
            ins.then_inc(es_ready.sem, 1)
            act.wait_ge(es_ready.sem, es_ready.after(u + 1))
            nc.scalar.activation(er[:, :], es[:, :], ACT.Sqrt, bias=net.table["rmseps"], scale=1.0 / DIM).then_inc(er_ready.sem, 1)

        def unit(u, before):
            for c in range(CH):
                take(u, c)
                second(u, c)
                if before:
                    if c == 1:
                        heads(u - 1)
                        squares(u - 1)
                    elif c == 2:
                        head_roots(u - 1)
                    elif c == 3:
                        row_roots(u - 1)

        unit(0, False)
        with act.Fori(1, UNITS) as u:
            unit(u, True)
        heads(UNITS - 1)
        squares(UNITS - 1)
        head_roots(UNITS - 1)
        row_roots(UNITS - 1)

    @block.vector
    def _(dve):
        steps = Steps(step.sem)

        def take(u, c):
            n = CH * u + c
            dve.wait_ge(o_made.sem, o_made.after(n + 1))
            if c == 0:
                dve.wait_ge(w_made.sem, w_made.after(4 * u))
            dve.tensor_copy(ob[:, :, c * STEPS:(c + 1) * STEPS].rearrange("p h t -> p t h"), pO[c % 2][:, :, :]).then_inc(o_taken.sem, 1)

        def inverse(root, mean_sq_scale, sums, out):
            dve.reciprocal(out, root).then_inc(steps.sem, 1)
            dve.wait_ge(steps.sem, steps.done(1))
            dve.tensor_scalar(root, sums, mean_sq_scale, RMS_EPS, ALU.mult, ALU.add).then_inc(steps.sem, 1)
            dve.wait_ge(steps.sem, steps.done(1))
            dve.tensor_tensor(root, root, out, ALU.mult).then_inc(steps.sem, 1)
            dve.wait_ge(steps.sem, steps.done(1))
            dve.tensor_tensor(root, root, out, ALU.mult).then_inc(steps.sem, 1)
            dve.wait_ge(steps.sem, steps.done(1))
            dve.tensor_scalar(root, root, -0.5, 1.5, ALU.mult, ALU.add).then_inc(steps.sem, 1)
            dve.wait_ge(steps.sem, steps.done(1))
            dve.tensor_tensor(out, out, root, ALU.mult).then_inc(steps.sem, 1)
            dve.wait_ge(steps.sem, steps.done(1))

        def heads(u):
            for r in (2, 3):
                dve.wait_ge(w_made.sem, w_made.after(4 * u + r + 1))
                ins = dve.tensor_copy(heads_of(u, r), pW[r][:, :, :].rearrange("p g (j d) -> p g j d", d=HD))
                ins.then_inc(w_dve.sem, 1)

        def head_sums(u):
            dve.wait_ge(squared.sem, squared.after(u + 1))
            dve.tensor_reduce(hs[:, :], sqall[:, :].rearrange("p (g d) -> p g d", d=HD), AX.X, ALU.add).then_inc(sums_ready.sem, 1)

        def head_norm(u):
            per_head = unit_rows(u).rearrange("p j (h d) -> p (j h) d", d=HD)
            dve.wait_ge(root_ready.sem, root_ready.after(u + 1))
            inverse(hr[:, :], 1.0 / HD, hs[:, :], hy[:, :])
            dve.tensor_tensor(per_head, per_head, hy[:, :].rearrange("p (g a) -> p g a", a=1).broadcast_to([P, GROUPS * HEADS, HD]), ALU.mult)\
                .then_inc(steps.sem, 1)
            dve.wait_ge(steps.sem, steps.done(1))
            dve.tensor_tensor(per_head, per_head, g2[:, :].rearrange("p (a d) -> p a d", a=1).broadcast_to([P, GROUPS * HEADS, HD]), ALU.mult)\
                .then_inc(scaled.sem, 1)

        def row_norm(u):
            dve.wait_ge(er_ready.sem, er_ready.after(u + 1))
            inverse(er[:, :], 1.0 / DIM, es[:, :], ey[:, :])
            for j in range(GROUPS):
                dve.tensor_scalar(mrow[:, j, :], g3[:, :], ey[:, j:j + 1], 1.0, ALU.mult, ALU.add).then_inc(steps.sem, 1)
            dve.wait_ge(steps.sem, steps.done(GROUPS))
            dve.tensor_tensor(unit_rows(u), unit_rows(u), mrow, ALU.mult).then_inc(steps.sem, 1)
            dve.wait_ge(steps.sem, steps.done(1))

        def unit(u, before):
            for c in range(CH):
                if c == 0 and before:
                    heads(u - 1)
                take(u, c)
                if c and before:
                    (head_sums, head_norm, row_norm)[c - 1](u - 1)

        dve.memset(zeroed(kb, 0), 0.0).then_inc(cleared_k.sem, 1)
        dve.memset(zeroed(vb, 0), 0.0).then_inc(cleared_v.sem, 1)
        dve.wait_ge(g_in.sem, g_in.after(32))
        dve.tensor_scalar(g2[:, :], g2[:, :], 1.0 - LAMBDA_INIT, None, ALU.mult).then_inc(steps.sem, 1)
        dve.wait_ge(steps.sem, steps.done(1))
        unit(0, False)
        with dve.Fori(1, UNITS) as u:
            steps.enter(u - 1, 6 + 1 + 6 + GROUPS + 1)
            unit(u, True)
            steps.leave(UNITS - 1)
        heads(UNITS - 1)
        head_sums(UNITS - 1)
        head_norm(UNITS - 1)
        row_norm(UNITS - 1)


def attention_mlp_and_route(net, ctx):
    nc, a = net.nc, net.args
    ph = Phase(net, ctx, "m")
    net.wi = [net.sb(f"wi{i}", [P, KD, HID]) for i in range(2)]
    net.wo = [net.sb(f"wo{i}", [P, NH, DIM]) for i in range(2)]
    own, net.signals = net.signals, []
    net.w_in = [Signal(net, net.ctx, f"w_in{i}") for i in range(2)]
    net.signals = own
    two = range(2)
    wr = ph.sb("wr", [P, KD, EXPERTS])
    ac = ph.sb("ac", [P, TPB, DIM])
    aT = ph.sb("aT", [P, KD, SEQ])
    hT = ph.sb("hT", [P, KD, SEQ])
    s = ph.sb("s", [P, TPB, DIM])
    y, xn = ph.sb("y", [P, TPB, DIM]), ph.sb("xn", [P, TPB, DIM])
    xT = ph.sb("xT", [P, KD, SEQ])
    yst, ymv, yrs = ph.sb("yst", [P, TPB, 6]), ph.sb("ymv", [P, TPB, 2]), ph.sb("yrs", [P, TPB])
    pX = ph.ps("pX", [P, KD, SEQ])
    pH = [ph.ps(f"pH{i}", [P, SEQ]) for i in two]
    pY = [ph.ps(f"pY{i}", [P, 2, DIM]) for i in two]
    pZ, pLC = ph.ps("pZ", [P, SEQ]), ph.ps("pLC", [P, 512])
    pL = pLC[:, 0:TPB * EXPERTS].rearrange("p (t e) -> p t e", e=EXPERTS)
    pC = pLC[:, TPB * EXPERTS:TPB * EXPERTS + TOPK * TPG * EXPERTS]
    w_in, copied, turned, aT_ready = (ph.sig(n) for n in ("w_in", "copied", "turned", "aT_ready"))
    h_made, gelued, y_made, y_taken = ph.sig("h_made"), ph.sig("gelued"), ph.sig("y_made", 2), ph.sig("y_taken", 2)
    s_ready, mv_ready, yrs_ready, xn_ready = (ph.sig(n) for n in ("s_ready", "mv_ready", "yrs_ready", "xn_ready"))
    z_turned, xT_ready, l_made, l_taken = ph.sig("z_turned", 2), ph.sig("xT_ready", 1), ph.sig("l_made", 1), ph.sig("l_taken", 1)
    step, pool_step = ph.sig("step"), ph.sig("pool_step")
    lg = net.lg
    pr, s8, tmp = ph.sb("pr", [P, TILES, EXPERTS]), ph.sb("s8", [P, TILES, EXPERTS]), ph.sb("tmp", [P, TILES, EXPERTS])
    m1 = ph.sb("m1", [P, TILES])
    big = [P, MGROUPS, TOPK, TPG, EXPERTS]
    mask, pos, tot = ph.sb("mask", big), ph.sb("pos", big), ph.sb("tot", big)
    acc = [ph.sb(f"acc{i}", big) for i in two]
    posk, row, keep, idxf = (ph.sb(n, big[:-1]) for n in ("posk", "row", "keep", "idxf"))
    idx_out = ph.sb("idx_out", big[:-1], U32)
    zeros = ph.sb("zeros", [P, SLOTS // P * DIM])
    shifted, exped, mask_ready, n_made, n_taken, p_made, p_taken, idx_ready, cleared = (
        ph.sig(n) for n in ("shifted", "exped", "mask_ready", "n_made", "n_taken", "p_made", "p_taken", "idx_ready", "cleared"))
    zero_ready, sent = ph.sig("zero_ready"), ph.sig("sent")
    GB = BATCH // MGROUPS

    def all_batches(eng, body, steps=None, per=0):
        body(0, False, True)
        with eng.Fori(1, GB) as b:
            if steps:
                steps.enter(b - 1, per)
            body(b, True, True)
            if steps:
                steps.leave(GB - 1)
        for b in range(GB, BATCH):
            body(b, True, b < BATCH - 1)

    nc.all_engine_barrier()
    block = ctx.enter_context(nc.Block())

    @block.sync
    def _(sp):
        sp.dma_start(wr[:, :, :], a["L1_ffn_w_router"].rearrange("(k p) n -> p k n", p=P)).then_inc(w_in.sem, 16)
        sp.wait_ge(w_in.sem, w_in.after(16))
        sp.wait_ge(zero_ready.sem, zero_ready.after(1))
        sp.dma_start(net.xe_dram.rearrange("(p r) d -> p (r d)", p=P), zeros[:, :]).then_inc(cleared.sem, 16)
        sp.dma_start(net.ye_dram[SLOTS:SLOTS + 1, :], zeros[0:1, 0:DIM]).then_inc(cleared.sem, 16)
        for e in range(2):
            load_expert(net, sp, e, e)
        sp.wait_ge(cleared.sem, cleared.after(32))

    @block.gpsimd
    def _(pool):
        steps = Steps(pool_step.sem)

        def base(b):
            pool.wait_ge(y_taken.sem, y_taken.after(2 * b))
            pool.sem_inc(net.passed_pool, 1)
            pool.tensor_tensor(s[:, :, :], net.x_res[:, bass.ds(b * TPB, TPB), :], net.att_res[:, bass.ds(b * TPB, TPB), :], ALU.add)\
                .then_inc(s_ready.sem, 1)

        def send(g, first, last):
            pool.wait_ge(idx_ready.sem, idx_ready.after(g + 1))
            pool.wait_ge(cleared.sem, cleared.after(32))
            for n in range(first, last):
                k, t = n // TPG, n % TPG
                pool.indirect_dma_start(net.xe_dram[:, :], bass.IndirectOffsetOnAxis(ap=idx_out[:, g, k, t:t + 1], axis=0),
                                        net.x_res[:, g * TPG + t, :], None, bounds_check=SLOTS - 1, oob_is_err=False)\
                    .then_inc(sent.sem, 16)

        EARLY = 10

        def body(b, before, behind):
            pool.wait_ge(mv_ready.sem, mv_ready.after(b + 1))
            rstd_of(pool, steps, yrs[:, :], ymv[:, :, 1], LN_EPS, net).then_inc(yrs_ready.sem, 1)
            if behind:
                base(b + 1)
            if isinstance(b, int) and b == BATCH - 2:
                send(0, 0, EARLY)

        base(0)
        all_batches(pool, body, steps, 1)
        send(0, EARLY, TOPK * TPG)
        send(1, 0, TOPK * TPG)
        pool.wait_ge(sent.sem, sent.after(16 * MGROUPS * TOPK * TPG))

    @block.tensor
    def _(pe):
        pe.wait_ge(w_in.sem, w_in.after(16))

        def turn(b):
            pe.wait_ge(copied.sem, copied.after(b + 1))
            if not isinstance(b, int) or b:
                pe.wait_ge(aT_ready.sem, aT_ready.after(b))
            for k in range(KD):
                for t in range(TPB):
                    mm = pe.transpose(pX[:, k, t * P:(t + 1) * P], ac[:, t, k * P:(k + 1) * P], net.table["ident"])
            mm.then_inc(turned.sem, 1)

        def up(b):
            pe.wait_ge(aT_ready.sem, aT_ready.after(b + 1))
            if not isinstance(b, int) or b:
                pe.wait_ge(gelued.sem, gelued.after(2 * b))
            for m in two:
                for k in range(KD):
                    mm = pe.matmul(pH[m][:, :], net.w1T[:, k, m * P:(m + 1) * P], aT[:, k, :], start=(k == 0), stop=(k == KD - 1))
                mm.then_inc(h_made.sem, 1)

        def down(b):
            pe.wait_ge(gelued.sem, gelued.after(2 * b + 2))
            for h in two:
                pe.wait_ge(y_taken.sem, y_taken.after(2 * b + h + 1 - 2))
                for t in (2 * h, 2 * h + 1):
                    for k in range(KD):
                        mm = pe.matmul(pY[h][:, t % 2, :], hT[:, k, t * P:(t + 1) * P], net.w2T[:, k, :],
                                       start=(k == 0), stop=(k == KD - 1))
                mm.then_inc(y_made.sem, 1)

        def turn_x(b, k):
            if k == 0:
                pe.wait_ge(xn_ready.sem, xn_ready.after(b + 1))
            pe.wait_ge(xT_ready.sem, xT_ready.after(2 * b + k))
            for t in range(TPB):
                mm = pe.transpose(pZ[:, t * P:(t + 1) * P], xn[:, t, k * P:(k + 1) * P], net.table["ident"])
            mm.then_inc(z_turned.sem, 1)

        def logits(b):
            pe.wait_ge(xT_ready.sem, xT_ready.after(2 * b + 2))
            pe.wait_ge(l_taken.sem, l_taken.after(b))
            if isinstance(b, int) and b > GB:
                pe.wait_ge(p_taken.sem, p_taken.after(1))
            for t in range(TPB):
                for k in range(KD):
                    mm = pe.matmul(pL[:, t, :], xT[:, k, t * P:(t + 1) * P], wr[:, k, :], start=(k == 0), stop=(k == KD - 1))
            mm.then_inc(l_made.sem, 1)

        def count(g, kept):
            pe.wait_ge(mask_ready.sem, mask_ready.after(g + 1))
            pe.wait_ge(l_taken.sem, l_taken.after(kept))
            chosen = mask[:, g, :, :, :].rearrange("p k t e -> p (k t e)")
            pe.matmul(pC, net.table["ones"], chosen, start=True, stop=True).then_inc(n_made.sem, 1)
            pe.wait_ge(n_taken.sem, n_taken.after(g + 1))
            pe.matmul(pC, net.table["tri"], chosen, start=True, stop=True).then_inc(p_made.sem, 1)

        def body(b, before, behind):
            if before:
                turn_x(b - 1, 0)
            if behind:
                turn(b + 1)
            down(b)
            if before:
                turn_x(b - 1, 1)
            if behind:
                up(b + 1)
            if before:
                logits(b - 1)
            if isinstance(b, int) and b == GB + 1:
                count(0, GB + 1)

        turn(0)
        up(0)
        all_batches(pe, body)
        turn_x(BATCH - 1, 0)
        turn_x(BATCH - 1, 1)
        logits(BATCH - 1)
        count(1, BATCH)

    @block.scalar
    def _(act):
        def copy(b):
            act.sem_inc(net.passed_act, 1)
            for t in range(TPB):
                att = net.att_res[:, bass.ds(b * TPB + t, 1), :].rearrange("p a d -> p (a d)")
                ins = nc.scalar.activation(ac[:, t, :], att, ACT.Copy)
            ins.then_inc(copied.sem, 1)

        def take(b):
            act.wait_ge(turned.sem, turned.after(b + 1))
            nc.scalar.activation(aT[:, :, :], pX[:, :, :], ACT.Copy).then_inc(aT_ready.sem, 1)

        def gelu(b):
            for m in two:
                act.wait_ge(h_made.sem, h_made.after(2 * b + m + 1))
                if m == 0 and (not isinstance(b, int) or b):
                    act.wait_ge(y_made.sem, y_made.after(2 * b))
                nc.scalar.activation(hT[:, m, :], pH[m][:, :], ACT.Gelu).then_inc(gelued.sem, 1)

        def take_x(b, k):
            act.wait_ge(z_turned.sem, z_turned.after(2 * b + k + 1))
            act.wait_ge(l_made.sem, l_made.after(b))
            nc.scalar.activation(xT[:, k, :], pZ[:, :], ACT.Copy).then_inc(xT_ready.sem, 1)

        def exp(g):
            tiles = slice(g * TPG, (g + 1) * TPG)
            act.wait_ge(shifted.sem, shifted.after(g + 1))
            nc.scalar.activation(pr[:, tiles, :], lg[:, tiles, :], ACT.Exp).then_inc(exped.sem, 1)

        def body(b, before, behind):
            if behind:
                copy(b + 1)
            if before:
                take_x(b - 1, 0)
            if behind:
                take(b + 1)
            if before:
                take_x(b - 1, 1)
            if behind:
                gelu(b + 1)
            if isinstance(b, int) and b == GB:
                exp(0)

        copy(0)
        take(0)
        gelu(0)
        all_batches(act, body)
        take_x(BATCH - 1, 0)
        take_x(BATCH - 1, 1)
        exp(1)

    @block.vector
    def _(dve):
        steps = Steps(step.sem)

        def rows(b):
            dve.wait_ge(s_ready.sem, s_ready.after(b + 1))
            for h in two:
                dve.wait_ge(y_made.sem, y_made.after(2 * b + h + 1))
                dve.tensor_tensor(y[:, 2 * h:2 * h + 2, :], pY[h][:, :, :], s[:, 2 * h:2 * h + 2, :], ALU.add).then_inc(y_taken.sem, 1)
            for t in range(TPB):
                if t % 2 == 0:
                    dve.wait_ge(y_taken.sem, y_taken.after(2 * b + t // 2 + 1))
                ins = dve.bn_stats(yst[:, t, :], y[:, t, :])
            ins.then_inc(steps.sem, 1)
            dve.wait_ge(steps.sem, steps.done(1))
            dve.sem_inc(net.passed, 1)
            for t in range(TPB):
                ins = dve.bn_aggr(ymv[:, t, :], yst[:, t, :])
            ins.then_inc(mv_ready.sem, 1)

        def norm(b):
            dve.wait_ge(yrs_ready.sem, yrs_ready.after(b + 1))
            dve.wait_ge(z_turned.sem, z_turned.after(2 * b))
            for t in range(TPB):
                ins = dve.tensor_scalar(xn[:, t, :], y[:, t, :], ymv[:, t, 0:1], yrs[:, t:t + 1], ALU.subtract, ALU.mult)
            ins.then_inc(xn_ready.sem, 1)
            for t in range(TPB):
                ins = dve.tensor_scalar(tile_of(net, b * TPB + t), y[:, t, :], ymv[:, t, 0:1], yrs[:, t:t + 1], ALU.subtract, ALU.mult)
            ins.then_inc(steps.sem, 1)
            dve.wait_ge(steps.sem, steps.done(1))

        def keep_logits(b):
            dve.wait_ge(l_made.sem, l_made.after(b + 1))
            dve.tensor_copy(net.lg[:, bass.ds(b * TPB, TPB), :], pL[:, :, :]).then_inc(l_taken.sem, 1)

        def choose(g):
            tiles = slice(g * TPG, (g + 1) * TPG)
            lgg, prg, s8g, tmpg, m1g = lg[:, tiles, :], pr[:, tiles, :], s8[:, tiles, :], tmp[:, tiles, :], m1[:, tiles]

            def each(x):
                return x.rearrange("p (t a) -> p t a", a=1).broadcast_to([P, TPG, EXPERTS])

            dve.wait_ge(l_taken.sem, l_taken.after((g + 1) * GB))
            dve.tensor_reduce(m1g, lgg, AX.X, ALU.max).then_inc(steps.sem, 1)
            dve.wait_ge(steps.sem, steps.done(1))
            dve.tensor_tensor(lgg, lgg, each(m1g), ALU.subtract).then_inc(shifted.sem, 1)
            dve.wait_ge(exped.sem, exped.after(g + 1))
            dve.tensor_reduce(m1g, prg, AX.X, ALU.add).then_inc(steps.sem, 1)
            dve.wait_ge(steps.sem, steps.done(1))
            dve.reciprocal(m1g, m1g).then_inc(steps.sem, 1)
            dve.wait_ge(steps.sem, steps.done(1))
            dve.tensor_tensor(prg, prg, each(m1g), ALU.mult).then_inc(steps.sem, 1)
            dve.wait_ge(steps.sem, steps.done(1))
            first = net.table["first"].rearrange("p (a e) -> p a e", a=1).broadcast_to([P, TPG, EXPERTS])
            for k in range(TOPK):
                gate, chosen = net.gates[:, k, tiles], mask[:, g, k, :, :]
                dve.tensor_reduce(gate, prg, AX.X, ALU.max).then_inc(steps.sem, 1)
                dve.wait_ge(steps.sem, steps.done(1))
                dve.tensor_tensor(s8g, prg, each(gate), ALU.is_equal).then_inc(steps.sem, 1)
                dve.wait_ge(steps.sem, steps.done(1))
                dve.tensor_tensor(s8g, s8g, first, ALU.mult).then_inc(steps.sem, 1)
                dve.wait_ge(steps.sem, steps.done(1))
                dve.tensor_reduce(m1g, s8g, AX.X, ALU.max).then_inc(steps.sem, 1)
                dve.wait_ge(steps.sem, steps.done(1))
                dve.tensor_tensor(chosen, s8g, each(m1g), ALU.is_equal).then_inc(steps.sem, 1)
                dve.wait_ge(steps.sem, steps.done(1))
                if k < TOPK - 1:
                    dve.scalar_tensor_tensor(out=prg, in0=chosen, scalar=-2.0, in1=prg, op0=ALU.mult, op1=ALU.add).then_inc(steps.sem, 1)
                    dve.wait_ge(steps.sem, steps.done(1))
            dve.sem_inc(mask_ready.sem, 1)

        def place(g):
            maskg, posg, totg = mask[:, g, :, :, :], pos[:, g, :, :, :], tot[:, g, :, :, :]

            def flat(t):
                return t.rearrange("p k t e -> p (k t e)")

            def five(t):
                return t.rearrange("p k t e -> p (k t) e")

            def four(t):
                return t[:, g, :, :].rearrange("p k t -> p (k t)")

            dve.wait_ge(n_made.sem, n_made.after(g + 1))
            dve.tensor_copy(flat(totg), pC).then_inc(n_taken.sem, 1)
            dve.wait_ge(n_taken.sem, n_taken.after(g + 1))
            av = [five(totg)] + [five(t[:, g, :, :, :]) for t in acc]
            src, dst, dist = 0, 1, 1
            while dist < TOPK * TPG:
                dve.tensor_copy(av[dst][:, 0:dist, :], av[src][:, 0:dist, :])
                dve.tensor_tensor(av[dst][:, dist:, :], av[src][:, dist:, :], av[src][:, 0:TOPK * TPG - dist, :], ALU.add).then_inc(steps.sem, 1)
                dve.wait_ge(steps.sem, steps.done(1))
                src, dst, dist = dst, 3 - dst, 2 * dist
            upto = acc[src - 1][:, g, :, :, :]
            dve.tensor_tensor(flat(upto), flat(upto), flat(totg), ALU.subtract).then_inc(steps.sem, 1)
            dve.wait_ge(steps.sem, steps.done(1))
            dve.wait_ge(p_made.sem, p_made.after(g + 1))
            dve.tensor_tensor(flat(posg), pC, flat(upto), ALU.add).then_inc(p_taken.sem, 1)
            dve.wait_ge(p_taken.sem, p_taken.after(g + 1))
            dve.tensor_tensor(flat(posg), flat(posg), flat(maskg), ALU.mult).then_inc(steps.sem, 1)
            dve.wait_ge(steps.sem, steps.done(1))
            dve.tensor_reduce(four(posk), five(posg), AX.X, ALU.add).then_inc(steps.sem, 1)
            dve.wait_ge(steps.sem, steps.done(1))
            base = net.table["base"].rearrange("p (a e) -> p a e", a=1).broadcast_to([P, TOPK * TPG, EXPERTS])
            dve.tensor_tensor(five(posg), five(maskg), base, ALU.mult).then_inc(steps.sem, 1)
            dve.wait_ge(steps.sem, steps.done(1))
            dve.tensor_reduce(four(row), five(posg), AX.X, ALU.add).then_inc(steps.sem, 1)
            dve.wait_ge(steps.sem, steps.done(1))
            dve.scalar_tensor_tensor(out=four(row), in0=four(row), scalar=float(g * CAP - 1), in1=four(posk),
                                     op0=ALU.add, op1=ALU.add).then_inc(steps.sem, 1)
            dve.wait_ge(steps.sem, steps.done(1))
            dve.tensor_scalar(four(keep), four(posk), float(CAP), None, ALU.is_le).then_inc(steps.sem, 1)
            dve.wait_ge(steps.sem, steps.done(1))
            dve.tensor_scalar(four(idxf), four(row), float(SLOTS), None, ALU.subtract).then_inc(steps.sem, 1)
            dve.wait_ge(steps.sem, steps.done(1))
            dve.tensor_tensor(four(idxf), four(idxf), four(keep), ALU.mult).then_inc(steps.sem, 1)
            dve.wait_ge(steps.sem, steps.done(1))
            dve.tensor_scalar(four(idxf), four(idxf), float(SLOTS), None, ALU.add).then_inc(steps.sem, 1)
            dve.wait_ge(steps.sem, steps.done(1))
            dve.tensor_copy(four(idx_out), four(idxf))
            dve.tensor_copy(net.idx_back[:, g * TPG:(g + 1) * TPG, :].rearrange("p t k -> p k t"), idxf[:, g, :, :]).then_inc(idx_ready.sem, 1)

        def body(b, before, behind):
            rows(b)
            norm(b)
            if before:
                keep_logits(b - 1)
            if isinstance(b, int) and b == GB:
                choose(0)
            if isinstance(b, int) and b == GB + 1:
                place(0)

        dve.memset(zeros[:, :], 0.0).then_inc(zero_ready.sem, 1)
        all_batches(dve, body, steps, 2)
        keep_logits(BATCH - 1)
        choose(1)
        place(1)


def load_expert(net, sp, e, p):
    a = net.args
    sp.dma_start(net.wi[p][:, :, :], a["L1_ffn_wi"][bass.ds(e, 1), :, :].rearrange("a (k p) n -> p (a k) n", p=P)).then_inc(net.w_in[p].sem, 16)
    sp.dma_start(net.wo[p][:, :, :], a["L1_ffn_wo"][bass.ds(e, 1), :, :].rearrange("a (k p) n -> p (a k) n", p=P)).then_inc(net.w_in[p].sem, 16)


def experts(net, ctx):
    nc = net.nc
    ph = Phase(net, ctx, "e")
    two = range(2)
    wi, wo, w_in = net.wi, net.wo, net.w_in
    wih, wil = (ph.sb(n, [P, KD, HID], F32R) for n in ("wih", "wil"))
    woh, wol = (ph.sb(n, [P, NH, DIM], F32R) for n in ("woh", "wol"))
    xr = [ph.sb(f"xr{i}", [P, 3, DIM]) for i in two]
    xh, xl = ([ph.sb(f"{n}{i}", [P, KD, ROWS], F32R) for i in two] for n in ("xh", "xl"))
    hh, hl = (ph.sb(n, [P, NH, ROWS], F32R) for n in ("hh", "hl"))
    yo = [ph.sb(f"yo{i}", [P, 3, DIM]) for i in two]
    pX = [ph.ps(f"pX{k}", [P, ROWS]) for k in range(KD)]
    pH = [ph.ps(f"pH{i}", [P, ROWS]) for i in range(4)]
    pD = [ph.ps(f"pD{i}", [P, DIM]) for i in two]
    x_in, stored = ([ph.sig(f"{n}{i}", h) for i in two] for n, h in (("x_in", 0), ("stored", 48)))
    turned, x_split, h_made, h_high, h_split, d_made, d_act, d_dve = (
        ph.sig(n, 3) for n in ("turned", "x_split", "h_made", "h_high", "h_split", "d_made", "d_act", "d_dve"))
    wi_high, wi_split, wo_high, wo_split, step = (ph.sig(n) for n in ("wi_high", "wi_split", "wo_high", "wo_split", "step"))
    DTILES = [(0, 0, 128), (128, 0, 128), (ROWS - P, P - RTILES[2][1], P)]

    def later(i, n):
        return not isinstance(i, int) or i >= n

    def in_pairs(eng, body, steps=None, per=0):
        with eng.Fori(0, EXPERTS // 2 - 1) as i:
            if steps:
                steps.enter(i, 2 * per)
            for p in two:
                body(2 * i + p, p, True)
            if steps:
                steps.leave(EXPERTS // 2 - 1)
        body(EXPERTS - 2, 0, True)
        body(EXPERTS - 1, 1, False)

    nc.all_engine_barrier()
    block = ctx.enter_context(nc.Block())

    @block.sync
    def _(sp):

        def front(e, p):
            if later(e, 2):
                sp.wait_ge(d_made.sem, d_made.after(3 * (e - 1)))
            for r, (r0, n) in enumerate(RTILES):
                sp.dma_start(xr[p][0:n, r, :], net.xe_dram[bass.ds(e * ROWS + r0, n), :]).then_inc(x_in[p].sem, 16)
            if later(e, 2):
                load_expert(net, sp, e, p)

        def back(e, p):
            for r, (r0, n) in enumerate(RTILES):
                if r == 0:
                    sp.wait_ge(d_act.sem, d_act.after(2 * e + 1))
                elif r == 1:
                    sp.wait_ge(d_dve.sem, d_dve.after(e + 1))
                else:
                    sp.wait_ge(d_act.sem, d_act.after(2 * e + 2))
                first = DTILES[r][1]
                sp.dma_start(net.ye_dram[bass.ds(e * ROWS + r0, n), :], yo[p][first:first + n, r, :]).then_inc(stored[p].sem, 16)

        front(0, 0)
        front(1, 1)
        back(0, 0)
        with sp.Fori(0, EXPERTS // 2 - 1) as i:
            for p in two:
                front(2 * i + 2 + p, p)
                back(2 * i + 1 + p, 1 - p)
        back(EXPERTS - 1, 1)
        for p in two:
            sp.wait_ge(stored[p].sem, stored[p].after(48 * EXPERTS // 2))

    @block.tensor
    def _(pe):
        def front(e, p):
            pe.wait_ge(x_in[p].sem, x_in[p].after(24 * (e - p) + 48))
            if later(e, 1):
                pe.wait_ge(x_split.sem, x_split.after(e))
            for k in range(KD):
                for r, (r0, n) in enumerate(RTILES):
                    mm = pe.transpose(pX[k][:, r0:r0 + n], xr[p][0:n, r, k * P:(k + 1) * P], net.table["ident"][0:n, 0:n])
            mm.then_inc(turned.sem, 1)

        def body(e, p, behind):
            pe.wait_ge(wi_split.sem, wi_split.after(e + 1))
            pe.wait_ge(x_split.sem, x_split.after(e + 1))
            for c in range(NH):
                if later(e, 1) or c >= 4:
                    pe.wait_ge(h_split.sem, h_split.after(NH * e + c - 3))
                terms = [(w, x, k) for w, x in ((wih, xh), (wih, xl), (wil, xh)) for k in range(KD)]
                for j, (w, x, k) in enumerate(terms):
                    mm = pe.matmul(pH[c % 4][:, :], w[:, k, c * P:(c + 1) * P], x[p][:, k, :], start=(j == 0), stop=(j == len(terms) - 1))
                mm.then_inc(h_made.sem, 1)
            if behind:
                front(e + 1, 1 - p)
            pe.wait_ge(wo_split.sem, wo_split.after(e + 1))
            pe.wait_ge(h_split.sem, h_split.after(NH * (e + 1)))
            for r, (c0, _, _) in enumerate(DTILES):
                if r == 2:
                    pe.wait_ge(d_act.sem, d_act.after(2 * e + 1))
                elif later(e, 1):
                    if r == 0:
                        pe.wait_ge(d_act.sem, d_act.after(2 * e))
                    else:
                        pe.wait_ge(d_dve.sem, d_dve.after(e))
                terms = [(h, w, c) for h, w in ((hh, woh), (hh, wol), (hl, woh)) for c in range(NH)]
                for j, (h, w, c) in enumerate(terms):
                    mm = pe.matmul(pD[r % 2][:, :], h[:, c, c0:c0 + P], w[:, c, :], start=(j == 0), stop=(j == len(terms) - 1))
                mm.then_inc(d_made.sem, 1)

        front(0, 0)
        in_pairs(pe, body)

    @block.scalar
    def _(act):
        def wi_part(e, p):
            act.wait_ge(w_in[p].sem, w_in[p].after(16 * (e - p) + 32))
            if later(e, 1):
                act.wait_ge(h_made.sem, h_made.after(NH * e))
            nc.scalar.activation(wih[:, :, :], wi[p][:, :, :], ACT.Copy).then_inc(wi_high.sem, 1)

        def wo_part(e, p):
            if later(e, 1):
                act.wait_ge(d_made.sem, d_made.after(3 * e))
            nc.scalar.activation(woh[:, :, :], wo[p][:, :, :], ACT.Copy).then_inc(wo_high.sem, 1)

        def body(e, p, behind):
            if later(e, 1):
                act.wait_ge(d_made.sem, d_made.after(3 * e))
            for c in range(NH):
                act.wait_ge(h_made.sem, h_made.after(NH * e + c + 1))
                nc.scalar.activation(hh[:, c, :], pH[c % 4][:, :], ACT.Relu).then_inc(h_high.sem, 1)
            if behind:
                wi_part(e + 1, 1 - p)
            act.wait_ge(stored[p].sem, stored[p].after(24 * (e - p)))
            for r in (0, 2):
                first, last = DTILES[r][1:]
                act.wait_ge(d_made.sem, d_made.after(3 * e + r + 1))
                nc.scalar.activation(yo[p][first:last, r, :], pD[0][first:last, :], ACT.Copy).then_inc(d_act.sem, 1)
            if behind:
                wo_part(e + 1, 1 - p)

        wi_part(0, 0)
        wo_part(0, 0)
        in_pairs(act, body)

    @block.vector
    def _(dve):
        def wi_part(e, p):
            dve.wait_ge(wi_high.sem, wi_high.after(e + 1))
            dve.tensor_tensor(wil[:, :, :], wi[p][:, :, :], wih[:, :, :], ALU.subtract).then_inc(wi_split.sem, 1)

        def wo_part(e, p):
            dve.wait_ge(wo_high.sem, wo_high.after(e + 1))
            dve.tensor_tensor(wol[:, :, :], wo[p][:, :, :], woh[:, :, :], ALU.subtract).then_inc(wo_split.sem, 1)

        def front(e, p):
            dve.wait_ge(turned.sem, turned.after(e + 1))
            for k in range(KD):
                ins = dve.tensor_copy(xh[p][:, k, :], pX[k][:, :])
            ins.then_inc(step.sem, 1)
            dve.wait_ge(step.sem, step.after(e + 1))
            for k in range(KD):
                ins = dve.tensor_tensor(xl[p][:, k, :], pX[k][:, :], xh[p][:, k, :], ALU.subtract)
            ins.then_inc(x_split.sem, 1)

        def body(e, p, behind):
            for c in range(NH):
                dve.wait_ge(h_high.sem, h_high.after(NH * e + c + 1))
                dve.scalar_tensor_tensor(out=hl[:, c, :], in0=pH[c % 4][:, :], scalar=0.0, in1=hh[:, c, :],
                                         op0=ALU.max, op1=ALU.subtract).then_inc(h_split.sem, 1)
                if c == 3 and later(e, 1):
                    wo_part(e, p)
            if behind:
                front(e + 1, 1 - p)
                wi_part(e + 1, 1 - p)
            dve.wait_ge(stored[p].sem, stored[p].after(24 * (e - p)))
            dve.wait_ge(d_made.sem, d_made.after(3 * e + 2))
            dve.tensor_copy(yo[p][:, 1, :], pD[1][:, :]).then_inc(d_dve.sem, 1)

        wi_part(0, 0)
        wo_part(0, 0)
        front(0, 0)
        in_pairs(dve, body)


def combine(net, ctx):
    nc = net.nc
    ph = Phase(net, ctx, "c")
    NB = 8
    NG = 4
    idx = [ph.sb(f"idx{i}", [P, NG, TOPK], U32) for i in range(NB // NG)]
    ya = [[ph.sb(f"ya{k}{i}", [P, DIM]) for k in range(TOPK)] for i in range(NB)]
    y, yo = ([ph.sb(f"{n}{i}", [P, DIM]) for i in range(NB)] for n in ("y", "yo"))
    yst, ymv, yrs = ([ph.sb(f"{n}{i}", [P, NG, w]) for i in range(NB // NG)] for n, w in (("yst", 6), ("ymv", 2), ("yrs", 1)))
    gathered = [ph.sig(f"gathered{i}") for i in range(NB)]
    stored = [ph.sig(f"stored{i}", 16) for i in range(NB)]
    ya_used, ymv_ready, yrs_ready, normed, step, pool_step = (
        ph.sig(n, h) for n, h in (("ya_used", NB), ("ymv_ready", 0), ("yrs_ready", 0), ("normed", NB), ("step", 0),
                                  ("pool_step", 0)))
    out_rows = net.out.rearrange("b (t p) d -> (b t) p d", p=P)

    nc.all_engine_barrier()
    block = ctx.enter_context(nc.Block())

    @block.gpsimd
    def _(pool):
        steps = Steps(pool_step.sem)
        def gather(b, g):
            n = b * NB + g * NG
            pool.wait_ge(ya_used.sem, ya_used.after(n + NG - NB))
            pool.tensor_copy(idx[g][:, :, :], net.idx_back[:, bass.ds(n, NG), :]).then_inc(steps.sem, 1)
            pool.wait_ge(steps.sem, steps.done(1))
            pool.sem_inc(net.passed_pool, 1)
            for t in range(NG):
                for k in range(TOPK):
                    pool.indirect_dma_start(ya[g * NG + t][k][:, :], None, net.ye_dram[:, :],
                                            bass.IndirectOffsetOnAxis(ap=idx[g][:, t, k:k + 1], axis=0),
                                            bounds_check=SLOTS, oob_is_err=False).then_inc(gathered[g * NG + t].sem, 16)

        def roots(m, g):
            pool.wait_ge(ymv_ready.sem, ymv_ready.after(m + 1))
            rstd_of(pool, steps, yrs[g][:, :, 0], ymv[g][:, :, 1], LN_EPS, net).then_inc(yrs_ready.sem, 1)

        gather(0, 0)
        gather(0, 1)
        roots(0, 0)
        with pool.Fori(1, TILES // NB) as b:
            steps.enter(b - 1, 4)
            gather(b, 0)
            roots(2 * b - 1, 1)
            gather(b, 1)
            roots(2 * b, 0)
            steps.leave(TILES // NB - 1)
        roots(2 * (TILES // NB) - 1, 1)

    @block.vector
    def _(dve):
        steps = Steps(step.sem)

        def add_rows(b, g):
            for t in range(g * NG, (g + 1) * NG):
                i = b * NB + t
                dve.wait_ge(gathered[t].sem, gathered[t].after(32 * (b + 1)))
                dve.wait_ge(normed.sem, normed.after(i + 1 - NB))
                src = tile_of(net, i)
                for k in range(TOPK):
                    gate = net.gates[:, k, bass.ds(i, 1)]
                    dve.scalar_tensor_tensor(out=y[t][:, :], in0=ya[t][k][:, :], scalar=gate, in1=src, op0=ALU.mult, op1=ALU.add)\
                        .then_inc(steps.sem, 1)
                    dve.wait_ge(steps.sem, steps.done(1))
                    src = y[t][:, :]
                dve.sem_inc(ya_used.sem, 1)
                dve.bn_stats(yst[g][:, t % NG, :], y[t][:, :]).then_inc(steps.sem, 1)
                dve.wait_ge(steps.sem, steps.done(1))
                dve.sem_inc(net.passed, 1)
                ins = dve.bn_aggr(ymv[g][:, t % NG, :], yst[g][:, t % NG, :])
            ins.then_inc(ymv_ready.sem, 1)

        def norm_rows(m, g):
            dve.wait_ge(yrs_ready.sem, yrs_ready.after(m + 1))
            for t in range(NG):
                dve.wait_ge(stored[g * NG + t].sem, stored[g * NG + t].after(8 * (m - g)))
                dve.tensor_scalar(yo[g * NG + t][:, :], y[g * NG + t][:, :], ymv[g][:, t, 0:1], yrs[g][:, t, :], ALU.subtract, ALU.mult)\
                    .then_inc(normed.sem, 1)

        add_rows(0, 0)
        add_rows(0, 1)
        norm_rows(0, 0)
        with dve.Fori(1, TILES // NB) as b:
            steps.enter(b - 1, 3 * NB)
            add_rows(b, 0)
            norm_rows(2 * b - 1, 1)
            add_rows(b, 1)
            norm_rows(2 * b, 0)
            steps.leave(TILES // NB - 1)
        norm_rows(2 * (TILES // NB) - 1, 1)

    @block.sync
    def _(sp):
        with sp.Fori(0, TILES // NB) as b:
            for t in range(NB):
                i = b * NB + t
                sp.wait_ge(normed.sem, normed.after(i + 1))
                sp.dma_start(out_rows[bass.ds(i, 1), :, :].rearrange("a p d -> (a p) d"), yo[t][:, :]).then_inc(stored[t].sem, 16)
        for s in stored:
            sp.wait_ge(s.sem, s.after(16 * TILES // NB))


PHASES = [prepare, retention, ternary_ffn, attention_inputs, per_token_attention, attention_mlp_and_route, experts, combine]
FINAL = True


def program(nc, args, out, phases=len(PHASES), shown=False):
    with ExitStack() as whole:
        net = Net(nc, whole, args)
        net.out = out
        for phase in PHASES[:phases]:
            net.signals = []
            with ExitStack() as ctx:
                phase(net, ctx)
            if phase is ternary_ffn:
                net.layer0.close()
            if phase is attention_inputs:
                net.projections.close()
            for sem in net.signals:
                nc.sync.sem_clear(sem)
        net.layer0.close()
        net.projections.close()
        if shown:
            with ExitStack() as ctx:
                done = ctx.enter_context(nc.semaphore("shown"))
                block = ctx.enter_context(nc.Block())
                src = net.att_res if shown == "att" else net.x_res

                @block.sync
                def _(sp):
                    sp.dma_start(out.rearrange("b (t p) d -> p (b t) d", p=P), src[:, :, :]).then_inc(done, 16)
                    sp.wait_ge(done, 16)


NAMES = ["L0_attn_x", "L0_attn_past_kv", "L0_attn_W_qkv", "L0_attn_gn_weight", "L0_attn_gn_bias", "L0_ffn_W_fc",
         "L0_ffn_ln_w", "L0_ffn_ln_b", "L0_ffn_W_proj", "L1_attn_Wq", "L1_attn_Wk", "L1_attn_Wv",
         "L1_attn_lambda_params", "L1_attn_g1", "L1_attn_g2", "L1_attn_g3", "L1_attn_W1", "L1_attn_W2",
         "L1_ffn_w_router", "L1_ffn_wi", "L1_ffn_wo"]


def kernel(**inputs):
    import concourse.bacc as bacc
    from concourse.bass_utils import run_bass_kernel_spmd

    nc = bacc.Bacc("TRN2", target_bir_lowering=False, num_devices=1)
    arrays = {name: np.ascontiguousarray(inputs[name]) for name in NAMES}
    arrays["consts"], arrays["consts0"] = CONSTS, CONSTS0
    args = {n: nc.dram_tensor(n, a.shape, mybir.dt.from_np(a.dtype), kind="ExternalInput").ap() for n, a in arrays.items()}
    out = nc.dram_tensor("out", (BATCH, SEQ, DIM), F32, kind="ExternalOutput").ap()
    program(nc, args, out)
    return run_bass_kernel_spmd(nc, [arrays], core_ids=[0]).results[0]["out"]
```
